# Optimizing a Trainium2 kernel written in Bass

```python
import numpy as np
import jax
import jax.numpy as jnp

def _softmax(x, axis=-1):
    return jax.nn.softmax(x, axis=axis)

def _gelu(x):
    return jax.nn.gelu(x, approximate=True)

def _silu(x):
    return jax.nn.silu(x)

def _sigmoid(x):
    return jax.nn.sigmoid(x)

def _layernorm(x, axis=-1, eps=1e-05):
    m = jnp.mean(x, axis=axis, keepdims=True)
    v = jnp.var(x, axis=axis, keepdims=True)
    return (x - m) / jnp.sqrt(v + eps)

def _scatter_add(tgt, idx, src, axis=0):
    return tgt.at[idx].add(src)

def _segment_sum(src, seg, n):
    return jax.ops.segment_sum(src, seg, n)
kernel_name = 'mk_xattn_ffn_d2_seqx_r8_c37d2c'

def setup_inputs(seed: int=0):
    np.random.seed(seed)
    _w = jnp.asarray

    def _rec_inputs():
        import jax
        import jax.numpy as jnp
        _rk = jax.random.key(seed)
        x = 7.22e-05 + 1 * jax.random.normal(jax.random.fold_in(_rk, 1), (2, 512, 128), jnp.float32)
        _lenS = 512 - jax.random.randint(jax.random.fold_in(_rk, 7), (2,), 0, max(1, 512 // 4) + 1, jnp.int32)
        _lenS2 = 77 - jax.random.randint(jax.random.fold_in(_rk, 8), (2,), 0, max(1, 77 // 4) + 1, jnp.int32)
        _ctx_1024P = jax.random.normal(jax.random.fold_in(_rk, 11), (2, 16, 128), jnp.float32)
        _ctx_1024c = jax.random.dirichlet(jax.random.fold_in(_rk, 511), 0.3 * jnp.ones((16,), jnp.float32), (2, 77))
        _ctx_1024t = jnp.einsum('bsk,bkd->bsd', _ctx_1024c, _ctx_1024P)
        _ctx_1024t = _ctx_1024t * jax.lax.rsqrt(jnp.mean(jnp.square(_ctx_1024t)) + 1e-12) * 0.953939
        ctx_1024 = 4.13588e-05 + 0.999923 * (_ctx_1024t + 0.3 * jax.random.normal(jax.random.fold_in(_rk, 611), (2, 77, 128), jnp.float32))
        return (x, ctx_1024)
    x, ctx_1024 = _rec_inputs()

    def _L0_xattn_setup():
        import jax, jax.numpy as jnp
        import numpy as np
        NUM_HEADS = 16
        EPS = 1e-05

        def layer_norm(x, w, b):
            mu = jnp.mean(x, axis=-1, keepdims=True)
            var = jnp.var(x, axis=-1, keepdims=True)
            return (x - mu) * jax.lax.rsqrt(var + EPS) * w + b
        key = jax.random.key(seed)
        ks = jax.random.split(key, 12)
        B, Nq, Nkv, Cq, Ckv, QK, V, O = (4, 256, 256, 128, 128, 128, 128, 128)
        s = lambda fan_in: 1.0 / np.sqrt(fan_in)
        return {'inputs_q': jax.random.normal(ks[0], (B, Nq, Cq), jnp.float32), 'inputs_kv': jax.random.normal(ks[1], (B, Nkv, Ckv), jnp.float32), 'ln_q_w': jnp.ones((Cq,), jnp.float32), 'ln_q_b': jnp.zeros((Cq,), jnp.float32), 'ln_k_w': jnp.ones((Ckv,), jnp.float32), 'ln_k_b': jnp.zeros((Ckv,), jnp.float32), 'ln_v_w': jnp.ones((Ckv,), jnp.float32), 'ln_v_b': jnp.zeros((Ckv,), jnp.float32), 'Wq': jax.random.normal(ks[2], (Cq, QK), jnp.float32) * s(Cq), 'bq': jnp.zeros((QK,), jnp.float32), 'Wk': jax.random.normal(ks[3], (Ckv, QK), jnp.float32) * s(Ckv), 'bk': jnp.zeros((QK,), jnp.float32), 'Wv': jax.random.normal(ks[4], (Ckv, V), jnp.float32) * s(Ckv), 'bv': jnp.zeros((V,), jnp.float32), 'Wo': jax.random.normal(ks[5], (V, O), jnp.float32) * s(V), 'bo': jnp.zeros((O,), jnp.float32)}
    _L0_xattn_all = _L0_xattn_setup()
    _L0_xattn_in = {k: v for k, v in _L0_xattn_all.items() if k in ('ln_q_w', 'ln_q_b', 'ln_k_w', 'ln_k_b', 'ln_v_w', 'ln_v_b', 'Wq', 'bq', 'Wk', 'bk', 'Wv', 'bv', 'Wo', 'bo')}
    del _L0_xattn_all

    def _L0_ffn_setup():
        import jax, jax.numpy as jnp
        import numpy as np
        from jax import lax
        B, S, D = (4, 256, 128)
        E = 8
        K = 2
        F = 408
        NORM_TOPK = True
        key = jax.random.key(seed)
        ks = jax.random.split(key, 8)
        sd = 0.02
        return {'x': jax.random.normal(ks[0], (B, S, D), jnp.float32), 'gate_w': jax.random.normal(ks[1], (E, D), jnp.float32) * sd, 'gate_b': jnp.zeros((E,), jnp.float32), 'up_w': jax.random.normal(ks[2], (E, F, D), jnp.float32) * sd, 'up_b': jnp.zeros((E, F), jnp.float32), 'gp_w': jax.random.normal(ks[3], (E, F, D), jnp.float32) * sd, 'gp_b': jnp.zeros((E, F), jnp.float32), 'down_w': jax.random.normal(ks[4], (E, D, F), jnp.float32) * sd, 'down_b': jnp.zeros((E, D), jnp.float32)}
    _L0_ffn_all = _L0_ffn_setup()
    _L0_ffn_in = {k: v for k, v in _L0_ffn_all.items() if k in ('gate_w', 'gate_b', 'up_w', 'up_b', 'gp_w', 'gp_b', 'down_w', 'down_b')}
    del _L0_ffn_all

    def _L1_xattn_setup():
        import jax, jax.numpy as jnp
        import numpy as np
        B, S, D = (4, 512, 128)
        key = jax.random.key(seed)
        kq, kk, kv = jax.random.split(key, 3)
        q = jax.random.normal(kq, (B, S, D), dtype=jnp.float32)
        k = jax.random.normal(kk, (B, S, D), dtype=jnp.float32)
        v = jax.random.normal(kv, (B, S, D), dtype=jnp.float32)
        return {'q': q, 'k': k, 'v': v}
    _L1_xattn_all = _L1_xattn_setup()
    _L1_xattn_in = {k: v for k, v in _L1_xattn_all.items() if k in ()}
    del _L1_xattn_all

    def _L1_ffn_setup():
        import jax, jax.numpy as jnp
        import numpy as np
        B, S, H, F, E = (4, 256, 128, 512, 8)
        key = jax.random.key(seed)
        ks = jax.random.split(key, 8)
        s = 1.0 / np.sqrt(H)
        sf = 1.0 / np.sqrt(F)
        return {'x': jax.random.normal(ks[0], (B, S, H), jnp.float32), 'wr': jax.random.uniform(ks[1], (H, E), jnp.float32, -s, s), 'br': jax.random.uniform(ks[2], (E,), jnp.float32, -s, s), 'w1': jax.random.uniform(ks[3], (E, H, F), jnp.float32, -s, s), 'b1': jax.random.uniform(ks[4], (E, F), jnp.float32, -s, s), 'w2': jax.random.uniform(ks[5], (E, F, H), jnp.float32, -sf, sf), 'b2': jax.random.uniform(ks[6], (E, H), jnp.float32, -sf, sf)}
    _L1_ffn_all = _L1_ffn_setup()
    _L1_ffn_in = {k: v for k, v in _L1_ffn_all.items() if k in ('wr', 'br', 'w1', 'b1', 'w2', 'b2')}
    del _L1_ffn_all
    return {'x': x, 'ctx_1024': ctx_1024, 'L0_xattn_ln_q_w': _L0_xattn_in['ln_q_w'], 'L0_xattn_ln_q_b': _L0_xattn_in['ln_q_b'], 'L0_xattn_ln_k_w': _L0_xattn_in['ln_k_w'], 'L0_xattn_ln_k_b': _L0_xattn_in['ln_k_b'], 'L0_xattn_ln_v_w': _L0_xattn_in['ln_v_w'], 'L0_xattn_ln_v_b': _L0_xattn_in['ln_v_b'], 'L0_xattn_Wq': _L0_xattn_in['Wq'], 'L0_xattn_bq': _L0_xattn_in['bq'], 'L0_xattn_Wk': _L0_xattn_in['Wk'], 'L0_xattn_bk': _L0_xattn_in['bk'], 'L0_xattn_Wv': _L0_xattn_in['Wv'], 'L0_xattn_bv': _L0_xattn_in['bv'], 'L0_xattn_Wo': _L0_xattn_in['Wo'], 'L0_xattn_bo': _L0_xattn_in['bo'], 'L0_ffn_gate_w': _L0_ffn_in['gate_w'], 'L0_ffn_gate_b': _L0_ffn_in['gate_b'], 'L0_ffn_up_w': _L0_ffn_in['up_w'], 'L0_ffn_up_b': _L0_ffn_in['up_b'], 'L0_ffn_gp_w': _L0_ffn_in['gp_w'], 'L0_ffn_gp_b': _L0_ffn_in['gp_b'], 'L0_ffn_down_w': _L0_ffn_in['down_w'], 'L0_ffn_down_b': _L0_ffn_in['down_b'], 'L1_ffn_wr': _L1_ffn_in['wr'], 'L1_ffn_br': _L1_ffn_in['br'], 'L1_ffn_w1': _L1_ffn_in['w1'], 'L1_ffn_b1': _L1_ffn_in['b1'], 'L1_ffn_w2': _L1_ffn_in['w2'], 'L1_ffn_b2': _L1_ffn_in['b2']}

def reference(x, ctx_1024, L0_xattn_ln_q_w, L0_xattn_ln_q_b, L0_xattn_ln_k_w, L0_xattn_ln_k_b, L0_xattn_ln_v_w, L0_xattn_ln_v_b, L0_xattn_Wq, L0_xattn_bq, L0_xattn_Wk, L0_xattn_bk, L0_xattn_Wv, L0_xattn_bv, L0_xattn_Wo, L0_xattn_bo, L0_ffn_gate_w, L0_ffn_gate_b, L0_ffn_up_w, L0_ffn_up_b, L0_ffn_gp_w, L0_ffn_gp_b, L0_ffn_down_w, L0_ffn_down_b, L1_ffn_wr, L1_ffn_br, L1_ffn_w1, L1_ffn_b1, L1_ffn_w2, L1_ffn_b2):
    import jax
    import jax.numpy as jnp

    def _L0_xattn_ref(inputs_q, inputs_kv, ln_q_w, ln_q_b, ln_k_w, ln_k_b, ln_v_w, ln_v_b, Wq, bq, Wk, bk, Wv, bv, Wo, bo):
        import jax, jax.numpy as jnp
        import numpy as np
        NUM_HEADS = 16
        EPS = 1e-05

        def layer_norm(x, w, b):
            mu = jnp.mean(x, axis=-1, keepdims=True)
            var = jnp.var(x, axis=-1, keepdims=True)
            return (x - mu) * jax.lax.rsqrt(var + EPS) * w + b
        H = NUM_HEADS
        q = layer_norm(inputs_q, ln_q_w, ln_q_b) @ Wq + bq
        k = layer_norm(inputs_kv, ln_k_w, ln_k_b) @ Wk + bk
        v = layer_norm(inputs_kv, ln_v_w, ln_v_b) @ Wv + bv
        b_, n, qk = q.shape
        m = k.shape[1]
        vc = v.shape[2]
        q = q.reshape(b_, n, H, qk // H)
        k = k.reshape(b_, m, H, qk // H)
        v = v.reshape(b_, m, H, vc // H)
        scale = 1.0 / np.sqrt(qk // H)
        scores = jnp.einsum('bnhc,bmhc->bhnm', q, k) * scale
        probs = jax.nn.softmax(scores, axis=-1)
        out = jnp.einsum('bhnm,bmhd->bnhd', probs, v)
        out = out.reshape(b_, n, vc)
        return out @ Wo + bo

    def _L0_ffn_ref(x, gate_w, gate_b, up_w, up_b, gp_w, gp_b, down_w, down_b):
        import jax, jax.numpy as jnp
        import numpy as np
        from jax import lax
        B, S, D = (4, 256, 128)
        E = 8
        K = 2
        F = 408
        NORM_TOPK = True
        bs, slen, dim = x.shape
        xf = x.reshape(-1, dim)
        N = xf.shape[0]
        scores = jax.nn.softmax(xf @ gate_w.T + gate_b, axis=-1)
        top_w, top_idx = lax.top_k(scores, K)
        if NORM_TOPK:
            top_w = top_w / (top_w.sum(-1, keepdims=True) + 1e-20)
        comb = jnp.zeros((N, E), xf.dtype).at[jnp.arange(N)[:, None], top_idx].add(top_w)

        def step(acc, p):
            uw, ub, gw, gb, dw, db, w = p
            h = jax.nn.silu((xf @ gw.T + gb) * (xf @ uw.T + ub))
            return (acc + w[:, None] * (h @ dw.T + db), None)
        y0 = jnp.zeros_like(xf)
        y, _ = lax.scan(step, y0, (up_w, up_b, gp_w, gp_b, down_w, down_b, comb.T))
        return y.reshape(bs, slen, dim)

    def _L1_xattn_ref(q, k, v):
        import jax, jax.numpy as jnp
        import numpy as np
        B, S, D = (4, 512, 128)
        scale = jnp.asarray(q.shape[-1], q.dtype) ** (-0.5)
        logits = jnp.einsum('bqd,bkd->bqk', q, k) * scale
        weights = jax.nn.softmax(logits, axis=-1)
        return jnp.einsum('bqk,bkd->bqd', weights, v)

    def _L1_ffn_ref(x, wr, br, w1, b1, w2, b2):
        import jax, jax.numpy as jnp
        import numpy as np
        B, S, H, F, E = (4, 256, 128, 512, 8)
        scores = jnp.einsum('bsh,he->bse', x, wr) + br
        expert_id = jnp.argmax(scores, axis=-1)
        h = jnp.einsum('bsh,ehf->ebsf', x, w1) + b1[:, None, None, :]
        h = jax.nn.gelu(h, approximate=False)
        y = jnp.einsum('ebsf,efh->ebsh', h, w2) + b2[:, None, None, :]
        one_hot = jax.nn.one_hot(expert_id, E, dtype=x.dtype)
        out = jnp.einsum('ebsh,bse->bsh', y, one_hot)
        return out
    x = x + _L0_xattn_ref(_layernorm(x, axis=-1), ctx_1024, L0_xattn_ln_q_w, L0_xattn_ln_q_b, L0_xattn_ln_k_w, L0_xattn_ln_k_b, L0_xattn_ln_v_w, L0_xattn_ln_v_b, L0_xattn_Wq, L0_xattn_bq, L0_xattn_Wk, L0_xattn_bk, L0_xattn_Wv, L0_xattn_bv, L0_xattn_Wo, L0_xattn_bo)
    x = x + _L0_ffn_ref(_layernorm(x, axis=-1), L0_ffn_gate_w, L0_ffn_gate_b, L0_ffn_up_w, L0_ffn_up_b, L0_ffn_gp_w, L0_ffn_gp_b, L0_ffn_down_w, L0_ffn_down_b)
    x = x + _L1_xattn_ref(_layernorm(x, axis=-1), ctx_1024, ctx_1024)
    x = x + _L1_ffn_ref(_layernorm(x, axis=-1), L1_ffn_wr, L1_ffn_br, L1_ffn_w1, L1_ffn_b1, L1_ffn_w2, L1_ffn_b2)
    return x

_drawn_inputs = setup_inputs


def setup_inputs(seed=0):
    import zlib

    import numpy as np

    out = dict(_drawn_inputs(seed))
    spreads = {'L0_xattn_ln_q_w': (1.0, 0.2),
     'L0_xattn_ln_q_b': (0.0, 0.1),
     'L0_xattn_ln_k_w': (1.0, 0.2),
     'L0_xattn_ln_k_b': (0.0, 0.8),
     'L0_xattn_ln_v_w': (1.0, 0.2),
     'L0_xattn_ln_v_b': (0.0, 0.1),
     'L0_xattn_bq': (0.0, 0.1),
     'L0_xattn_bk': (0.0, 0.8),
     'L0_xattn_bv': (0.0, 0.1),
     'L0_xattn_bo': (0.0, 0.1),
     'L0_ffn_gate_b': (0.0, 0.1),
     'L0_ffn_up_b': (0.0, 0.609),
     'L0_ffn_gp_b': (0.0, 0.8),
     'L0_ffn_down_b': (0.0, 0.1)}
    factors = {'L0_ffn_up_w': 3.86,
     'L0_ffn_gp_w': 4.386,
     'L0_ffn_down_w': 3.436,
     'L1_ffn_b1': 4.042,
     'L1_ffn_b2': 2.841}
    for name, (base, spread) in spreads.items():
        noise = np.random.default_rng([zlib.crc32(name.encode()), seed]).standard_normal(out[name].shape)
        drawn = base * np.exp(spread * noise) if base else spread * noise
        out[name] = jnp.asarray(drawn.astype(out[name].dtype))
    for name, factor in factors.items():
        out[name] = (out[name] * factor).astype(out[name].dtype)
    return out
```

```python
from contextlib import ExitStack

import concourse.bass as bass
from concourse import mybir

F32 = mybir.dt.float32
BF16 = mybir.dt.bfloat16
I32 = mybir.dt.int32
U32 = mybir.dt.uint32
ALU = mybir.AluOpType
ACT = mybir.ActivationFunctionType
AX = mybir.AxisListType

P = 128
D = 128
B = 2
C = 8
CB = C // B
N = C * P
M = 77
H = 16
DH = D // H
HH = H // 2
W = HH * M
J = -(-W // P)
WP = J * P
OW = DH + 1
G = C * 2
E = 8
F0 = 408
K0 = 4
FB0 = F0 // K0
F1 = 512
K1 = 4
T0 = 2 * N // P + E - 1
T1 = N // P + E - 1
BI0 = 2 * F0 + D
BI1 = F1 + D
BIAS = E * (BI0 + BI1)
BC = BIAS // P
EPS = 1e-5
NEG = -3.0e38

CONST_PARTS = [("ident", P), ("headmask", H), ("blockmask", J * HH), ("sel", WP), ("before", P),
               ("ones", P), ("rev", C * E), ("kstep", E * E), ("earlier", E * E),
               ("iota", P), ("tstep", T0), ("tilecol", T0 * E), ("tokval", 2 * C * 2)]
CONST_AT = {}
_at = 0
for _name, _n in CONST_PARTS:
    CONST_AT[_name] = (_at, _at + _n)
    _at += _n
CONSTS = _at
VECS = ["lnqw", "lnqb", "lnkw", "lnkb", "lnvw", "lnvb", "bq", "bk", "bv"]
ROWS = D + 2 * E


def two_blocks(nc, x_in, ctx_in, wqkvo_in, vecs_in, rows_in, consts_in, gate_in, wgu_in,
               dw_in, w1_in, w2_in, bias_in, out):
    stack = ExitStack()
    with stack:
        def sb(name, shape, dt=F32):
            return stack.enter_context(nc.sbuf_tensor(name, shape, dt))

        def bank(name, columns=512):
            return stack.enter_context(nc.psum_tensor(name, [P, columns], F32))

        def sem(name):
            return stack.enter_context(nc.semaphore(name))

        rows0 = nc.dram_tensor("rows0", (N, D), F32).ap()
        back0 = nc.dram_tensor("back0", (2 * N, D), F32).ap()
        rows1 = nc.dram_tensor("rows1", (N, 2 * D), F32).ap()
        parts = nc.dram_tensor("parts", (3, BIAS), BF16).ap()

        x = sb("x", [P, C, D])
        ctx = sb("ctx", [M, B, D])
        wqkvo = sb("wqkvo", [P, 4, D])
        vecs = sb("vecs", [P, len(VECS)])
        rows = sb("rows", [P, ROWS])
        consts = sb("consts", [P, CONSTS])
        gate = sb("gate", [P, 2, E])
        wgu = sb("wgu", [P, E * 2 * F0])
        dw = sb("dw", [FB0, E * K0 * D])
        w1 = sb("w1", [P, E * F1])
        w2 = sb("w2", [P, E * K1 * D])
        bias = sb("bias", [P, BC])
        part = sb("part", [P, 3, BC], BF16)
        rest = sb("rest", [P, 2, BC])
        bias3 = sb("bias3", [3, BIAS], BF16)
        ones3 = sb("ones3", [3, P], BF16)

        stat = sb("stat", [P, C, 6])
        mv = sb("mv", [P, C, 2])
        rstd = sb("rstd", [P, C])
        cstat = sb("cstat", [M, B, 6])
        cmv = sb("cmv", [M, B, 2])
        crstd = sb("crstd", [M, B])
        xn = sb("xn", [P, C, D])
        cn = sb("cn", [M, B, D])
        xbo = sb("xbo", [P, C, D])
        xnT = sb("xnT", [P, N])
        cT = sb("cT", [P, B, M])
        ckT = sb("ckT", [P, B, M])
        cvT = sb("cvT", [P, B, M])
        qT = sb("qT", [P, N])
        kT = sb("kT", [P, B, M])
        v = sb("v", [M, B, D])
        kblk = sb("kblk", [P, B, H, M])
        vblk = sb("vblk", [P, B, 2, J, HH, OW])
        smax = sb("smax", [P, 2, HH])
        prob = sb("prob", [P, 3, WP])
        probT = sb("probT", [P, 2, WP])
        rsum = sb("rsum", [P, H])
        on = sb("on", [P, 2, D])
        onT = sb("onT", [P, 2, D])
        x1 = sb("x1", [P, C, D])
        stat1 = sb("stat1", [P, C, 6])
        mv1 = sb("mv1", [P, C, 2])
        rstd1 = sb("rstd1", [P, C])
        neghalf = sb("neghalf", [P, C])
        xf = sb("xf", [P, C, D])
        xfT = sb("xfT", [P, 2, D])

        lg = sb("lg", [P, C, E])
        lg2 = sb("lg2", [P, C, E])
        key = sb("key", [P, C, E])
        top = sb("top", [P, 2, C])
        kmax = sb("kmax", [P, 2, C])
        pick = sb("pick", [P, 2, C, E])
        both = sb("both", [P, C, E])
        ex = sb("ex", [P, C, E])
        ex2 = sb("ex2", [P, C])
        wt = sb("wt", [P, 6, C])
        ntl = sb("ntl", [P, E])
        over = sb("over", [P, E, E])
        base = sb("base", [P, E])
        ends = sb("ends", [P, E])
        place = sb("place", [P, C, E])
        slots = sb("slots", [P, 2, C, E])
        slot = sb("slot", [P, 2 * C], I32)
        lane = sb("lane", [P, 2 * C], I32)
        lanef = sb("lanef", [P, 2 * C])
        tilef = sb("tilef", [P, 2 * C])
        onehot = kblk[:, :, :, :].rearrange("p b h m -> p (b h m)")[:, 0:2 * C * P].rearrange(
            "p (q s) -> p q s", q=2 * C)
        intile = sb("intile", [P, 2 * C, T0])
        vals = sb("vals", [P, 2 * C, 3])
        tabv = sb("tabv", [P, 2 * C, 3, T0])
        etile = sb("etile", [P, T0, E])
        esum = sb("esum", [P, T0])
        padrow = sb("padrow", [P, T0])

        expert = [sb(f"expert{l}", [P, t], I32) for l, t in enumerate((T0, T1))]
        token = [sb(f"token{l}", [P, t], U32) for l, t in enumerate((T0, T1))]
        dest = [sb(f"dest{l}", [P, t], U32) for l, t in enumerate((T0, T1))]
        slotw = sb("slotw", [P, T0])

        xs = [sb(f"xs{i}", [P, 2 * D]) for i in range(4)]
        xsT = [sb(f"xsT{i}", [P, P]) for i in range(2)]
        z = [sb(f"z{i}", [P, F0]) for i in range(2)]
        h = [sb(f"h{i}", [P, F1]) for i in range(2)]
        hT = [sb(f"hT{i}", [P, K1 * P]) for i in range(2)]
        keep = [sb(f"keep{i}", [P, D]) for i in range(4)]
        y = [sb(f"y{i}", [P, D]) for i in range(4)]

        y01, x2n, o2 = xbo, xn, x
        x2T = xnT[:, :].rearrange("p (c t) -> p c t", c=C)
        x3T = qT[:, :].rearrange("p (c t) -> p c t", c=C)
        ybk = kblk[:, :, :, :].rearrange("p b h m -> p (b h m)")[:, 0:C * 2 * D].rearrange(
            "p (c j d) -> p c j d", c=C, j=2)
        x2 = wgu[:, 0:N].rearrange("p (c d) -> p c d", c=C)
        row1 = wgu[:, N:3 * N].rearrange("p (c j d) -> p c j d", c=C, j=2)
        prob2T = wgu[0:M, 3 * N:4 * N].rearrange("p (c t) -> p c t", c=C)
        prob2 = wgu[:, 4 * N:4 * N + C * M].rearrange("p (c m) -> p c m", c=C)
        stat2 = sb("stat2", [P, C, 6])
        mv2 = sb("mv2", [P, C, 2])
        rstd2 = sb("rstd2", [P, C])
        smax2 = sb("smax2", [P, C])
        ssum2 = sb("ssum2", [P, C])
        rsum2 = sb("rsum2", [P, C])
        stat3 = sb("stat3", [P, C, 6])
        mv3 = sb("mv3", [P, C, 2])
        rstd3 = sb("rstd3", [P, C])

        psS = [bank("psS0", 1024), bank("psS1", 1024)]
        psT = bank("psT", 1024)
        psO = bank("psO")
        psX = bank("psX")
        b0, b1, b2, b3 = psS[0][:, 0:512], psS[0][:, 512:1024], psS[1][:, 0:512], psS[1][:, 512:1024]
        b4, b5 = psT[:, 0:512], psT[:, 512:1024]
        mis_onT, mis_out, mis_xT = psX[:, 0:128], psX[:, 128:256], psX[:, 256:384]
        logit = psX[:, 384:448].rearrange("p (c e) -> p c e", e=E)

        def wait_past(eng, semaphore, count):
            if count > 0:
                eng.wait_ge(semaphore, count)

        def cst(name, partitions=P):
            a, b = CONST_AT[name]
            return consts[0:partitions, a:b]

        def vec(name):
            i = VECS.index(name)
            return vecs[:, i:i + 1]

        ident = cst("ident")
        wq, wk, wv, wo = (wqkvo[:, i, :] for i in range(4))
        bo_row, gateb_row, br_row = rows[:, 0:D], rows[:, D:D + E], rows[:, D + E:D + 2 * E]

        x_in_s = [sem(f"x_loaded{b}") for b in range(B)]
        small_s = sem("small_loaded")
        ctx_s = sem("ctx_loaded")
        const_s = sem("consts_loaded")
        bias_s = sem("bias_loaded")
        parts_ready = sem("bias_parts_ready")
        parts_stored = sem("bias_parts_stored")
        bias3_s = sem("bias3_loaded")
        f0_w = sem("mixture0_weights_loaded")
        f1_w = sem("mixture1_weights_loaded")
        pool_step = sem("pool_step")
        var_ready = sem("variances_ready")
        rstd_ready = sem("rstd_ready")
        dve_step = sem("dve_step")
        xn_ready = sem("xn_ready")
        cn_ready = sem("cn_ready")
        ctxT_ps = sem("ctxT_in_psum")
        ctxT_ready = sem("ctxT_ready")
        xT_ps = sem("xT_in_psum")
        xnT_ready = sem("xnT_ready")
        k_ps = sem("k_in_psum")
        kT_ready = sem("kT_ready")
        v_ps = sem("v_in_psum")
        v_ready = sem("v_ready")
        vv_ps = sem("v_spread_in_psum")
        vblk_ready = sem("vblk_ready")
        q_ps = sem("q_in_psum")
        q_ready = sem("q_ready")
        kblk_ready = sem("kblk_ready")
        xbo_ready = sem("xbo_ready")
        prob_zero = sem("prob_padding_zero")
        s_ps = sem("scores_in_psum")
        sub_ready = sem("scores_less_max_ready")
        exp_ready = sem("exp_ready")
        pT_ps = sem("probT_in_psum")
        pT_ready = sem("probT_ready")
        o_ps = sem("heads_in_psum")
        on_ready = sem("heads_normalized")
        onT_ps = sem("headsT_in_psum")
        onT_ready = sem("headsT_ready")
        out_ps = sem("projection_in_psum")
        x1_ready = sem("x1_ready")
        xf_ready = sem("xf_ready")
        xf_stored = sem("xf_stored")
        xfT_ps = sem("xfT_in_psum")
        xfT_ready = sem("xfT_ready")
        logit_ps = sem("gate_logits_in_psum")

        l_less = [sem(f"logits_less_max{l}") for l in range(2)]
        ex_ready = sem("gate_exp_ready")
        pick_ready = [sem(f"picks_ready{l}") for l in range(2)]
        rank_ps = [sem(f"ranks_in_psum{l}") for l in range(2)]
        spread_ready = [sem(f"slots_spread{l}") for l in range(2)]
        table_ps = [sem(f"table_in_psum{l}") for l in range(2)]
        experts_ready = [sem(f"experts_ready{l}") for l in range(2)]
        table_ready = [sem(f"table_ready{l}") for l in range(2)]

        gathered = [[sem(f"gathered{l}_{i}") for i in range(4)] for l in range(2)]
        xsT_ps = [sem(f"xsT_in_psum{l}") for l in range(2)]
        xsT_ready = [sem(f"xsT_ready{l}") for l in range(2)]
        up_ps = [sem(f"hidden_in_psum{l}") for l in range(2)]
        up_half = sem("up_in_psum")
        z_up = sem("up_ready")
        z_ready = sem("gated_ready")
        h_ready = [sem(f"hidden_ready{l}") for l in range(2)]
        hT_ps = [sem(f"hiddenT_in_psum{l}") for l in range(2)]
        hT_ready = [sem(f"hiddenT_ready{l}") for l in range(2)]
        y_ps = [sem(f"y_in_psum{l}") for l in range(2)]
        y_ready = [sem(f"y_ready{l}") for l in range(2)]
        scattered = [[sem(f"scattered{l}_{i}") for i in range(4)] for l in range(2)]

        back_s = [sem(f"rows_back{b}") for b in range(B)]
        kept = sem("residual_rows_kept")
        x2n_ready = sem("x2n_ready")
        x2T_ps = sem("x2T_in_psum")
        x2T_ready = sem("x2T_ready")
        s2_ps = sem("scores2_in_psum")
        sub2_ready = sem("scores2_less_max_ready")
        exp2_ready = sem("exp2_ready")
        p2T_ps = sem("prob2T_in_psum")
        p2T_ready = sem("prob2T_ready")
        o2_ps = sem("attended_in_psum")
        x3_ready = sem("x3_ready")
        row1_ready = sem("row1_ready")
        row1_stored = sem("row1_stored")
        x3T_ps = sem("x3T_in_psum")
        x3T_ready = sem("x3T_ready")
        logit1_ps = sem("router_logits_in_psum")

        block = stack.enter_context(nc.Block())

        @block.sync
        def _(sp):
            for b in range(B):
                sp.dma_start(x[:, CB * b:CB * (b + 1), :],
                             x_in[b].rearrange("(c p) d -> p c d", p=P)).then_inc(x_in_s[b], 16)
                if b == 0:
                    sp.dma_start(ctx[:, :, :], ctx_in.rearrange("b m d -> m b d")).then_inc(ctx_s, 16)
                    sp.dma_start(consts[:, :], consts_in).then_inc(const_s, 16)
                    sp.dma_start(vecs[:, :], vecs_in).then_inc(small_s, 16)
                    sp.dma_start(wqkvo[:, :, :], wqkvo_in).then_inc(small_s, 16)
            sp.dma_start(rows[:, :], rows_in.partition_broadcast(P)).then_inc(small_s, 16)
            sp.dma_start(gate[:, :, :], gate_in).then_inc(small_s, 16)
            sp.dma_start(bias[:, :], bias_in).then_inc(bias_s, 16)
            half = E * F0
            sp.dma_start(wgu[:, 0:half], wgu_in[:, 0:half]).then_inc(f0_w, 16)
            sp.wait_ge(parts_ready, 3)
            for i in range(3):
                sp.dma_start(parts[i].rearrange("(p n) -> p n", p=P), part[:, i, :]).then_inc(parts_stored, 16)
            sp.dma_start(wgu[:, half:], wgu_in[:, half:]).then_inc(f0_w, 16)
            sp.wait_ge(parts_stored, 48)
            sp.dma_start(bias3[:, :], parts).then_inc(bias3_s, 16)
            sp.dma_start(dw[:, :], dw_in).then_inc(f0_w, 16)
            sp.dma_start(w1[:, :], w1_in).then_inc(f1_w, 16)
            sp.dma_start(w2[:, :], w2_in).then_inc(f1_w, 16)
            for c in range(C):
                sp.wait_ge(xf_ready, c + 1)
                sp.dma_start(rows0[P * c:P * (c + 1), :], xf[:, c, :]).then_inc(xf_stored, 16)
            for i in range(4):
                sp.wait_ge(scattered[0][i], 16 * len(range(i, T0, 4)))
            for b in range(B):
                sp.dma_start(ybk[:, CB * b:CB * (b + 1), :, :],
                             back0[2 * P * CB * b:2 * P * CB * (b + 1), :].rearrange(
                                 "(c p j) d -> p c j d", p=P, j=2)).then_inc(back_s[b], 16)
            for b in range(B):
                sp.wait_ge(row1_ready, b + 1)
                sp.dma_start(rows1[P * CB * b:P * CB * (b + 1), :].rearrange("(c p) d -> p c d", p=P),
                             row1[:, CB * b:CB * (b + 1), :, :].rearrange("p c j d -> p c (j d)")
                             ).then_inc(row1_stored, 16)
            for i in range(4):
                sp.wait_ge(scattered[1][i], 16 * len(range(i, T1, 4)))

        @block.gpsimd
        def _(pool):
            pool.memset(neghalf[:, :], -0.5).then_inc(pool_step, 1)
            pool.memset(ones3[:, :], 1.0).then_inc(pool_step, 1)
            roots = [0]

            def root(r):
                if roots[0] == 0:
                    pool.wait_ge(pool_step, 1)
                roots[0] += 1
                pool.wait_ge(var_ready, roots[0])
                pool.tensor_tensor(r, r, neghalf[0:r.shape[0], 0:r.shape[1]], ALU.pow).then_inc(rstd_ready, 1)

            root(crstd[:, :])
            root(rstd[:, 0:CB])
            root(rstd[:, CB:C])
            pool.memset(prob[:, :, W:WP], 0.0).then_inc(prob_zero, 1)
            pool.wait_ge(small_s, 64)
            for b in range(B):
                pool.wait_ge(x_in_s[b], 16)
                cs = slice(CB * b, CB * (b + 1))
                pool.tensor_tensor(xbo[:, cs, :], x[:, cs, :],
                                   bo_row.unsqueeze(1).broadcast_to([P, CB, D]), ALU.add).then_inc(xbo_ready, 1)
            pool.wait_ge(bias_s, 16)
            pool.tensor_copy(part[:, 0, :], bias[:, :]).then_inc(parts_ready, 1)
            pool.wait_ge(parts_ready, 1)
            pool.tensor_tensor(rest[:, 0, :], bias[:, :], part[:, 0, :], ALU.subtract).then_inc(pool_step, 1)
            pool.wait_ge(pool_step, 3)
            pool.tensor_copy(part[:, 1, :], rest[:, 0, :]).then_inc(parts_ready, 1)
            pool.wait_ge(parts_ready, 2)
            pool.tensor_tensor(rest[:, 1, :], rest[:, 0, :], part[:, 1, :], ALU.subtract).then_inc(pool_step, 1)
            pool.wait_ge(pool_step, 4)
            pool.tensor_copy(part[:, 2, :], rest[:, 1, :]).then_inc(parts_ready, 1)
            pool.wait_ge(const_s, 16)
            pool.wait_ge(kT_ready, 1)
            pool.tensor_tensor(kblk[:, 1, :, :], kT[:, 1:2, :].broadcast_to([P, H, M]),
                               cst("headmask").unsqueeze(2).broadcast_to([P, H, M]), ALU.mult
                               ).then_inc(kblk_ready, 1)

            def gather(l, t):
                source, width = ((rows0, D), (rows1, 2 * D))[l]
                pool.indirect_dma_start(xs[t % 4][:, 0:width], None, source,
                                        bass.IndirectOffsetOnAxis(ap=token[l][:, t:t + 1], axis=0)
                                        ).then_inc(gathered[l][t % 4], 16)

            def scatter(l, t):
                target = (back0, out)[l]
                pool.indirect_dma_start(target, bass.IndirectOffsetOnAxis(ap=dest[l][:, t:t + 1], axis=0),
                                        y[t % 4][:, :], None, bounds_check=target.shape[0] - 1,
                                        oob_is_err=False).then_inc(scattered[l][t % 4], 16)

            for c in range(C):
                root(rstd1[:, c:c + 1])

            for l, tiles in enumerate((T0, T1)):
                if l == 1:
                    for r in (rstd2, rstd3):
                        for b in range(B):
                            root(r[:, CB * b:CB * (b + 1)])
                pool.wait_ge((xf_stored, row1_stored)[l], (16 * C, 16 * B)[l])
                pool.wait_ge(table_ready[l], 1)
                for t in range(4):
                    gather(l, t)
                for t in range(tiles):
                    if t + 4 < tiles:
                        pool.wait_ge(xsT_ps[l], t + 1)
                        if l == 1:
                            pool.wait_ge(kept, t + 1)
                        gather(l, t + 4)
                    pool.wait_ge(y_ready[l], t + 1)
                    scatter(l, t)

        @block.vector
        def _(dve):
            steps = [0]

            def link(ins):
                steps[0] += 1
                ins.then_inc(dve_step, 1)
                dve.wait_ge(dve_step, steps[0])

            rooted = [0]

            def stats(source, st, m, r, chunks, extra=0.0):
                n = source.shape[0]
                for c in chunks:
                    last = dve.bn_stats(st[0:n, c, :], source[:, c, :])
                link(last)
                for c in chunks:
                    last = dve.bn_aggr(m[0:n, c, :], st[0:n, c, :])
                link(last)
                a, b = chunks[0], chunks[-1] + 1
                dve.tensor_scalar(r[0:n, a:b], m[0:n, a:b, 1], 1.0 + extra, extra * extra if extra else EPS,
                                  ALU.mult, ALU.add).then_inc(var_ready, 1)
                rooted[0] += 1
                return rooted[0]

            def normal(target, source, m, r, c):
                n = source.shape[0]
                return dve.tensor_scalar(target, source[:, c, :], m[0:n, c, 0:1], r[0:n, c:c + 1],
                                         ALU.subtract, ALU.mult)

            dve.wait_ge(ctx_s, 16)
            dve.wait_ge(rstd_ready, stats(ctx[:, :, :], cstat, cmv, crstd, range(B)))
            for b in range(B):
                normal(cn[:, b, :], ctx[:, :, :], cmv, crstd, b).then_inc(cn_ready, 1)
            for b in range(B):
                dve.wait_ge(x_in_s[b], 16)
                cs = range(CB * b, CB * (b + 1))
                dve.wait_ge(rstd_ready, stats(x[:, :, :], stat, mv, rstd, cs, extra=EPS))
                for c in cs:
                    normal(xn[:, c, :], x[:, :, :], mv, rstd, c).then_inc(xn_ready, 1)
                if b == 0:
                    dve.wait_ge(small_s, 64)
                    dve.wait_ge(ctxT_ps, 2)
                    raw = b5[:, 0:2 * B * M].rearrange("p (k b m) -> p k b m", k=2, b=B)
                    dve.tensor_scalar(ckT[:, :, :], raw[:, 0], vec("lnkw"), vec("lnkb"), ALU.mult, ALU.add
                                      ).then_inc(ctxT_ready, 1)
                    dve.tensor_scalar(cvT[:, :, :], raw[:, 0], vec("lnvw"), vec("lnvb"), ALU.mult, ALU.add
                                      ).then_inc(ctxT_ready, 1)
                    dve.tensor_copy(cT[:, :, :], raw[:, 1]).then_inc(ctxT_ready, 1)
                    dve.wait_ge(k_ps, 1)
                    dve.tensor_scalar(kT[:, :, :], psX[:, 0:B * M].rearrange("p (b m) -> p b m", b=B),
                                      vec("bk"), None, ALU.add).then_inc(kT_ready, 1)
                    dve.wait_ge(v_ps, 1)
                    dve.tensor_copy(v[:, :, :], psO[0:M, 0:B * D].rearrange("p (b d) -> p b d", b=B)
                                    ).then_inc(v_ready, 1)
                    dve.wait_ge(kT_ready, 1)
                    dve.tensor_tensor(kblk[:, 0, :, :], kT[:, 0:1, :].broadcast_to([P, H, M]),
                                      cst("headmask").unsqueeze(2).broadcast_to([P, H, M]), ALU.mult
                                      ).then_inc(kblk_ready, 1)
                dve.wait_ge(q_ps, b + 1)
                dve.tensor_scalar(qT[:, 512 * b:512 * (b + 1)], (b2, b3)[b], vec("bq"), DH ** -0.5,
                                  ALU.add, ALU.mult).then_inc(q_ready, 1)
                if b == 0:
                    mask = cst("blockmask").rearrange("p (j h) -> p j h", j=J)
                    for bb in range(B):
                        dve.wait_ge(vv_ps, bb + 1)
                        vv = psT[:, 0:J * D].rearrange("p (j s h c) -> p s j h c", j=J, s=2, h=HH)
                        for s in range(2):
                            for j in range(J):
                                last = dve.tensor_tensor(
                                    vblk[:, bb, s, j, :, 0:DH], vv[:, s, j],
                                    mask[:, j].unsqueeze(2).broadcast_to([P, HH, DH]), ALU.mult)
                            last = dve.tensor_copy(vblk[:, bb, s, :, :, DH], mask)
                        last.then_inc(vblk_ready, 1)

            def scores(g):
                s = psS[g % 2][:, 0:W].rearrange("p (h m) -> p h m", h=HH)
                dve.wait_ge(s_ps, g + 1)
                link(dve.tensor_reduce(smax[:, g % 2, :], s, AX.X, ALU.max))
                if g == 0:
                    dve.wait_ge(prob_zero, 1)
                if g >= 3:
                    dve.wait_ge(pT_ps, g - 2)
                dve.tensor_tensor(prob[:, g % 3, 0:W].rearrange("p (h m) -> p h m", h=HH), s,
                                  smax[:, g % 2, :].unsqueeze(2).broadcast_to([P, HH, M]), ALU.subtract
                                  ).then_inc(sub_ready, 1)

            def heads(c):
                o = psO[:, 0:H * OW].rearrange("p (h w) -> p h w", h=H)
                dve.wait_ge(o_ps, 2 * c + 2)
                link(dve.reciprocal(rsum[:, :], o[:, :, DH]))
                if c >= 2:
                    dve.wait_ge(onT_ps, c - 1)
                dve.tensor_tensor(on[:, c % 2, :].rearrange("p (h w) -> p h w", h=H), o[:, :, 0:DH],
                                  rsum[:, :].unsqueeze(2).broadcast_to([P, H, DH]), ALU.mult
                                  ).then_inc(on_ready, 1)

            def residual(c):
                dve.wait_ge(out_ps, c + 1)
                if c % CB == 0:
                    dve.wait_ge(xbo_ready, c // CB + 1)
                dve.tensor_tensor(x1[:, c, :], mis_out, xbo[:, c, :], ALU.add).then_inc(x1_ready, 1)
                dve.wait_ge(x1_ready, c + 1)
                stats(x1[:, :, :], stat1, mv1, rstd1, range(c, c + 1))

            def rows_for_gate(c):
                dve.wait_ge(rstd_ready, 3 + c + 1)
                normal(xf[:, c, :], x1[:, :, :], mv1, rstd1, c).then_inc(xf_ready, 1)

            for g in range(G + 7):
                if g < G:
                    scores(g)
                if g >= 8 and g % 2 == 0 and (g - 8) // 2 < C:
                    rows_for_gate((g - 8) // 2)
                if g >= 4 and g % 2 == 0 and (g - 4) // 2 < C:
                    heads((g - 4) // 2)
                if g >= 6 and g % 2 == 0 and (g - 6) // 2 < C:
                    residual((g - 6) // 2)

            def spread(chunked, *shape):
                return chunked.broadcast_to(list(shape))

            def route(l):
                J2 = (2, 1)[l]
                tiles = (T0, T1)[l]
                rev = cst("rev").rearrange("p (c e) -> p c e", e=E)
                dve.wait_ge((logit_ps, logit1_ps)[l], C)
                bias_row = (gateb_row, br_row)[l]
                link(dve.tensor_tensor(lg[:, :, :], logit, bias_row.unsqueeze(1).broadcast_to([P, C, E]), ALU.add))
                link(dve.tensor_reduce(top[:, 0, :], lg[:, :, :], AX.X, ALU.max))
                dve.tensor_tensor(lg2[:, :, :], lg[:, :, :], top[:, 0, :].unsqueeze(2).broadcast_to([P, C, E]),
                                  ALU.subtract).then_inc(l_less[l], 1)
                dve.wait_ge(l_less[l], 1)
                link(dve.scalar_tensor_tensor(out=key[:, :, :], in0=lg2[:, :, :], scalar=0.0, in1=rev,
                                              op0=ALU.is_ge, op1=ALU.mult))
                link(dve.tensor_reduce(kmax[:, 0, :], key[:, :, :], AX.X, ALU.max))
                first = dve.tensor_tensor(pick[:, 0, :, :], rev, kmax[:, 0, :].unsqueeze(2).broadcast_to([P, C, E]),
                                          ALU.is_equal)
                if l == 1:
                    first.then_inc(pick_ready[l], 1)
                    dve.wait_ge(pick_ready[l], 1)
                else:
                    link(first)
                    link(dve.scalar_tensor_tensor(out=lg[:, :, :], in0=pick[:, 0, :, :], scalar=NEG,
                                                  in1=lg2[:, :, :], op0=ALU.mult, op1=ALU.add))
                    dve.tensor_reduce(top[:, 1, :], lg[:, :, :], AX.X, ALU.max).then_inc(l_less[l], 1)
                    dve.wait_ge(l_less[l], 2)
                    link(dve.tensor_tensor(key[:, :, :], lg[:, :, :],
                                           top[:, 1, :].unsqueeze(2).broadcast_to([P, C, E]), ALU.is_ge))
                    link(dve.tensor_tensor(key[:, :, :], key[:, :, :], rev, ALU.mult))
                    link(dve.tensor_reduce(kmax[:, 1, :], key[:, :, :], AX.X, ALU.max))
                    link(dve.tensor_tensor(pick[:, 1, :, :], rev,
                                           kmax[:, 1, :].unsqueeze(2).broadcast_to([P, C, E]), ALU.is_equal))
                    dve.tensor_tensor(both[:, :, :], pick[:, 0, :, :], pick[:, 1, :, :], ALU.add
                                      ).then_inc(pick_ready[l], 1)
                    dve.wait_ge(ex_ready, 2)
                    link(dve.tensor_reduce(wt[:, 0, :], ex[:, :, :], AX.X, ALU.add))
                    link(dve.reciprocal(wt[:, 1, :], wt[:, 0, :]))
                    link(dve.tensor_tensor(wt[:, 2, :], ex2[:, :], wt[:, 1, :], ALU.mult))
                    link(dve.scalar_tensor_tensor(out=wt[:, 3, :], in0=wt[:, 1, :], scalar=1e-20, in1=wt[:, 2, :],
                                                  op0=ALU.add, op1=ALU.add))
                    link(dve.reciprocal(wt[:, 4, :], wt[:, 3, :]))
                    dve.tensor_copy(vals[:, :, 0:2],
                                    cst("tokval").rearrange("p (q k) -> p q k", k=2))
                    for j in range(2):
                        last = dve.tensor_tensor(vals[:, C * j:C * (j + 1), 2], wt[:, 1 + j, :], wt[:, 4, :], ALU.mult)
                    link(last)
                dve.wait_ge(rank_ps[l], 1)
                rank = b0[:, 0:C * E].rearrange("p (c e) -> p c e", e=E)
                count = b1[:, 0:E]
                link(dve.tensor_tensor(over[:, :, :], count.unsqueeze(2).broadcast_to([P, E, E]),
                                       cst("kstep").rearrange("p (e k) -> p e k", k=E), ALU.is_gt))
                link(dve.tensor_reduce(ntl[:, :], over[:, :, :], AX.X, ALU.add))
                link(dve.tensor_tensor(over[:, :, :], ntl[:, :].unsqueeze(1).broadcast_to([P, E, E]),
                                       cst("earlier").rearrange("p (e k) -> p e k", k=E), ALU.mult))
                link(dve.tensor_reduce(base[:, :], over[:, :, :], AX.X, ALU.add))
                link(dve.tensor_tensor(ends[:, :], base[:, :], ntl[:, :], ALU.add))
                link(dve.scalar_tensor_tensor(out=place[:, :, :], in0=base[:, :].unsqueeze(1).broadcast_to([P, C, E]),
                                              scalar=float(P), in1=rank, op0=ALU.mult, op1=ALU.add))
                link(dve.tensor_tensor(slots[:, 0:J2, :, :], pick[:, 0:J2, :, :],
                                       place[:, :, :].unsqueeze(1).broadcast_to([P, J2, C, E]), ALU.mult))
                q = J2 * C
                with nc.allow_low_precision(reason="slot numbers are integers below 4096"):
                    link(dve.tensor_reduce(slot[:, 0:q], slots[:, 0:J2, :, :].rearrange("p j c e -> p (j c) e"),
                                           AX.X, ALU.add))
                link(dve.tensor_scalar(lane[:, 0:q], slot[:, 0:q], P - 1, None, ALU.bitwise_and))
                dve.tensor_copy(lanef[:, 0:q], lane[:, 0:q])
                link(dve.tensor_tensor(tilef[:, 0:q], slot[:, 0:q], lane[:, 0:q], ALU.subtract))
                link(dve.tensor_tensor(intile[:, 0:q, 0:tiles], cst("tstep")[:, 0:tiles].unsqueeze(1).broadcast_to([P, q, tiles]),
                                       tilef[:, 0:q].unsqueeze(2).broadcast_to([P, q, tiles]), ALU.is_equal))
                k = (3, 2)[l]
                dve.tensor_tensor(tabv[:, 0:q, 0:k, 0:tiles], intile[:, 0:q, 0:tiles].unsqueeze(2).broadcast_to([P, q, k, tiles]),
                                  vals[:, 0:q, 0:k].unsqueeze(3).broadcast_to([P, q, k, tiles]), ALU.mult)
                for i in range(q):
                    last = dve.tensor_scalar(onehot[:, i, :], cst("iota"), lanef[:, i:i + 1], None, ALU.is_equal)
                last.then_inc(spread_ready[l], 1)
                link(dve.tensor_tensor(etile[:, 0:tiles, :], ends[:, :].unsqueeze(1).broadcast_to([P, tiles, E]),
                                       cst("tilecol").rearrange("p (t e) -> p t e", e=E)[:, 0:tiles], ALU.is_le))
                link(dve.tensor_reduce(esum[:, 0:tiles], etile[:, 0:tiles, :], AX.X, ALU.add))
                dve.tensor_scalar(expert[l][:, :], esum[:, 0:tiles], float(E - 1), None, ALU.min
                                  ).then_inc(experts_ready[l], 1)
                dve.wait_ge(table_ps[l], 1)
                table = b2[:, 0:k * tiles].rearrange("p (k t) -> p k t", k=k)
                beyond = float(4 * N)
                link(dve.tensor_scalar(padrow[:, 0:tiles], table[:, 1], 0.0, beyond, ALU.is_equal, ALU.mult))
                if l == 0:
                    dve.tensor_copy(slotw[:, :], table[:, 2])
                    dve.tensor_copy(token[l][:, :], table[:, 0])
                    dve.scalar_tensor_tensor(out=dest[l][:, :], in0=table[:, 1], scalar=-1.0,
                                             in1=padrow[:, 0:tiles], op0=ALU.add, op1=ALU.add
                                             ).then_inc(table_ready[l], 1)
                else:
                    dve.tensor_copy(token[l][:, :], table[:, 0])
                    dve.scalar_tensor_tensor(out=dest[l][:, :], in0=table[:, 0], scalar=0.0,
                                             in1=padrow[:, 0:tiles], op0=ALU.add, op1=ALU.add
                                             ).then_inc(table_ready[l], 1)

            route(0)


            def mix(l):
                tiles = (T0, T1)[l]
                rows_ = (FB0, P)[l]

                def step(n):
                    if l == 0 and (n < tiles):
                        dve.wait_ge(up_ps[0], n + 1)
                        dve.wait_ge(z_up, n + 1)
                        dve.tensor_tensor(z[n % 2][:, :], (b1, b3)[n % 2][:, 0:F0], z[n % 2][:, :], ALU.mult
                                          ).then_inc(z_ready, 1)
                    if 1 <= n <= tiles:
                        dve.wait_ge(hT_ps[l], n)
                        wait_past(dve, y_ps[l], n - 2)
                        dve.tensor_copy(hT[(n - 1) % 2][0:rows_, :], b4[0:rows_, :]).then_inc(hT_ready[l], 1)
                    if 2 <= n <= tiles + 1:
                        dve.wait_ge(y_ps[l], n - 1)
                        wait_past(dve, scattered[l][(n - 2) % 4], (n - 2) // 4 * 16)
                        source = psO[:, 0:D]
                        if l == 0:
                            weight = slotw[:, n - 2:n - 1]
                            dve.tensor_scalar(y[(n - 2) % 4][:, :], source, weight, None, ALU.mult
                                              ).then_inc(y_ready[l], 1)
                        else:
                            dve.wait_ge(kept, n - 1)
                            dve.tensor_tensor(y[(n - 2) % 4][:, :], source, keep[(n - 2) % 4][:, :], ALU.add
                                              ).then_inc(y_ready[l], 1)

                for n in range(tiles + 2):
                    step(n)

            mix(0)

            groups = [range(CB * b, CB * (b + 1)) for b in range(B)]
            spans = [slice(g[0], g[-1] + 1) for g in groups]
            for b, (cs, sp_) in enumerate(zip(groups, spans)):
                dve.wait_ge(back_s[b], 16)
                link(dve.tensor_tensor(y01[:, sp_, :], ybk[:, sp_, 0, :], ybk[:, sp_, 1, :], ALU.add))
                link(dve.tensor_tensor(x2[:, sp_, :], x1[:, sp_, :], y01[:, sp_, :], ALU.add))
                dve.wait_ge(rstd_ready, stats(x2[:, :, :], stat2, mv2, rstd2, cs))
                for c in cs:
                    normal(x2n[:, c, :], x2[:, :, :], mv2, rstd2, c).then_inc(x2n_ready, 1)
            for b, sp_ in enumerate(spans):
                s2 = (b2, b3)[b][:, 0:CB * M].rearrange("p (c m) -> p c m", m=M)
                dve.wait_ge(s2_ps, b + 1)
                link(dve.tensor_reduce(smax2[:, sp_], s2, AX.X, ALU.max))
                dve.tensor_tensor(prob2[:, sp_, :], s2, smax2[:, sp_].unsqueeze(2).broadcast_to([P, CB, M]),
                                  ALU.subtract).then_inc(sub2_ready, 1)
            for b, sp_ in enumerate(spans):
                dve.wait_ge(exp2_ready, b + 1)
                link(dve.tensor_reduce(ssum2[:, sp_], prob2[:, sp_, :], AX.X, ALU.add))
                link(dve.reciprocal(rsum2[:, sp_], ssum2[:, sp_]))
            for b, (cs, sp_) in enumerate(zip(groups, spans)):
                dve.wait_ge(o2_ps, b + 1)
                dve.tensor_tensor(o2[:, sp_, :], psO[:, :].rearrange("p (c d) -> p c d", c=CB),
                                  rsum2[:, sp_].unsqueeze(2).broadcast_to([P, CB, D]), ALU.mult
                                  ).then_inc(x3_ready, 1)
                dve.wait_ge(x3_ready, b + 1)
                link(dve.tensor_tensor(row1[:, sp_, 1, :], o2[:, sp_, :], x2[:, sp_, :], ALU.add))
                dve.wait_ge(rstd_ready, stats(row1[:, :, 1, :], stat3, mv3, rstd3, cs))
                for c in cs:
                    last = normal(row1[:, c, 0, :], row1[:, :, 1, :], mv3, rstd3, c)
                last.then_inc(row1_ready, 1)

            route(1)
            mix(1)

        @block.scalar
        def _(act):
            def gate_rows(c):
                act.wait_ge(xfT_ps, c + 1)
                if c >= 2:
                    act.wait_ge(logit_ps, c - 1)
                act.copy(xfT[:, c % 2, :], mis_xT).then_inc(xfT_ready, 1)

            act.wait_ge(small_s, 64)
            for b in range(B):
                act.wait_ge(xT_ps, b + 1)
                act.activation(xnT[:, 512 * b:512 * (b + 1)], (b0, b1)[b], ACT.Identity, bias=vec("lnqb"),
                               scale=vec("lnqw")).then_inc(xnT_ready, 1)

            for g in range(G + 8):
                if g < G:
                    act.wait_ge(sub_ready, g + 1)
                    act.activation(prob[:, g % 3, 0:W], prob[:, g % 3, 0:W], ACT.Exp).then_inc(exp_ready, 1)
                if 2 <= g < G + 2:
                    act.wait_ge(pT_ps, g - 1)
                    if g >= 4:
                        act.wait_ge(o_ps, g - 3)
                    act.copy(probT[:, g % 2, :], psT[:, 0:WP]).then_inc(pT_ready, 1)
                if g >= 5 and g % 2 == 1 and (g - 5) // 2 < C:
                    c = (g - 5) // 2
                    act.wait_ge(onT_ps, c + 1)
                    if c >= 2:
                        act.wait_ge(xfT_ps, c - 1)
                    if c >= 2:
                        act.wait_ge(out_ps, c - 1)
                    act.activation(onT[:, c % 2, :], mis_onT, ACT.Identity, bias=vec("bv")).then_inc(onT_ready, 1)
                if g >= 9 and g % 2 == 1 and (g - 9) // 2 < C:
                    gate_rows((g - 9) // 2)
            act.wait_ge(l_less[0], 1)
            act.activation(ex[:, :, :], lg2[:, :, :], ACT.Exp).then_inc(ex_ready, 1)
            act.wait_ge(l_less[0], 2)
            act.activation(ex2[:, :], top[:, 1, :], ACT.Exp).then_inc(ex_ready, 1)

            def mix(l):
                tiles = (T0, T1)[l]

                def take(n):
                    act.wait_ge(xsT_ps[l], n + 1)
                    wait_past(act, up_ps[l], n - 1)
                    act.copy(xsT[n % 2][:, :], psX[:, 0:P]).then_inc(xsT_ready[l], 1)
                    if l == 1:
                        wait_past(act, y_ready[1], n - 3)
                        act.copy(keep[n % 4][:, :], xs[n % 4][:, D:2 * D]).then_inc(kept, 1)

                def step(n):
                    if n + 1 < tiles:
                        take(n + 1)
                    if n < tiles:
                        wait_past(act, hT_ps[l], n - 1)
                        if l == 0:
                            act.wait_ge(up_half, n + 1)
                            act.copy(z[n % 2][:, :], (b0, b2)[n % 2][:, 0:F0]).then_inc(z_up, 1)
                            act.wait_ge(z_ready, n + 1)
                            act.activation(h[n % 2][:, 0:F0], z[n % 2][:, :], ACT.Silu).then_inc(h_ready[0], 1)
                        else:
                            act.wait_ge(up_ps[1], n + 1)
                            act.activation(h[n % 2][:, :], (b0, b1)[n % 2], ACT.Gelu).then_inc(h_ready[1], 1)

                take(0)
                for n in range(tiles + 2):
                    step(n)

            mix(0)

            for b in range(B):
                act.wait_ge(x2T_ps, b + 1)
                act.copy(x2T[:, CB * b:CB * (b + 1), :].rearrange("p c t -> p (c t)"), (b0, b1)[b]
                         ).then_inc(x2T_ready, 1)
            for b in range(B):
                act.wait_ge(sub2_ready, b + 1)
                p2 = prob2[:, CB * b:CB * (b + 1), :].rearrange("p c m -> p (c m)")
                act.activation(p2, p2, ACT.Exp, scale=float(D) ** -0.5).then_inc(exp2_ready, 1)
            for b in range(B):
                act.wait_ge(p2T_ps, b + 1)
                act.copy(prob2T[:, CB * b:CB * (b + 1), :].rearrange("m c t -> m (c t)"), (b4, b5)[b][0:M, :]
                         ).then_inc(p2T_ready, 1)
            for b in range(B):
                act.wait_ge(x3T_ps, b + 1)
                act.copy(x3T[:, CB * b:CB * (b + 1), :].rearrange("p c t -> p (c t)"), (b0, b1)[b]
                         ).then_inc(x3T_ready, 1)

            mix(1)

        @block.tensor
        def _(pe):
            pe.wait_ge(const_s, 16)
            pe.wait_ge(cn_ready, B)
            for source, k in ((cn, 0), (ctx, 1)):
                for b in range(B):
                    i = k * B + b
                    last = pe.transpose(b5[:, i * M:(i + 1) * M], source[:, b, :], ident[0:M, 0:M])
                last.then_inc(ctxT_ps, 1)
            pe.wait_ge(small_s, 64)
            pe.wait_ge(ctxT_ready, 3)
            pe.matmul(psX[:, 0:B * M], wk, ckT[:, :, :].rearrange("p b m -> p (b m)"), start=True, stop=True
                      ).then_inc(k_ps, 1)
            for b in range(B):
                last = pe.matmul(psO[0:M, b * D:(b + 1) * D], cvT[:, b, :], wv, start=True, stop=True)
            last.then_inc(v_ps, 1)

            def queries(b):
                pe.wait_ge(xn_ready, CB * (b + 1))
                for c in range(CB):
                    last = pe.transpose((b0, b1)[b][:, P * c:P * (c + 1)], xn[:, CB * b + c, :], ident)
                last.then_inc(xT_ps, 1)
                pe.wait_ge(xnT_ready, b + 1)
                pe.matmul((b2, b3)[b], wq, xnT[:, 512 * b:512 * (b + 1)], start=True, stop=True).then_inc(q_ps, 1)

            queries(0)
            pe.wait_ge(v_ready, 1)
            for b in range(B):
                if b:
                    pe.wait_ge(vblk_ready, b)
                for j in range(J):
                    last = pe.matmul(psT[:, P * j:P * (j + 1)], cst("sel", M)[:, P * j:P * (j + 1)], v[:, b, :],
                                     start=True, stop=True)
                last.then_inc(vv_ps, 1)
            queries(1)

            def scores(g):
                c, s = g // 2, g % 2
                b = c // CB
                if g == 0:
                    pe.wait_ge(q_ready, B)
                if g % G == 0 or g == G // 2:
                    pe.wait_ge(kblk_ready, b + 1)
                if g >= 2:
                    pe.wait_ge(sub_ready, g - 1)
                keys = kblk[:, b, HH * s:HH * (s + 1), :].rearrange("p h m -> p (h m)")
                pe.matmul(psS[g % 2][:, 0:512], qT[:, P * c:P * (c + 1)], keys[:, 0:512], start=True, stop=True)
                pe.matmul(psS[g % 2][:, 512:W], qT[:, P * c:P * (c + 1)], keys[:, 512:W], start=True, stop=True
                          ).then_inc(s_ps, 1)

            def turn(g):
                pe.wait_ge(exp_ready, g + 1)
                if g >= 1:
                    pe.wait_ge(pT_ready, g)
                else:
                    pe.wait_ge(vblk_ready, B)
                for j in range(J):
                    last = pe.transpose(psT[:, P * j:P * (j + 1)], prob[:, g % 3, P * j:P * (j + 1)], ident)
                last.then_inc(pT_ps, 1)

            def attend(g):
                c, s = g // 2, g % 2
                pe.wait_ge(pT_ready, g + 1)
                if s == 0 and c >= 1:
                    pe.wait_ge(on_ready, c)
                for j in range(J):
                    ha, hb = P * j // M, min((P * (j + 1) - 1) // M, HH - 1) + 1
                    a = OW * (HH * s + ha)
                    last = pe.matmul(psO[:, a:a + OW * (hb - ha)], probT[:, g % 2, P * j:P * (j + 1)],
                                     vblk[:, c // CB, s, j, ha:hb, :].rearrange("p h w -> p (h w)"),
                                     start=(j == 0), stop=(j == J - 1), skip_group_check=True)
                last.then_inc(o_ps, 1)

            for g in range(G + 9):
                if g < G:
                    scores(g)
                if 2 <= g < G + 2:
                    turn(g - 2)
                if 3 <= g < G + 3:
                    attend(g - 3)
                c = (g - 5) // 2
                if g >= 5 and g % 2 == 1 and c < C:
                    pe.wait_ge(on_ready, c + 1)
                    if c >= 1:
                        pe.wait_ge(x1_ready, c)
                    pe.transpose(mis_onT, on[:, c % 2, :], ident).then_inc(onT_ps, 1)
                c = (g - 9) // 2
                if g >= 9 and g % 2 == 1 and c < C:
                    pe.wait_ge(xf_ready, c + 1)
                    pe.wait_ge(x1_ready, min(c + 2, C))
                    pe.transpose(mis_xT, xf[:, c, :], ident).then_inc(xfT_ps, 1)
                c = (g - 10) // 2
                if g >= 10 and g % 2 == 0 and c < C:
                    pe.wait_ge(xfT_ready, c + 1)
                    if c + 2 < C:
                        pe.wait_ge(onT_ready, c + 3)
                    pe.matmul(logit[:, c, :], xfT[:, c % 2, :], gate[:, 0, :], start=True, stop=True
                              ).then_inc(logit_ps, 1)
                c = (g - 6) // 2
                if g >= 6 and g % 2 == 0 and c < C:
                    pe.wait_ge(onT_ready, c + 1)
                    pe.matmul(mis_out, onT[:, c % 2, :], wo, start=True, stop=True).then_inc(out_ps, 1)

            def route(l):
                chosen = both[:, :, :] if l == 0 else pick[:, 0, :, :]
                pe.wait_ge(pick_ready[l], 1)
                pe.matmul(b0[:, 0:C * E], cst("before"), chosen.rearrange("p c e -> p (c e)"), start=True, stop=False,
                          skip_group_check=True)
                for s in range(1, C):
                    pe.matmul(b0[:, s * E:C * E], cst("ones"), chosen[:, 0:C - s, :].rearrange("p c e -> p (c e)"),
                              start=False, stop=(s == C - 1), skip_group_check=True)
                for c in range(C):
                    last = pe.matmul(b1[:, 0:E], cst("ones"), chosen[:, c, :], start=(c == 0), stop=(c == C - 1))
                last.then_inc(rank_ps[l], 1)
                pe.wait_ge(spread_ready[l], 1)
                q, k, tiles = ((2 * C, 3, T0), (C, 2, T1))[l]
                for i in range(q):
                    last = pe.matmul(b2[:, 0:k * tiles].rearrange("p (k t) -> p k t", k=k), onehot[:, i, :],
                                     tabv[:, i, 0:k, 0:tiles], start=(i == 0), stop=(i == q - 1))
                last.then_inc(table_ps[l], 1)
                pe.wait_ge(experts_ready[l], 1)

            def mix(l):
                tiles = (T0, T1)[l]

                its = {}

                def choose(n):
                    its[n] = pe.value_load(expert[l][0:1, n:n + 1], min_val=0, max_val=E - 1)

                def take(n):
                    pe.wait_ge(gathered[l][n % 4], (n // 4 + 1) * 16)
                    wait_past(pe, xsT_ready[l], n)
                    pe.transpose(psX[:, 0:P], xs[n % 4][:, 0:D], ident
                                 ).then_inc(xsT_ps[l], 1)

                def up(n):
                    e = its[n]
                    pe.wait_ge(xsT_ready[l], n + 1)
                    wait_past(pe, (z_ready, h_ready[1])[l], n - 1)
                    if l == 0:
                        for k, target in enumerate(((b0, b1), (b2, b3))[n % 2]):
                            pe.matmul(target[:, 0:F0], xsT[n % 2][:, :], wgu[:, bass.ds(e * (2 * F0) + (1 - k) * F0, F0)],
                                      start=True, stop=False)
                            last = pe.matmul(target[:, 0:F0], ones3[:, :], bias3[:, bass.ds(e * BI0 + (1 - k) * F0, F0)],
                                             start=False, stop=True)
                            if k == 0:
                                last.then_inc(up_half, 1)
                    else:
                        target = (b0, b1)[n % 2]
                        pe.matmul(target, xsT[n % 2][:, :], w1[:, bass.ds(e * F1, F1)], start=True, stop=False)
                        last = pe.matmul(target, ones3[:, :], bias3[:, bass.ds(e * BI1 + E * BI0, F1)],
                                         start=False, stop=True)
                    last.then_inc(up_ps[l], 1)

                def turn(n):
                    pe.wait_ge(h_ready[l], n + 1)
                    wait_past(pe, hT_ready[l], n)
                    f = (FB0, P)[l]
                    for k in range(K0):
                        last = pe.transpose(b4[0:f, P * k:P * (k + 1)], h[n % 2][:, f * k:f * (k + 1)], ident)
                    last.then_inc(hT_ps[l], 1)

                def down(n):
                    e = its.pop(n)
                    pe.wait_ge(hT_ready[l], n + 1)
                    wait_past(pe, y_ready[l], n)
                    f = (FB0, P)[l]
                    target = psO[:, 0:D]
                    w, stride, b_at = ((dw, K0 * D, e * BI0 + 2 * F0), (w2, K1 * D, e * BI1 + (E * BI0 + F1)))[l]
                    for k in range(K0):
                        pe.matmul(target, hT[n % 2][0:f, P * k:P * (k + 1)], w[:, bass.ds(e * stride + k * D, D)],
                                  start=(k == 0), stop=False)
                    pe.matmul(target, ones3[:, :], bias3[:, bass.ds(b_at, D)], start=False, stop=True
                              ).then_inc(y_ps[l], 1)

                def step(n):
                    if n + 1 < tiles:
                        take(n + 1)
                    if n < tiles:
                        up(n)
                    if 1 <= n <= tiles:
                        turn(n - 1)
                    if n + 1 < tiles:
                        choose(n + 1)
                    if 2 <= n <= tiles + 1:
                        down(n - 2)

                pe.wait_ge((f0_w, f1_w)[l], (48, 32)[l])
                choose(0)
                take(0)
                for n in range(tiles + 2):
                    step(n)

            route(0)
            pe.wait_ge(bias3_s, 16)
            pe.wait_ge(pool_step, 4)
            mix(0)

            for b in range(B):
                pe.wait_ge(x2n_ready, CB * (b + 1))
                for c in range(CB):
                    last = pe.transpose((b0, b1)[b][:, P * c:P * (c + 1)], x2n[:, CB * b + c, :], ident)
                last.then_inc(x2T_ps, 1)
                pe.wait_ge(x2T_ready, b + 1)
                for c in range(CB):
                    last = pe.matmul((b2, b3)[b][:, M * c:M * (c + 1)], x2T[:, CB * b + c, :], cT[:, b, :],
                                     start=True, stop=True)
                last.then_inc(s2_ps, 1)
            for b in range(B):
                pe.wait_ge(exp2_ready, b + 1)
                for c in range(CB):
                    last = pe.transpose((b4, b5)[b][0:M, P * c:P * (c + 1)], prob2[:, CB * b + c, :], ident)
                last.then_inc(p2T_ps, 1)
            for b in range(B):
                pe.wait_ge(p2T_ready, b + 1)
                if b:
                    pe.wait_ge(x3_ready, b)
                for c in range(CB):
                    last = pe.matmul(psO[:, D * c:D * (c + 1)], prob2T[:, CB * b + c, :], ctx[:, b, :],
                                     start=True, stop=True)
                last.then_inc(o2_ps, 1)
            for b in range(B):
                pe.wait_ge(row1_ready, b + 1)
                for c in range(CB):
                    last = pe.transpose((b0, b1)[b][:, P * c:P * (c + 1)], row1[:, CB * b + c, 0, :], ident)
                last.then_inc(x3T_ps, 1)
                pe.wait_ge(x3T_ready, b + 1)
                for c in range(CB * b, CB * (b + 1)):
                    pe.matmul(logit[:, c, :], x3T[:, c, :], gate[:, 1, :], start=True, stop=True
                              ).then_inc(logit1_ps, 1)
            route(1)
            mix(1)


def constant_table():
    import numpy as np

    p = np.arange(P)[:, None]
    parts = {}
    parts["ident"] = np.eye(P)
    parts["headmask"] = p // DH == np.arange(H)[None, :]
    j, hh = np.arange(J)[:, None], np.arange(HH)[None, :]
    flat = P * j[None] + p[:, :, None]
    parts["blockmask"] = flat // M == hh[None]
    sel = np.zeros((P, WP))
    sel[np.arange(W) % M, np.arange(W)] = 1
    parts["sel"] = sel
    parts["before"] = p < np.arange(P)[None, :]
    parts["ones"] = np.ones((P, P))
    e = np.arange(E)
    one = np.ones((P, 1))
    parts["rev"] = one * np.tile(E - e, C)[None]
    parts["kstep"] = one * np.tile(P * e, E)[None]
    parts["earlier"] = one * (e[None, :] < e[:, None]).reshape(1, -1)
    parts["iota"] = one * np.arange(P)[None]
    parts["tstep"] = one * (P * np.arange(T0))[None]
    parts["tilecol"] = one * np.repeat(np.arange(T0), E)[None]
    q = np.arange(2 * C)[None, :]
    tok = P * (q % C) + p
    parts["tokval"] = np.stack([tok, 2 * tok + q // C + 1], 2)
    return np.concatenate([parts[name].reshape(P, n) for name, n in CONST_PARTS], 1).astype(np.float32)


def kernel(**inputs):
    import numpy as np
    import concourse.bacc as bacc
    from concourse.bass_utils import run_bass_kernel_spmd

    a = {k: np.asarray(val) for k, val in inputs.items()}
    f0, f1, x0 = "L0_ffn_", "L1_ffn_", "L0_xattn_"
    arrays = {
        "x": a["x"],
        "ctx": a["ctx_1024"],
        "wqkvo": np.stack([a[x0 + w] for w in ("Wq", "Wk", "Wv", "Wo")], 1),
        "vecs": np.stack([a[x0 + w] for w in ("ln_q_w", "ln_q_b", "ln_k_w", "ln_k_b", "ln_v_w", "ln_v_b",
                                              "bq", "bk", "bv")], 1),
        "rows": np.concatenate([a[x0 + "bo"], a[f0 + "gate_b"], a[f1 + "br"]]),
        "consts": constant_table(),
        "gate": np.stack([a[f0 + "gate_w"].T, a[f1 + "wr"]], 1),
        "wgu": np.stack([a[f0 + "gp_w"], a[f0 + "up_w"]], 1).transpose(3, 0, 1, 2).reshape(P, -1),
        "dw": a[f0 + "down_w"].reshape(E, D, K0, FB0).transpose(3, 0, 2, 1).reshape(FB0, -1),
        "w1": a[f1 + "w1"].transpose(1, 0, 2).reshape(P, -1),
        "w2": a[f1 + "w2"].reshape(E, K1, P, D).transpose(2, 0, 1, 3).reshape(P, -1),
        "bias": np.concatenate([np.concatenate([a[f0 + "gp_b"], a[f0 + "up_b"], a[f0 + "down_b"]], 1).ravel(),
                                np.concatenate([a[f1 + "b1"], a[f1 + "b2"]], 1).ravel()]).reshape(P, BC),
    }
    arrays = {f"in_{k}": np.ascontiguousarray(val) for k, val in arrays.items()}
    nc = bacc.Bacc("TRN2", target_bir_lowering=False, num_devices=1)
    aps = [nc.dram_tensor(k, val.shape, mybir.dt.from_np(val.dtype), kind="ExternalInput").ap()
           for k, val in arrays.items()]
    out = nc.dram_tensor("out", (N, D), F32, kind="ExternalOutput").ap()
    two_blocks(nc, *aps, out)
    r = run_bass_kernel_spmd(nc, [arrays], core_ids=[0])
    return r.results[0]["out"].reshape(B, N // B, D)
```

```python
from contextlib import ExitStack

import concourse.bass as bass
from concourse import mybir

F32 = mybir.dt.float32
BF16 = mybir.dt.bfloat16
I32 = mybir.dt.int32
U32 = mybir.dt.uint32
ALU = mybir.AluOpType
ACT = mybir.ActivationFunctionType
AX = mybir.AxisListType

P = 128
D = 128
B = 2
C = 8
CB = C // B
N = C * P
M = 77
H = 16
DH = D // H
HH = H // 2
W = HH * M
J = -(-W // P)
WP = J * P
OW = DH + 1
G = C * 2
E = 8
F0 = 408
K0 = 4
FB0 = F0 // K0
F1 = 512
K1 = 4
T0 = 2 * N // P + E - 1
T1 = N // P + E - 1
BI0 = 2 * F0 + D
BI1 = F1 + D
BIAS = E * (BI0 + BI1)
BC = BIAS // P
EPS = 1e-5
NEG = -3.0e38

CONST_PARTS = [("ident", P), ("headmask", H), ("blockmask", J * HH), ("sel", WP), ("before", P),
               ("ones", P), ("iota", P), ("rev", C * E), ("kstep", E * E), ("earlier", E * E),
               ("tstep", T0), ("tilecol", T0 * E), ("tokval", 2 * C * 2), ("lane", 1)]
FIRST_CONSTS = 4
RING = 6
CONST_AT = {}
_at = 0
for _name, _n in CONST_PARTS:
    CONST_AT[_name] = (_at, _at + _n)
    _at += _n
CONSTS = _at
CONST_SPLIT = CONST_AT[CONST_PARTS[FIRST_CONSTS][0]][0]
VECS = ["lnqw", "lnqb", "lnkw", "lnkb", "lnvw", "lnvb", "bq", "bk", "bv"]
ROWS = D + 2 * E


def two_blocks(nc, x_in, ctx_in, wqkvo_in, vecs_in, rows_in, consts_in, gate_in, wgu_in,
               dw_in, w1_in, w2_in, bias_in, out):
    stack = ExitStack()
    with stack:
        def sb(name, shape, dt=F32):
            return stack.enter_context(nc.sbuf_tensor(name, shape, dt))

        def bank(name, columns=512):
            return stack.enter_context(nc.psum_tensor(name, [P, columns], F32))

        def sem(name):
            return stack.enter_context(nc.semaphore(name))

        rows0 = nc.dram_tensor("rows0", (N, D), F32).ap()
        back0 = nc.dram_tensor("back0", (2 * N, D), F32).ap()
        rows1 = nc.dram_tensor("rows1", (N, 2 * D), F32).ap()
        parts = nc.dram_tensor("parts", (3, BIAS), BF16).ap()

        x = sb("x", [P, C, D])
        ctx = sb("ctx", [M, B, D])
        wqkvo = sb("wqkvo", [P, 4, D])
        vecs = sb("vecs", [P, len(VECS)])
        rows = sb("rows", [P, ROWS])
        consts = sb("consts", [P, CONSTS])
        gate = sb("gate", [P, 2, E])
        wgu = sb("wgu", [P, E * 2 * F0])
        dw = sb("dw", [FB0, E * K0 * D])
        w1 = sb("w1", [P, E * F1])
        w2 = sb("w2", [P, E * K1 * D])
        bias = sb("bias", [P, BC])
        part = sb("part", [P, 3, BC], BF16)
        rest = sb("rest", [P, 2, BC])
        bias3 = sb("bias3", [3, BIAS], BF16)
        ones3 = sb("ones3", [3, P], BF16)

        stat = sb("stat", [P, C, 6])
        mv = sb("mv", [P, C, 2])
        rstd = sb("rstd", [P, C])
        cstat = sb("cstat", [M, B, 6])
        cmv = sb("cmv", [M, B, 2])
        crstd = sb("crstd", [M, B])
        xn = sb("xn", [P, C, D])
        cn = sb("cn", [M, B, D])
        xbo = sb("xbo", [P, C, D])
        xnT = sb("xnT", [P, N])
        cT = sb("cT", [P, B, M])
        ckT = sb("ckT", [P, B, M])
        cvT = sb("cvT", [P, B, M])
        qT = sb("qT", [P, N])
        kT = sb("kT", [P, B, M])
        v = sb("v", [M, B, D])
        kblk = sb("kblk", [P, B, H, M])
        vblk = sb("vblk", [P, B, 2, J, HH, OW])
        smax = sb("smax", [P, 2, HH])
        prob = sb("prob", [P, 3, WP])
        probT = sb("probT", [P, 2, WP])
        rsum = sb("rsum", [P, H])
        on = sb("on", [P, 2, D])
        onT = sb("onT", [P, 2, D])
        x1 = sb("x1", [P, C, D])
        stat1 = sb("stat1", [P, C, 6])
        mv1 = sb("mv1", [P, C, 2])
        rstd1 = sb("rstd1", [P, C])
        neghalf = sb("neghalf", [P, C])
        idle = sb("idle", [P, 1])
        xf = sb("xf", [P, C, D])
        xfT = sb("xfT", [P, 2, D])

        lg = sb("lg", [P, C, E])
        lg2 = sb("lg2", [P, C, E])
        key = sb("key", [P, C, E])
        top = sb("top", [P, 2, C])
        kmax = sb("kmax", [P, 2, C])
        pick = sb("pick", [P, 2, C, E], BF16)
        both = sb("both", [P, C, E], BF16)
        ex = sb("ex", [P, C, E])
        ex2 = sb("ex2", [P, C])
        wt = sb("wt", [P, 5, C])
        weight = sb("weight", [P, 2, C])
        ntl = sb("ntl", [P, E])
        over = sb("over", [P, E, E])
        base = sb("base", [P, E])
        ends = sb("ends", [P, E])
        place = sb("place", [P, C, E])
        slots = sb("slots", [P, 2, C, E])
        slot = sb("slot", [P, 2 * C], I32)
        lane = sb("lane", [P, 2 * C], I32)
        lanef = sb("lanef", [P, 2 * C])
        tilef = sb("tilef", [P, 2 * C])
        intile = sb("intile", [P, 2 * C, T0], BF16)
        tabv = prob[:, :, :].rearrange("p i w -> p (i w)")[:, 0:3 * C * T0].bitcast(BF16).rearrange(
            "p (q k t) -> p q k t", q=2 * C, k=3)
        counts = sb("counts", [P, 3 * P], BF16)
        onehot = probT[:, :, :].rearrange("p i w -> p (i w)")[:, 0:C * P].bitcast(BF16).rearrange(
            "p (q s) -> p q s", q=2 * C)
        slottok = sb("slottok", [P, T0])
        etile = sb("etile", [P, T0, E])
        esum = sb("esum", [P, T0])
        padrow = sb("padrow", [P, T0])

        expert = [sb(f"expert{l}", [P, t], I32) for l, t in enumerate((T0, T1))]
        token = [sb(f"token{l}", [P, t], U32) for l, t in enumerate((T0, T1))]
        dest = [sb(f"dest{l}", [P, t], U32) for l, t in enumerate((T0, T1))]

        xs = [sb(f"xs{i}", [P, 2 * D]) for i in range(RING)]
        xsT = [sb(f"xsT{i}", [P, P]) for i in range(2)]
        z = [sb(f"z{i}", [P, F0]) for i in range(2)]
        h = [sb(f"h{i}", [P, F1]) for i in range(2)]
        hT = [sb(f"hT{i}", [P, K1 * P]) for i in range(2)]
        keep = [sb(f"keep{i}", [P, D]) for i in range(4)]
        y = [sb(f"y{i}", [P, D]) for i in range(4)]

        x2n, o2 = xn, x
        x2T = xnT[:, :].rearrange("p (c t) -> p c t", c=C)
        x3T = qT[:, :].rearrange("p (c t) -> p c t", c=C)
        ybk = kblk[:, :, :, :].rearrange("p b h m -> p (b h m)")[:, 0:C * 2 * D].rearrange(
            "p (c j d) -> p c j d", c=C, j=2)
        x2 = wgu[:, 0:N].rearrange("p (c d) -> p c d", c=C)
        row1 = wgu[:, N:3 * N].rearrange("p (c j d) -> p c j d", c=C, j=2)
        prob2T = wgu[0:M, 3 * N:4 * N].rearrange("p (c t) -> p c t", c=C)
        prob2 = wgu[:, 4 * N:4 * N + C * M].rearrange("p (c m) -> p c m", c=C)
        stat2 = sb("stat2", [P, C, 6])
        mv2 = sb("mv2", [P, C, 2])
        rstd2 = sb("rstd2", [P, C])
        smax2 = sb("smax2", [P, C])
        ssum2 = sb("ssum2", [P, C])
        rsum2 = sb("rsum2", [P, C])
        stat3 = sb("stat3", [P, C, 6])
        mv3 = sb("mv3", [P, C, 2])
        rstd3 = sb("rstd3", [P, C])

        psS = [bank("psS0", 1024), bank("psS1", 1024)]
        psT = bank("psT", 1024)
        psO = bank("psO")
        psX = bank("psX")
        b0, b1, b2, b3 = psS[0][:, 0:512], psS[0][:, 512:1024], psS[1][:, 0:512], psS[1][:, 512:1024]
        b4, b5 = psT[:, 0:512], psT[:, 512:1024]
        mis_onT, mis_out, mis_xT = psX[:, 0:128], psX[:, 128:256], psX[:, 256:384]
        logit = psX[:, 384:448].rearrange("p (c e) -> p c e", e=E)

        def wait_past(eng, semaphore, count):
            if count > 0:
                eng.wait_ge(semaphore, count)

        def cst(name, partitions=P):
            a, b = CONST_AT[name]
            return consts[0:partitions, a:b]

        def vec(name):
            i = VECS.index(name)
            return vecs[:, i:i + 1]

        ident = cst("ident")
        wq, wk, wv, wo = (wqkvo[:, i, :] for i in range(4))
        bo_row, gateb_row, br_row = rows[:, 0:D], rows[:, D:D + E], rows[:, D + E:D + 2 * E]

        x_in_s = [sem(f"x_loaded{b}") for b in range(B)]
        small_s = sem("attention_weights_loaded")
        rows_s = sem("row_vectors_loaded")
        ctx_s = sem("ctx_loaded")
        const_s = sem("first_consts_loaded")
        const2_s = sem("other_consts_loaded")
        counts_ready = sem("counts_ready")
        bias_s = sem("bias_loaded")
        parts_ready = sem("bias_parts_ready")
        parts_stored = sem("bias_parts_stored")
        bias3_s = sem("bias3_loaded")
        f0_w = sem("mixture0_weights_loaded")
        f1_w = sem("mixture1_weights_loaded")
        pool_step = sem("pool_step")
        var_ready = sem("variances_ready")
        rstd_ready = sem("rstd_ready")
        dve_step = sem("dve_step")
        xn_ready = sem("xn_ready")
        cn_ready = sem("cn_ready")
        ctxT_ps = sem("ctxT_in_psum")
        ctxT_ready = sem("ctxT_ready")
        xT_ps = sem("xT_in_psum")
        xnT_ready = sem("xnT_ready")
        table_taken = sem("function_table_taken")
        k_ps = sem("k_in_psum")
        kT_ready = sem("kT_ready")
        v_ps = sem("v_in_psum")
        v_ready = sem("v_ready")
        vv_ps = sem("v_spread_in_psum")
        vblk_ready = sem("vblk_ready")
        q_ps = sem("q_in_psum")
        q_ready = sem("q_ready")
        kblk_ready = [sem(f"kblk_ready{b}") for b in range(B)]
        ones_column = sem("ones_columns_ready")
        xbo_ready = sem("xbo_ready")
        prob_zero = sem("prob_padding_zero")
        s_ps = sem("scores_in_psum")
        sub_ready = sem("scores_less_max_ready")
        exp_ready = sem("exp_ready")
        pT_ps = sem("probT_in_psum")
        pT_ready = sem("probT_ready")
        o_ps = sem("heads_in_psum")
        on_ready = sem("heads_normalized")
        onT_ps = sem("headsT_in_psum")
        onT_ready = sem("headsT_ready")
        out_ps = sem("projection_in_psum")
        x1_ready = sem("x1_ready")
        xf_ready = sem("xf_ready")
        xf_stored = sem("xf_stored")
        xfT_ps = sem("xfT_in_psum")
        xfT_ready = sem("xfT_ready")
        logit_ps = sem("gate_logits_in_psum")

        l_less = [sem(f"logits_less_max{l}") for l in range(2)]
        ex_ready = sem("gate_exp_ready")
        pick_ready = [sem(f"picks_ready{l}") for l in range(2)]
        rank_ps = [sem(f"ranks_in_psum{l}") for l in range(2)]
        spread_ready = [sem(f"slots_spread{l}") for l in range(2)]
        table_ps = [sem(f"table_in_psum{l}") for l in range(2)]
        experts_ready = [sem(f"experts_ready{l}") for l in range(2)]
        token_ready = [sem(f"tokens_ready{l}") for l in range(2)]
        dest_ready = [sem(f"destinations_ready{l}") for l in range(2)]

        gathered = [[sem(f"gathered{l}_{i}") for i in range(RING)] for l in range(2)]
        xsT_ps = [sem(f"xsT_in_psum{l}") for l in range(2)]
        xsT_ready = [sem(f"xsT_ready{l}") for l in range(2)]
        up_ps = [sem(f"hidden_in_psum{l}") for l in range(2)]
        up_half = sem("up_in_psum")
        z_up = sem("up_ready")
        z_ready = sem("gated_ready")
        h_ready = [sem(f"hidden_ready{l}") for l in range(2)]
        hT_ps = [sem(f"hiddenT_in_psum{l}") for l in range(2)]
        hT_ready = [sem(f"hiddenT_ready{l}") for l in range(2)]
        y_ps = [sem(f"y_in_psum{l}") for l in range(2)]
        y_ready = [sem(f"y_ready{l}") for l in range(2)]
        scattered = [[sem(f"scattered{l}_{i}") for i in range(4)] for l in range(2)]

        back_s = [sem(f"rows_back{b}") for b in range(B)]
        kept = sem("residual_rows_kept")
        x2n_ready = sem("x2n_ready")
        x2T_ps = sem("x2T_in_psum")
        x2T_ready = sem("x2T_ready")
        s2_ps = sem("scores2_in_psum")
        sub2_ready = sem("scores2_less_max_ready")
        exp2_ready = sem("exp2_ready")
        p2T_ps = sem("prob2T_in_psum")
        p2T_ready = sem("prob2T_ready")
        o2_ps = sem("attended_in_psum")
        x3_ready = sem("x3_ready")
        row1_ready = sem("row1_ready")
        row1_stored = sem("row1_stored")
        x3T_ps = sem("x3T_in_psum")
        x3T_ready = sem("x3T_ready")
        logit1_ps = sem("router_logits_in_psum")

        block = stack.enter_context(nc.Block())

        @block.sync
        def _(sp):
            def load_x(b):
                sp.dma_start(x[:, CB * b:CB * (b + 1), :],
                             x_in[b].rearrange("(c p) d -> p c d", p=P)).then_inc(x_in_s[b], 16)

            load_x(0)
            sp.dma_start(ctx[:, :, :], ctx_in.rearrange("b m d -> m b d")).then_inc(ctx_s, 16)
            sp.dma_start(consts[:, 0:CONST_SPLIT], consts_in[:, 0:CONST_SPLIT]).then_inc(const_s, 16)
            sp.dma_start(vecs[:, :], vecs_in).then_inc(small_s, 16)
            sp.dma_start(wqkvo[:, :, :], wqkvo_in).then_inc(small_s, 16)
            load_x(1)
            sp.dma_start(consts[:, CONST_SPLIT:], consts_in[:, CONST_SPLIT:]).then_inc(const2_s, 16)
            sp.dma_start(rows[:, :], rows_in.partition_broadcast(P)).then_inc(rows_s, 16)
            sp.dma_start(gate[:, :, :], gate_in).then_inc(rows_s, 16)
            sp.dma_start(bias[:, :], bias_in).then_inc(bias_s, 16)
            half = E * F0
            sp.dma_start(wgu[:, 0:half], wgu_in[:, 0:half]).then_inc(f0_w, 16)
            sp.wait_ge(parts_ready, 3)
            for i in range(3):
                sp.dma_start(parts[i].rearrange("(p n) -> p n", p=P), part[:, i, :]).then_inc(parts_stored, 16)
            sp.dma_start(wgu[:, half:], wgu_in[:, half:]).then_inc(f0_w, 16)
            sp.wait_ge(parts_stored, 48)
            sp.dma_start(bias3[:, :], parts).then_inc(bias3_s, 16)
            sp.dma_start(dw[:, :], dw_in).then_inc(f0_w, 16)
            sp.dma_start(w1[:, :], w1_in).then_inc(f1_w, 16)
            sp.dma_start(w2[:, :], w2_in).then_inc(f1_w, 16)
            for c in range(C):
                sp.wait_ge(xf_ready, c + 1)
                sp.dma_start(rows0[P * c:P * (c + 1), :], xf[:, c, :]).then_inc(xf_stored, 16)
            for i in range(4):
                sp.wait_ge(scattered[0][i], 16 * len(range(i, T0, 4)))
            for b in range(B):
                sp.dma_start(ybk[:, CB * b:CB * (b + 1), :, :],
                             back0[2 * P * CB * b:2 * P * CB * (b + 1), :].rearrange(
                                 "(c p j) d -> p c j d", p=P, j=2)).then_inc(back_s[b], 16)
            for b in range(B):
                sp.wait_ge(row1_ready, b + 1)
                sp.dma_start(rows1[P * CB * b:P * CB * (b + 1), :].rearrange("(c p) d -> p c d", p=P),
                             row1[:, CB * b:CB * (b + 1), :, :].rearrange("p c j d -> p c (j d)")
                             ).then_inc(row1_stored, 16)
            for i in range(4):
                sp.wait_ge(scattered[1][i], 16 * len(range(i, T1, 4)))

        @block.gpsimd
        def _(pool):
            pool.memset(neghalf[:, :], -0.5).then_inc(pool_step, 1)
            pool.memset(ones3[:, :], 1.0).then_inc(pool_step, 1)
            roots = [0]

            def root(r):
                if roots[0] == 0:
                    pool.wait_ge(pool_step, 1)
                roots[0] += 1
                pool.wait_ge(var_ready, roots[0])
                pool.tensor_tensor(r, r, neghalf[0:r.shape[0], 0:r.shape[1]], ALU.pow).then_inc(rstd_ready, 1)

            pool.memset(prob[:, :, W:WP], 0.0).then_inc(prob_zero, 1)
            root(rstd[:, 0:CB])
            root(crstd[:, :])
            pool.wait_ge(const_s, 16)
            for b in range(B):
                for half in range(2):
                    pool.tensor_copy(vblk[:, b, half, :, :, DH],
                                     cst("blockmask").rearrange("p (j h) -> p j h", j=J)).then_inc(ones_column, 1)
            root(rstd[:, CB:C])
            pool.wait_ge(kT_ready, 1)
            pool.tensor_tensor(kblk[:, 1, :, :], kT[:, 1:2, :].broadcast_to([P, H, M]),
                               cst("headmask").unsqueeze(2).broadcast_to([P, H, M]), ALU.mult
                               ).then_inc(kblk_ready[1], 1)
            pool.wait_ge(const2_s, 16)
            small = CONST_AT["before"][0]
            pool.tensor_copy(counts[:, :], consts[:, small:small + 3 * P]).then_inc(counts_ready, 1)
            pool.wait_ge(rows_s, 32)
            for b in range(B):
                pool.wait_ge(x_in_s[b], 16)
                cs = slice(CB * b, CB * (b + 1))
                pool.tensor_tensor(xbo[:, cs, :], x[:, cs, :],
                                   bo_row.unsqueeze(1).broadcast_to([P, CB, D]), ALU.add).then_inc(xbo_ready, 1)
            pool.wait_ge(bias_s, 16)
            pool.tensor_copy(part[:, 0, :], bias[:, :]).then_inc(parts_ready, 1)
            pool.wait_ge(parts_ready, 1)
            pool.tensor_tensor(rest[:, 0, :], bias[:, :], part[:, 0, :], ALU.subtract).then_inc(pool_step, 1)
            pool.wait_ge(pool_step, 3)
            pool.tensor_copy(part[:, 1, :], rest[:, 0, :]).then_inc(parts_ready, 1)
            pool.wait_ge(parts_ready, 2)
            pool.tensor_tensor(rest[:, 1, :], rest[:, 0, :], part[:, 1, :], ALU.subtract).then_inc(pool_step, 1)
            pool.wait_ge(pool_step, 4)
            pool.tensor_copy(part[:, 2, :], rest[:, 1, :]).then_inc(parts_ready, 1)
            def gather(l, t):
                source, width = ((rows0, D), (rows1, 2 * D))[l]
                pool.indirect_dma_start(xs[t % RING][:, 0:width], None, source,
                                        bass.IndirectOffsetOnAxis(ap=token[l][:, t:t + 1], axis=0)
                                        ).then_inc(gathered[l][t % RING], 16)

            def scatter(l, t):
                target = (back0, out)[l]
                pool.indirect_dma_start(target, bass.IndirectOffsetOnAxis(ap=dest[l][:, t:t + 1], axis=0),
                                        y[t % 4][:, :], None, bounds_check=target.shape[0] - 1,
                                        oob_is_err=False).then_inc(scattered[l][t % 4], 16)

            for c in range(C):
                root(rstd1[:, c:c + 1])

            for l, tiles in enumerate((T0, T1)):
                if l == 1:
                    for source, target, m, r, done in ((x2, x2n, mv2, rstd2, x2n_ready),
                                                       (row1[:, :, 1, :], row1[:, :, 0, :], mv3, rstd3, row1_ready)):
                        for b in range(B):
                            root(r[:, CB * b:CB * (b + 1)])
                            pool.wait_ge(rstd_ready, roots[0])
                            for c in range(CB * b, CB * (b + 1)):
                                last = pool.tensor_scalar(target[:, c, :], source[:, c, :], m[:, c, 0:1],
                                                          r[:, c:c + 1], ALU.subtract, ALU.mult)
                            last.then_inc(done, 1)
                pool.wait_ge((xf_stored, row1_stored)[l], (16 * C, 16 * B)[l])
                pool.wait_ge(token_ready[l], 1)
                for t in range(RING):
                    gather(l, t)
                pool.wait_ge(dest_ready[l], 1)
                for t in range(tiles):
                    if t + RING < tiles:
                        pool.wait_ge(xsT_ps[l], t + 1)
                        if l == 1:
                            pool.wait_ge(kept, t + 1)
                        gather(l, t + RING)
                    pool.wait_ge(y_ready[l], t + 1)
                    scatter(l, t)

        @block.vector
        def _(dve):
            steps = [0]

            def link(ins):
                steps[0] += 1
                ins.then_inc(dve_step, 1)
                dve.wait_ge(dve_step, steps[0])

            rooted = [0]

            def stats(source, st, m, r, chunks, extra=0.0):
                n = source.shape[0]
                for c in chunks:
                    last = dve.bn_stats(st[0:n, c, :], source[:, c, :])
                link(last)
                for c in chunks:
                    last = dve.bn_aggr(m[0:n, c, :], st[0:n, c, :])
                link(last)
                a, b = chunks[0], chunks[-1] + 1
                dve.tensor_scalar(r[0:n, a:b], m[0:n, a:b, 1], 1.0 + extra, extra * extra if extra else EPS,
                                  ALU.mult, ALU.add).then_inc(var_ready, 1)
                rooted[0] += 1
                return rooted[0]

            def normal(target, source, m, r, c):
                n = source.shape[0]
                return dve.tensor_scalar(target, source[:, c, :], m[0:n, c, 0:1], r[0:n, c:c + 1],
                                         ALU.subtract, ALU.mult)

            def query_stats(b):
                dve.wait_ge(x_in_s[b], 16)
                stats(x[:, :, :], stat, mv, rstd, range(CB * b, CB * (b + 1)), extra=EPS)

            def query_rows(b):
                dve.wait_ge(rstd_ready, (1, 3)[b])
                for c in range(CB * b, CB * (b + 1)):
                    normal(xn[:, c, :], x[:, :, :], mv, rstd, c).then_inc(xn_ready, 1)

            def queries(b, source):
                dve.wait_ge(q_ps, b + 1)
                dve.tensor_scalar(qT[:, 512 * b:512 * (b + 1)], source, vec("bq"), DH ** -0.5,
                                  ALU.add, ALU.mult).then_inc(q_ready, 1)

            query_stats(0)
            dve.wait_ge(ctx_s, 16)
            stats(ctx[:, :, :], cstat, cmv, crstd, range(B))
            query_rows(0)
            dve.wait_ge(rstd_ready, 2)
            for b in range(B):
                normal(cn[:, b, :], ctx[:, :, :], cmv, crstd, b).then_inc(cn_ready, 1)
            dve.wait_ge(small_s, 32)
            dve.wait_ge(ctxT_ps, 2)
            raw = b5[:, 0:2 * B * M].rearrange("p (k b m) -> p k b m", k=2, b=B)
            dve.tensor_scalar(ckT[:, :, :], raw[:, 0], vec("lnkw"), vec("lnkb"), ALU.mult, ALU.add
                              ).then_inc(ctxT_ready, 1)
            dve.tensor_scalar(cvT[:, :, :], raw[:, 0], vec("lnvw"), vec("lnvb"), ALU.mult, ALU.add
                              ).then_inc(ctxT_ready, 1)
            dve.tensor_copy(cT[:, :, :], raw[:, 1]).then_inc(ctxT_ready, 1)
            dve.wait_ge(k_ps, 1)
            dve.tensor_scalar(kT[:, :, :], psX[:, 0:B * M].rearrange("p (b m) -> p b m", b=B),
                              vec("bk"), None, ALU.add).then_inc(kT_ready, 1)
            dve.wait_ge(v_ps, 1)
            dve.tensor_copy(v[:, :, :], psO[0:M, 0:B * D].rearrange("p (b d) -> p b d", b=B)
                            ).then_inc(v_ready, 1)
            dve.wait_ge(kT_ready, 1)
            dve.tensor_tensor(kblk[:, 0, :, :], kT[:, 0:1, :].broadcast_to([P, H, M]),
                              cst("headmask").unsqueeze(2).broadcast_to([P, H, M]), ALU.mult
                              ).then_inc(kblk_ready[0], 1)
            queries(0, b2)

            def values(b):
                mask = cst("blockmask").rearrange("p (j h) -> p j h", j=J).unsqueeze(3).broadcast_to([P, J, HH, DH])
                vv = psT[:, 0:J * D].rearrange("p (j s h c) -> p s j h c", j=J, s=2, h=HH)
                dve.wait_ge(vv_ps, b + 1)
                if b == 0:
                    dve.wait_ge(ones_column, 2 * B)
                for half in range(2):
                    last = dve.tensor_tensor(vblk[:, b, half, :, :, 0:DH], vv[:, half], mask, ALU.mult)
                last.then_inc(vblk_ready, 1)

            def scores(g):
                s = psS[g % 2][:, 0:W].rearrange("p (h m) -> p h m", h=HH)
                dve.wait_ge(s_ps, g + 1)
                link(dve.tensor_reduce(smax[:, g % 2, :], s, AX.X, ALU.max))
                if g == 0:
                    dve.wait_ge(prob_zero, 1)
                if g >= 3:
                    dve.wait_ge(pT_ps, g - 2)
                dve.tensor_tensor(prob[:, g % 3, 0:W].rearrange("p (h m) -> p h m", h=HH), s,
                                  smax[:, g % 2, :].unsqueeze(2).broadcast_to([P, HH, M]), ALU.subtract
                                  ).then_inc(sub_ready, 1)

            def heads(c):
                o = psO[:, 0:H * OW].rearrange("p (h w) -> p h w", h=H)
                dve.wait_ge(o_ps, 2 * c + 2)
                link(dve.reciprocal(rsum[:, :], o[:, :, DH]))
                if c >= 2:
                    dve.wait_ge(onT_ps, c - 1)
                dve.tensor_tensor(on[:, c % 2, :].rearrange("p (h w) -> p h w", h=H), o[:, :, 0:DH],
                                  rsum[:, :].unsqueeze(2).broadcast_to([P, H, DH]), ALU.mult
                                  ).then_inc(on_ready, 1)

            def residual(c):
                dve.wait_ge(out_ps, c + 1)
                if c % CB == 0:
                    dve.wait_ge(xbo_ready, c // CB + 1)
                dve.tensor_tensor(x1[:, c, :], mis_out, xbo[:, c, :], ALU.add).then_inc(x1_ready, 1)
                dve.wait_ge(x1_ready, c + 1)
                stats(x1[:, :, :], stat1, mv1, rstd1, range(c, c + 1))

            def rows_for_gate(c):
                dve.wait_ge(rstd_ready, 3 + c + 1)
                normal(xf[:, c, :], x1[:, :, :], mv1, rstd1, c).then_inc(xf_ready, 1)

            for g in range(G + 7):
                if g < G:
                    scores(g)
                if g < B:
                    values(g)
                if g == 0:
                    query_stats(1)
                if g == 1:
                    query_rows(1)
                if g == 3:
                    queries(1, psX[:, :])
                if g >= 8 and g % 2 == 0 and (g - 8) // 2 < C:
                    rows_for_gate((g - 8) // 2)
                if g >= 4 and g % 2 == 0 and (g - 4) // 2 < C:
                    heads((g - 4) // 2)
                if g >= 6 and g % 2 == 0 and (g - 6) // 2 < C:
                    residual((g - 6) // 2)

            def spread(chunked, *shape):
                return chunked.broadcast_to(list(shape))

            def route(l):
                J2 = (2, 1)[l]
                tiles = (T0, T1)[l]
                rev = cst("rev").rearrange("p (c e) -> p c e", e=E)
                dve.wait_ge((logit_ps, logit1_ps)[l], C)
                if l == 0:
                    dve.wait_ge(const2_s, 16)
                    dve.wait_ge(rows_s, 32)
                    dve.wait_ge(counts_ready, 1)
                bias_row = (gateb_row, br_row)[l]
                link(dve.tensor_tensor(lg[:, :, :], logit, bias_row.unsqueeze(1).broadcast_to([P, C, E]), ALU.add))
                link(dve.tensor_reduce(top[:, 0, :], lg[:, :, :], AX.X, ALU.max))
                dve.tensor_tensor(lg2[:, :, :], lg[:, :, :], top[:, 0, :].unsqueeze(2).broadcast_to([P, C, E]),
                                  ALU.subtract).then_inc(l_less[l], 1)
                dve.wait_ge(l_less[l], 1)
                link(dve.scalar_tensor_tensor(out=key[:, :, :], in0=lg2[:, :, :], scalar=0.0, in1=rev,
                                              op0=ALU.is_ge, op1=ALU.mult))
                link(dve.tensor_reduce(kmax[:, 0, :], key[:, :, :], AX.X, ALU.max))
                first = dve.tensor_tensor(pick[:, 0, :, :], rev, kmax[:, 0, :].unsqueeze(2).broadcast_to([P, C, E]),
                                          ALU.is_equal)
                if l == 1:
                    first.then_inc(pick_ready[l], 1)
                    dve.wait_ge(pick_ready[l], 1)
                else:
                    link(first)
                    link(dve.scalar_tensor_tensor(out=lg[:, :, :], in0=pick[:, 0, :, :], scalar=NEG,
                                                  in1=lg2[:, :, :], op0=ALU.mult, op1=ALU.add))
                    dve.tensor_reduce(top[:, 1, :], lg[:, :, :], AX.X, ALU.max).then_inc(l_less[l], 1)
                    dve.wait_ge(l_less[l], 2)
                    link(dve.tensor_tensor(key[:, :, :], lg[:, :, :],
                                           top[:, 1, :].unsqueeze(2).broadcast_to([P, C, E]), ALU.is_ge))
                    link(dve.tensor_tensor(key[:, :, :], key[:, :, :], rev, ALU.mult))
                    link(dve.tensor_reduce(kmax[:, 1, :], key[:, :, :], AX.X, ALU.max))
                    link(dve.tensor_tensor(pick[:, 1, :, :], rev,
                                           kmax[:, 1, :].unsqueeze(2).broadcast_to([P, C, E]), ALU.is_equal))
                    dve.tensor_tensor(both[:, :, :], pick[:, 0, :, :], pick[:, 1, :, :], ALU.add
                                      ).then_inc(pick_ready[l], 1)
                dve.wait_ge(rank_ps[l], 1)
                rank = b0[:, 0:C * E].rearrange("p (c e) -> p c e", e=E)
                count = b1[:, 0:E]
                link(dve.tensor_tensor(over[:, :, :], count.unsqueeze(2).broadcast_to([P, E, E]),
                                       cst("kstep").rearrange("p (e k) -> p e k", k=E), ALU.is_gt))
                link(dve.tensor_reduce(ntl[:, :], over[:, :, :], AX.X, ALU.add))
                link(dve.tensor_tensor(over[:, :, :], ntl[:, :].unsqueeze(1).broadcast_to([P, E, E]),
                                       cst("earlier").rearrange("p (e k) -> p e k", k=E), ALU.mult))
                link(dve.tensor_reduce(base[:, :], over[:, :, :], AX.X, ALU.add))
                link(dve.scalar_tensor_tensor(out=place[:, :, :], in0=base[:, :].unsqueeze(1).broadcast_to([P, C, E]),
                                              scalar=float(P), in1=rank, op0=ALU.mult, op1=ALU.add))
                link(dve.tensor_tensor(slots[:, 0:J2, :, :], pick[:, 0:J2, :, :],
                                       place[:, :, :].unsqueeze(1).broadcast_to([P, J2, C, E]), ALU.mult))
                q = J2 * C
                with nc.allow_low_precision(reason="slot numbers are integers below 4096"):
                    link(dve.tensor_reduce(slot[:, 0:q], slots[:, 0:J2, :, :].rearrange("p j c e -> p (j c) e"),
                                           AX.X, ALU.add))
                link(dve.tensor_scalar(lane[:, 0:q], slot[:, 0:q], P - 1, None, ALU.bitwise_and))
                dve.tensor_copy(lanef[:, 0:q], lane[:, 0:q])
                link(dve.tensor_tensor(tilef[:, 0:q], slot[:, 0:q], lane[:, 0:q], ALU.subtract))
                link(dve.tensor_tensor(intile[:, 0:q, 0:tiles], cst("tstep")[:, 0:tiles].unsqueeze(1).broadcast_to([P, q, tiles]),
                                       tilef[:, 0:q].unsqueeze(2).broadcast_to([P, q, tiles]), ALU.is_equal))
                for i in range(q):
                    dve.tensor_scalar(onehot[:, i, :], counts[:, 2 * P:3 * P], lanef[:, i:i + 1], None, ALU.is_equal)
                dve.tensor_tensor(tabv[:, 0:q, 0:2, 0:tiles],
                                  intile[:, 0:q, 0:tiles].unsqueeze(2).broadcast_to([P, q, 2, tiles]),
                                  cst("tokval").rearrange("p (q k) -> p q k", k=2)[:, 0:q, :].unsqueeze(3)
                                  .broadcast_to([P, q, 2, tiles]), ALU.mult)
                dve.tensor_scalar(tabv[:, 0:q, 2, 0:tiles], intile[:, 0:q, 0:tiles], cst("lane"), None, ALU.mult
                                  ).then_inc(spread_ready[l], 1)
                link(dve.tensor_tensor(ends[:, :], base[:, :], ntl[:, :], ALU.add))
                link(dve.tensor_tensor(etile[:, 0:tiles, :], ends[:, :].unsqueeze(1).broadcast_to([P, tiles, E]),
                                       cst("tilecol").rearrange("p (t e) -> p t e", e=E)[:, 0:tiles], ALU.is_le))
                link(dve.tensor_reduce(esum[:, 0:tiles], etile[:, 0:tiles, :], AX.X, ALU.add))
                dve.tensor_scalar(expert[l][:, :], esum[:, 0:tiles], float(E - 1), None, ALU.min
                                  ).then_inc(experts_ready[l], 1)
                dve.wait_ge(table_ps[l], 1)
                table = b5[:, 0:3 * tiles].rearrange("p (k t) -> p k t", k=3)
                dve.tensor_scalar(padrow[:, 0:tiles], table[:, 1], 0.0, float(4 * N), ALU.is_equal, ALU.mult)
                link(dve.tensor_copy(slottok[:, 0:tiles], table[:, 0]))
                link(dve.tensor_tensor(slottok[:, 0:tiles], slottok[:, 0:tiles], table[:, 2], ALU.add))
                dve.tensor_copy(token[l][:, :], slottok[:, 0:tiles]).then_inc(token_ready[l], 1)
                if l == 0:
                    link(dve.scalar_tensor_tensor(out=slottok[:, 0:tiles], in0=slottok[:, 0:tiles], scalar=2.0,
                                                  in1=table[:, 1], op0=ALU.mult, op1=ALU.add))
                dve.scalar_tensor_tensor(out=dest[l][:, :], in0=slottok[:, 0:tiles], scalar=(-1.0, 0.0)[l],
                                         in1=padrow[:, 0:tiles], op0=ALU.add, op1=ALU.add
                                         ).then_inc(dest_ready[l], 1)

            def choice_weights():
                dve.wait_ge(ex_ready, 2)
                link(dve.tensor_reduce(wt[:, 0, :], ex[:, :, :], AX.X, ALU.add))
                link(dve.reciprocal(wt[:, 1, :], wt[:, 0, :]))
                link(dve.tensor_tensor(wt[:, 2, :], ex2[:, :], wt[:, 1, :], ALU.mult))
                link(dve.scalar_tensor_tensor(out=wt[:, 3, :], in0=wt[:, 1, :], scalar=1e-20, in1=wt[:, 2, :],
                                              op0=ALU.add, op1=ALU.add))
                link(dve.reciprocal(wt[:, 4, :], wt[:, 3, :]))
                for j in range(2):
                    last = dve.tensor_tensor(weight[:, j, :], wt[:, 1 + j, :], wt[:, 4, :], ALU.mult)
                link(last)

            route(0)
            choice_weights()

            def mix(l):
                tiles = (T0, T1)[l]
                rows_ = (FB0, P)[l]

                def step(n):
                    if l == 0 and (n < tiles):
                        dve.wait_ge(up_ps[0], n + 1)
                        dve.wait_ge(z_up, n + 1)
                        dve.tensor_tensor(z[n % 2][:, :], (b1, b3)[n % 2][:, 0:F0], z[n % 2][:, :], ALU.mult
                                          ).then_inc(z_ready, 1)
                    if 1 <= n <= tiles:
                        dve.wait_ge(hT_ps[l], n)
                        wait_past(dve, y_ps[l], n - 2)
                        dve.tensor_copy(hT[(n - 1) % 2][0:rows_, :], b4[0:rows_, :]).then_inc(hT_ready[l], 1)
                    if 2 <= n <= tiles + 1:
                        dve.wait_ge(y_ps[l], n - 1)
                        wait_past(dve, scattered[l][(n - 2) % 4], (n - 2) // 4 * 16)
                        source = psO[:, 0:D]
                        if l == 0:
                            dve.tensor_copy(y[(n - 2) % 4][:, :], source).then_inc(y_ready[l], 1)
                        else:
                            dve.wait_ge(kept, n - 1)
                            dve.tensor_tensor(y[(n - 2) % 4][:, :], source, keep[(n - 2) % 4][:, :], ALU.add
                                              ).then_inc(y_ready[l], 1)

                for n in range(tiles + 2):
                    step(n)

            mix(0)

            groups = [range(CB * b, CB * (b + 1)) for b in range(B)]
            spans = [slice(g[0], g[-1] + 1) for g in groups]
            for b, (cs, sp_) in enumerate(zip(groups, spans)):
                dve.wait_ge(back_s[b], 16)
                for j, before in enumerate((x1, x2)):
                    for c in cs:
                        last = dve.scalar_tensor_tensor(out=x2[:, c, :], in0=ybk[:, c, j, :],
                                                        scalar=weight[:, j, c:c + 1], in1=before[:, c, :],
                                                        op0=ALU.mult, op1=ALU.add)
                    link(last)
                stats(x2[:, :, :], stat2, mv2, rstd2, cs)
            for b, sp_ in enumerate(spans):
                s2 = (b2, b3)[b][:, 0:CB * M].rearrange("p (c m) -> p c m", m=M)
                dve.wait_ge(s2_ps, b + 1)
                link(dve.tensor_reduce(smax2[:, sp_], s2, AX.X, ALU.max))
                dve.tensor_tensor(prob2[:, sp_, :], s2, smax2[:, sp_].unsqueeze(2).broadcast_to([P, CB, M]),
                                  ALU.subtract).then_inc(sub2_ready, 1)
            for b, sp_ in enumerate(spans):
                dve.wait_ge(exp2_ready, b + 1)
                link(dve.tensor_reduce(ssum2[:, sp_], prob2[:, sp_, :], AX.X, ALU.add))
                link(dve.reciprocal(rsum2[:, sp_], ssum2[:, sp_]))
            for b, (cs, sp_) in enumerate(zip(groups, spans)):
                dve.wait_ge(o2_ps, b + 1)
                dve.tensor_tensor(o2[:, sp_, :], psO[:, :].rearrange("p (c d) -> p c d", c=CB),
                                  rsum2[:, sp_].unsqueeze(2).broadcast_to([P, CB, D]), ALU.mult
                                  ).then_inc(x3_ready, 1)
                dve.wait_ge(x3_ready, b + 1)
                link(dve.tensor_tensor(row1[:, sp_, 1, :], o2[:, sp_, :], x2[:, sp_, :], ALU.add))
                stats(row1[:, :, 1, :], stat3, mv3, rstd3, cs)

            route(1)
            mix(1)

        @block.scalar
        def _(act):
            def gate_rows(c):
                act.wait_ge(xfT_ps, c + 1)
                if c >= 2:
                    act.wait_ge(logit_ps, c - 1)
                act.copy(xfT[:, c % 2, :], mis_xT).then_inc(xfT_ready, 1)

            def query_rows(b, source):
                act.wait_ge(xT_ps, b + 1)
                act.activation(xnT[:, 512 * b:512 * (b + 1)], source, ACT.Identity, bias=vec("lnqb"),
                               scale=vec("lnqw")).then_inc(xnT_ready, 1)

            def take_table(func):
                act.activation(idle[:, :], neghalf[:, 0:1], func).then_inc(table_taken, 1)

            act.wait_ge(pool_step, 1)
            take_table(ACT.Exp)
            act.wait_ge(small_s, 32)
            query_rows(0, b0)

            for g in range(G + 8):
                if g < G:
                    act.wait_ge(sub_ready, g + 1)
                    act.activation(prob[:, g % 3, 0:W], prob[:, g % 3, 0:W], ACT.Exp).then_inc(exp_ready, 1)
                if g == 2:
                    query_rows(1, psX[:, :])
                if 2 <= g < G + 2:
                    act.wait_ge(pT_ps, g - 1)
                    if g >= 4:
                        act.wait_ge(o_ps, g - 3)
                    act.copy(probT[:, g % 2, :], psT[:, 0:WP]).then_inc(pT_ready, 1)
                if g >= 5 and g % 2 == 1 and (g - 5) // 2 < C:
                    c = (g - 5) // 2
                    act.wait_ge(onT_ps, c + 1)
                    if c >= 2:
                        act.wait_ge(xfT_ps, c - 1)
                    if c >= 2:
                        act.wait_ge(out_ps, c - 1)
                    act.activation(onT[:, c % 2, :], mis_onT, ACT.Identity, bias=vec("bv")).then_inc(onT_ready, 1)
                if g >= 9 and g % 2 == 1 and (g - 9) // 2 < C:
                    gate_rows((g - 9) // 2)
            act.wait_ge(l_less[0], 1)
            act.activation(ex[:, :, :], lg2[:, :, :], ACT.Exp).then_inc(ex_ready, 1)
            act.wait_ge(l_less[0], 2)
            act.activation(ex2[:, :], top[:, 1, :], ACT.Exp).then_inc(ex_ready, 1)
            act.wait_ge(table_taken, 1)
            take_table(ACT.Silu)

            def mix(l):
                tiles = (T0, T1)[l]

                def take(n):
                    act.wait_ge(xsT_ps[l], n + 1)
                    wait_past(act, up_ps[l], n - 1)
                    act.copy(xsT[n % 2][:, :], psX[:, 0:P]).then_inc(xsT_ready[l], 1)
                    if l == 1:
                        wait_past(act, y_ready[1], n - 3)
                        act.copy(keep[n % 4][:, :], xs[n % RING][:, D:2 * D]).then_inc(kept, 1)

                def step(n):
                    if n + 1 < tiles:
                        take(n + 1)
                    if n < tiles:
                        wait_past(act, hT_ps[l], n - 1)
                        if l == 0:
                            act.wait_ge(up_half, n + 1)
                            act.copy(z[n % 2][:, :], (b0, b2)[n % 2][:, 0:F0]).then_inc(z_up, 1)
                            act.wait_ge(z_ready, n + 1)
                            act.activation(h[n % 2][:, 0:F0], z[n % 2][:, :], ACT.Silu).then_inc(h_ready[0], 1)
                        else:
                            act.wait_ge(up_ps[1], n + 1)
                            act.activation(h[n % 2][:, :], (b0, b1)[n % 2], ACT.Gelu).then_inc(h_ready[1], 1)

                take(0)
                for n in range(tiles + 2):
                    step(n)

            mix(0)
            act.wait_ge(table_taken, 2)
            take_table(ACT.Exp)

            for b in range(B):
                act.wait_ge(x2T_ps, b + 1)
                act.copy(x2T[:, CB * b:CB * (b + 1), :].rearrange("p c t -> p (c t)"), (b0, b1)[b]
                         ).then_inc(x2T_ready, 1)
            for b in range(B):
                act.wait_ge(sub2_ready, b + 1)
                p2 = prob2[:, CB * b:CB * (b + 1), :].rearrange("p c m -> p (c m)")
                act.activation(p2, p2, ACT.Exp, scale=float(D) ** -0.5).then_inc(exp2_ready, 1)
            for b in range(B):
                act.wait_ge(p2T_ps, b + 1)
                act.copy(prob2T[:, CB * b:CB * (b + 1), :].rearrange("m c t -> m (c t)"), (b4, b5)[b][0:M, :]
                         ).then_inc(p2T_ready, 1)
            act.wait_ge(table_taken, 3)
            take_table(ACT.Gelu)
            for b in range(B):
                act.wait_ge(x3T_ps, b + 1)
                act.copy(x3T[:, CB * b:CB * (b + 1), :].rearrange("p c t -> p (c t)"), (b0, b1)[b]
                         ).then_inc(x3T_ready, 1)

            mix(1)

        @block.tensor
        def _(pe):
            def query_rows(b, target):
                pe.wait_ge(xn_ready, CB * (b + 1))
                for c in range(CB):
                    last = pe.transpose(target[:, P * c:P * (c + 1)], xn[:, CB * b + c, :], ident)
                last.then_inc(xT_ps, 1)

            def queries(b, target):
                pe.wait_ge(xnT_ready, b + 1)
                pe.matmul(target, wq, xnT[:, 512 * b:512 * (b + 1)], start=True, stop=True).then_inc(q_ps, 1)

            pe.wait_ge(const_s, 16)
            query_rows(0, b0)
            pe.wait_ge(cn_ready, B)
            for source, k in ((cn, 0), (ctx, 1)):
                for b in range(B):
                    i = k * B + b
                    last = pe.transpose(b5[:, i * M:(i + 1) * M], source[:, b, :], ident[0:M, 0:M])
                last.then_inc(ctxT_ps, 1)
            pe.wait_ge(small_s, 32)
            queries(0, b2)
            pe.wait_ge(ctxT_ready, 3)
            pe.matmul(psX[:, 0:B * M], wk, ckT[:, :, :].rearrange("p b m -> p (b m)"), start=True, stop=True
                      ).then_inc(k_ps, 1)
            for b in range(B):
                last = pe.matmul(psO[0:M, b * D:(b + 1) * D], cvT[:, b, :], wv, start=True, stop=True)
            last.then_inc(v_ps, 1)

            def values(b):
                pe.wait_ge(v_ready, 1)
                if b:
                    pe.wait_ge(vblk_ready, b)
                for j in range(J):
                    last = pe.matmul(psT[:, P * j:P * (j + 1)], cst("sel", M)[:, P * j:P * (j + 1)], v[:, b, :],
                                     start=True, stop=True)
                last.then_inc(vv_ps, 1)

            def scores(g):
                c, s = g // 2, g % 2
                b = c // CB
                if g in (0, G // 2):
                    pe.wait_ge(q_ready, b + 1)
                    pe.wait_ge(kblk_ready[b], 1)
                if g >= 2:
                    pe.wait_ge(sub_ready, g - 1)
                keys = kblk[:, b, HH * s:HH * (s + 1), :].rearrange("p h m -> p (h m)")
                pe.matmul(psS[g % 2][:, 0:512], qT[:, P * c:P * (c + 1)], keys[:, 0:512], start=True, stop=True)
                pe.matmul(psS[g % 2][:, 512:W], qT[:, P * c:P * (c + 1)], keys[:, 512:W], start=True, stop=True
                          ).then_inc(s_ps, 1)

            def turn(g):
                pe.wait_ge(exp_ready, g + 1)
                if g >= 1:
                    pe.wait_ge(pT_ready, g)
                else:
                    pe.wait_ge(vblk_ready, B)
                for j in range(J):
                    last = pe.transpose(psT[:, P * j:P * (j + 1)], prob[:, g % 3, P * j:P * (j + 1)], ident)
                last.then_inc(pT_ps, 1)

            def attend(g):
                c, s = g // 2, g % 2
                pe.wait_ge(pT_ready, g + 1)
                if s == 0 and c >= 1:
                    pe.wait_ge(on_ready, c)
                for j in range(J):
                    ha, hb = P * j // M, min((P * (j + 1) - 1) // M, HH - 1) + 1
                    a = OW * (HH * s + ha)
                    last = pe.matmul(psO[:, a:a + OW * (hb - ha)], probT[:, g % 2, P * j:P * (j + 1)],
                                     vblk[:, c // CB, s, j, ha:hb, :].rearrange("p h w -> p (h w)"),
                                     start=(j == 0), stop=(j == J - 1), skip_group_check=True)
                last.then_inc(o_ps, 1)

            for g in range(G + 9):
                if g < G:
                    scores(g)
                if g < B:
                    values(g)
                if g == 2:
                    query_rows(1, psX[:, :])
                if 2 <= g < G + 2:
                    turn(g - 2)
                if 3 <= g < G + 3:
                    attend(g - 3)
                if g == 3:
                    queries(1, psX[:, :])
                c = (g - 5) // 2
                if g >= 5 and g % 2 == 1 and c < C:
                    pe.wait_ge(on_ready, c + 1)
                    pe.wait_ge(q_ready, B)
                    if c >= 1:
                        pe.wait_ge(x1_ready, c)
                    pe.transpose(mis_onT, on[:, c % 2, :], ident).then_inc(onT_ps, 1)
                c = (g - 9) // 2
                if g >= 9 and g % 2 == 1 and c < C:
                    pe.wait_ge(xf_ready, c + 1)
                    pe.wait_ge(x1_ready, min(c + 2, C))
                    pe.transpose(mis_xT, xf[:, c, :], ident).then_inc(xfT_ps, 1)
                c = (g - 10) // 2
                if g >= 10 and g % 2 == 0 and c < C:
                    pe.wait_ge(xfT_ready, c + 1)
                    if c + 2 < C:
                        pe.wait_ge(onT_ready, c + 3)
                    pe.matmul(logit[:, c, :], xfT[:, c % 2, :], gate[:, 0, :], start=True, stop=True
                              ).then_inc(logit_ps, 1)
                c = (g - 6) // 2
                if g >= 6 and g % 2 == 0 and c < C:
                    pe.wait_ge(onT_ready, c + 1)
                    pe.matmul(mis_out, onT[:, c % 2, :], wo, start=True, stop=True).then_inc(out_ps, 1)

            def route(l):
                chosen = both[:, :, :] if l == 0 else pick[:, 0, :, :]
                before, ones = counts[:, 0:P], counts[:, P:2 * P]
                pe.wait_ge(counts_ready, 1)
                pe.wait_ge(pick_ready[l], 1)
                pe.matmul(b0[:, 0:C * E], before, chosen.rearrange("p c e -> p (c e)"), start=True, stop=False,
                          skip_group_check=True)
                for s in range(1, C):
                    pe.matmul(b0[:, s * E:C * E], ones, chosen[:, 0:C - s, :].rearrange("p c e -> p (c e)"),
                              start=False, stop=(s == C - 1), skip_group_check=True)
                for c in range(C):
                    last = pe.matmul(b1[:, 0:E], ones, chosen[:, c, :], start=(c == 0), stop=(c == C - 1))
                last.then_inc(rank_ps[l], 1)
                pe.wait_ge(spread_ready[l], 1)
                q, tiles = ((2 * C, T0), (C, T1))[l]
                for i in range(q):
                    last = pe.matmul(b5[:, 0:3 * tiles].rearrange("p (k t) -> p k t", k=3), onehot[:, i, :],
                                     tabv[:, i, :, 0:tiles], start=(i == 0), stop=(i == q - 1))
                last.then_inc(table_ps[l], 1)
                pe.wait_ge(experts_ready[l], 1)

            def mix(l):
                tiles = (T0, T1)[l]

                its = {}

                def choose(n):
                    its[n] = pe.value_load(expert[l][0:1, n:n + 1], min_val=0, max_val=E - 1)

                def take(n):
                    pe.wait_ge(gathered[l][n % RING], (n // RING + 1) * 16)
                    wait_past(pe, xsT_ready[l], n)
                    pe.transpose(psX[:, 0:P], xs[n % RING][:, 0:D], ident
                                 ).then_inc(xsT_ps[l], 1)

                def up(n):
                    e = its[n]
                    pe.wait_ge(xsT_ready[l], n + 1)
                    wait_past(pe, (z_ready, h_ready[1])[l], n - 1)
                    if l == 0:
                        for k, target in enumerate(((b0, b1), (b2, b3))[n % 2]):
                            pe.matmul(target[:, 0:F0], xsT[n % 2][:, :], wgu[:, bass.ds(e * (2 * F0) + (1 - k) * F0, F0)],
                                      start=True, stop=False)
                            last = pe.matmul(target[:, 0:F0], ones3[:, :], bias3[:, bass.ds(e * BI0 + (1 - k) * F0, F0)],
                                             start=False, stop=True)
                            if k == 0:
                                last.then_inc(up_half, 1)
                    else:
                        target = (b0, b1)[n % 2]
                        pe.matmul(target, xsT[n % 2][:, :], w1[:, bass.ds(e * F1, F1)], start=True, stop=False)
                        last = pe.matmul(target, ones3[:, :], bias3[:, bass.ds(e * BI1 + E * BI0, F1)],
                                         start=False, stop=True)
                    last.then_inc(up_ps[l], 1)

                def turn(n):
                    pe.wait_ge(h_ready[l], n + 1)
                    wait_past(pe, hT_ready[l], n)
                    f = (FB0, P)[l]
                    for k in range(K0):
                        last = pe.transpose(b4[0:f, P * k:P * (k + 1)], h[n % 2][:, f * k:f * (k + 1)], ident)
                    last.then_inc(hT_ps[l], 1)

                def down(n):
                    e = its.pop(n)
                    pe.wait_ge(hT_ready[l], n + 1)
                    wait_past(pe, y_ready[l], n)
                    f = (FB0, P)[l]
                    target = psO[:, 0:D]
                    w, stride, b_at = ((dw, K0 * D, e * BI0 + 2 * F0), (w2, K1 * D, e * BI1 + (E * BI0 + F1)))[l]
                    for k in range(K0):
                        pe.matmul(target, hT[n % 2][0:f, P * k:P * (k + 1)], w[:, bass.ds(e * stride + k * D, D)],
                                  start=(k == 0), stop=False)
                    pe.matmul(target, ones3[:, :], bias3[:, bass.ds(b_at, D)], start=False, stop=True
                              ).then_inc(y_ps[l], 1)

                def step(n):
                    if n + 1 < tiles:
                        take(n + 1)
                    if n < tiles:
                        up(n)
                    if 1 <= n <= tiles:
                        turn(n - 1)
                    if n + 1 < tiles:
                        choose(n + 1)
                    if 2 <= n <= tiles + 1:
                        down(n - 2)

                pe.wait_ge((f0_w, f1_w)[l], (48, 32)[l])
                choose(0)
                take(0)
                for n in range(tiles + 2):
                    step(n)

            route(0)
            pe.wait_ge(bias3_s, 16)
            pe.wait_ge(pool_step, 4)
            mix(0)

            for b in range(B):
                pe.wait_ge(x2n_ready, b + 1)
                for c in range(CB):
                    last = pe.transpose((b0, b1)[b][:, P * c:P * (c + 1)], x2n[:, CB * b + c, :], ident)
                last.then_inc(x2T_ps, 1)
                pe.wait_ge(x2T_ready, b + 1)
                for c in range(CB):
                    last = pe.matmul((b2, b3)[b][:, M * c:M * (c + 1)], x2T[:, CB * b + c, :], cT[:, b, :],
                                     start=True, stop=True)
                last.then_inc(s2_ps, 1)
            for b in range(B):
                pe.wait_ge(exp2_ready, b + 1)
                for c in range(CB):
                    last = pe.transpose((b4, b5)[b][0:M, P * c:P * (c + 1)], prob2[:, CB * b + c, :], ident)
                last.then_inc(p2T_ps, 1)
            for b in range(B):
                pe.wait_ge(p2T_ready, b + 1)
                if b:
                    pe.wait_ge(x3_ready, b)
                for c in range(CB):
                    last = pe.matmul(psO[:, D * c:D * (c + 1)], prob2T[:, CB * b + c, :], ctx[:, b, :],
                                     start=True, stop=True)
                last.then_inc(o2_ps, 1)
            for b in range(B):
                pe.wait_ge(row1_ready, b + 1)
                for c in range(CB):
                    last = pe.transpose((b0, b1)[b][:, P * c:P * (c + 1)], row1[:, CB * b + c, 0, :], ident)
                last.then_inc(x3T_ps, 1)
                pe.wait_ge(x3T_ready, b + 1)
                for c in range(CB * b, CB * (b + 1)):
                    pe.matmul(logit[:, c, :], x3T[:, c, :], gate[:, 1, :], start=True, stop=True
                              ).then_inc(logit1_ps, 1)
            route(1)
            mix(1)


def constant_table():
    import numpy as np

    p = np.arange(P)[:, None]
    parts = {}
    parts["ident"] = np.eye(P)
    parts["headmask"] = p // DH == np.arange(H)[None, :]
    j, hh = np.arange(J)[:, None], np.arange(HH)[None, :]
    flat = P * j[None] + p[:, :, None]
    parts["blockmask"] = flat // M == hh[None]
    sel = np.zeros((P, WP))
    sel[np.arange(W) % M, np.arange(W)] = 1
    parts["sel"] = sel
    parts["before"] = p < np.arange(P)[None, :]
    parts["ones"] = np.ones((P, P))
    e = np.arange(E)
    one = np.ones((P, 1))
    parts["rev"] = one * np.tile(E - e, C)[None]
    parts["kstep"] = one * np.tile(P * e, E)[None]
    parts["earlier"] = one * (e[None, :] < e[:, None]).reshape(1, -1)
    parts["iota"] = one * np.arange(P)[None]
    parts["tstep"] = one * (P * np.arange(T0))[None]
    parts["tilecol"] = one * np.repeat(np.arange(T0), E)[None]
    q = np.arange(2 * C)[None, :]
    parts["tokval"] = one[:, :, None] * np.stack([P * (q % C), q // C + 1], 2)
    parts["lane"] = p
    return np.concatenate([parts[name].reshape(P, n) for name, n in CONST_PARTS], 1).astype(np.float32)


def kernel(**inputs):
    import numpy as np
    import concourse.bacc as bacc
    from concourse.bass_utils import run_bass_kernel_spmd

    a = {k: np.asarray(val) for k, val in inputs.items()}
    f0, f1, x0 = "L0_ffn_", "L1_ffn_", "L0_xattn_"
    arrays = {
        "x": a["x"],
        "ctx": a["ctx_1024"],
        "wqkvo": np.stack([a[x0 + w] for w in ("Wq", "Wk", "Wv", "Wo")], 1),
        "vecs": np.stack([a[x0 + w] for w in ("ln_q_w", "ln_q_b", "ln_k_w", "ln_k_b", "ln_v_w", "ln_v_b",
                                              "bq", "bk", "bv")], 1),
        "rows": np.concatenate([a[x0 + "bo"], a[f0 + "gate_b"], a[f1 + "br"]]),
        "consts": constant_table(),
        "gate": np.stack([a[f0 + "gate_w"].T, a[f1 + "wr"]], 1),
        "wgu": np.stack([a[f0 + "gp_w"], a[f0 + "up_w"]], 1).transpose(3, 0, 1, 2).reshape(P, -1),
        "dw": a[f0 + "down_w"].reshape(E, D, K0, FB0).transpose(3, 0, 2, 1).reshape(FB0, -1),
        "w1": a[f1 + "w1"].transpose(1, 0, 2).reshape(P, -1),
        "w2": a[f1 + "w2"].reshape(E, K1, P, D).transpose(2, 0, 1, 3).reshape(P, -1),
        "bias": np.concatenate([np.concatenate([a[f0 + "gp_b"], a[f0 + "up_b"], a[f0 + "down_b"]], 1).ravel(),
                                np.concatenate([a[f1 + "b1"], a[f1 + "b2"]], 1).ravel()]).reshape(P, BC),
    }
    arrays = {f"in_{k}": np.ascontiguousarray(val) for k, val in arrays.items()}
    nc = bacc.Bacc("TRN2", target_bir_lowering=False, num_devices=1)
    aps = [nc.dram_tensor(k, val.shape, mybir.dt.from_np(val.dtype), kind="ExternalInput").ap()
           for k, val in arrays.items()]
    out = nc.dram_tensor("out", (N, D), F32, kind="ExternalOutput").ap()
    two_blocks(nc, *aps, out)
    r = run_bass_kernel_spmd(nc, [arrays], core_ids=[0])
    return r.results[0]["out"].reshape(B, N // B, D)
```

```python
from contextlib import ExitStack

import concourse.bass as bass
from concourse import mybir

F32 = mybir.dt.float32
BF16 = mybir.dt.bfloat16
I32 = mybir.dt.int32
U32 = mybir.dt.uint32
ALU = mybir.AluOpType
ACT = mybir.ActivationFunctionType
AX = mybir.AxisListType

P = 128
D = 128
B = 2
C = 8
CB = C // B
N = C * P
M = 77
H = 16
DH = D // H
HH = H // 2
W = HH * M
J = -(-W // P)
WP = J * P
OW = DH + 1
G = C * 2
E = 8
F0 = 408
K0 = 4
FB0 = F0 // K0
F1 = 512
K1 = 4
T0 = 2 * N // P + E - 1
T1 = N // P + E - 1
ALWAYS = (20, 12)
BI0 = 2 * F0 + D
BI1 = F1 + D
BIAS = E * (BI0 + BI1)
BC = BIAS // P
EPS = 1e-5
NEG = -3.0e38

CONST_PARTS = [("ident", P), ("headmask", H), ("blockmask", J * HH), ("sel", WP), ("before", P),
               ("ones", P), ("iota", P), ("rev", C * E), ("kstep", E * E), ("earlier", E * E),
               ("tstep", T0), ("tilecol", T0 * E), ("tokval", 2 * C * 3)]
FIRST_CONSTS = 4
RING = 6
WARM_START = 14
WARM_KEYS = 2
WARM_VALUES = 2
WARM_TAIL = (2, 1)
WARM_RANK = (16, 12)
WARM_TABLE = 12
WARM_BETWEEN = 70
WARM_STEP = 3
WARM_NORM = 16
WARM_TURN = 4
assert all(a + RING >= t for a, t in zip(ALWAYS, (T0, T1)))
CONST_AT = {}
_at = 0
for _name, _n in CONST_PARTS:
    CONST_AT[_name] = (_at, _at + _n)
    _at += _n
CONSTS = _at
CONST_SPLIT = CONST_AT[CONST_PARTS[FIRST_CONSTS][0]][0]
VECS = ["lnqw", "lnqb", "lnkw", "lnkb", "lnvw", "lnvb", "bq", "bk", "bv"]
ROWS = D + 2 * E


def two_blocks(nc, x_in, ctx_in, wqkvo_in, vecs_in, rows_in, consts_in, gate_in, wgu_in,
               dw_in, w1_in, w2_in, bias_in, out):
    stack = ExitStack()
    with stack:
        def sb(name, shape, dt=F32):
            return stack.enter_context(nc.sbuf_tensor(name, shape, dt))

        def bank(name, columns=512):
            return stack.enter_context(nc.psum_tensor(name, [P, columns], F32))

        def sem(name):
            return stack.enter_context(nc.semaphore(name))

        rows0 = nc.dram_tensor("rows0", (N, D), F32).ap()
        back0 = nc.dram_tensor("back0", (2 * N, D), F32).ap()
        rows1 = nc.dram_tensor("rows1", (N, 2 * D), F32).ap()
        parts = nc.dram_tensor("parts", (3, BIAS), BF16).ap()

        x = sb("x", [P, C, D])
        ctx = sb("ctx", [M, B, D])
        wqkvo = sb("wqkvo", [P, 4, D])
        vecs = sb("vecs", [P, len(VECS)])
        rows = sb("rows", [P, ROWS])
        consts = sb("consts", [P, CONSTS])
        gate = sb("gate", [P, 2, E])
        wgu = sb("wgu", [P, E * 2 * F0])
        dw = sb("dw", [FB0, E * K0 * D])
        w1 = sb("w1", [P, E * F1])
        w2 = sb("w2", [P, E * K1 * D])
        bias = sb("bias", [P, BC])
        part = sb("part", [P, 3, BC], BF16)
        rest = sb("rest", [P, 2, BC])
        bias3 = sb("bias3", [3, BIAS], BF16)
        ones3 = sb("ones3", [3, P], BF16)

        stat = sb("stat", [P, C, 6])
        mv = sb("mv", [P, C, 2])
        rstd = sb("rstd", [P, C])
        cstat = sb("cstat", [M, B, 6])
        cmv = sb("cmv", [M, B, 2])
        crstd = sb("crstd", [M, B])
        xn = sb("xn", [P, C, D])
        cn = sb("cn", [M, B, D])
        xbo = sb("xbo", [P, C, D])
        xnT = sb("xnT", [P, N])
        cT = sb("cT", [P, B, M])
        ckT = sb("ckT", [P, B, M])
        cvT = sb("cvT", [P, B, M])
        qT = sb("qT", [P, N])
        kT = sb("kT", [P, B, M])
        v = sb("v", [M, B, D])
        kblk = sb("kblk", [P, B, H, M])
        vblk = sb("vblk", [P, B, 2, J, HH, OW])
        smax = sb("smax", [P, 2, HH])
        prob = sb("prob", [P, 3, WP])
        probT = sb("probT", [P, 2, WP])
        rsum = sb("rsum", [P, H])
        on = sb("on", [P, 2, D])
        onT = sb("onT", [P, 2, D])
        x1 = sb("x1", [P, C, D])
        stat1 = sb("stat1", [P, C, 6])
        mv1 = sb("mv1", [P, C, 2])
        rstd1 = sb("rstd1", [P, C])
        neghalf = sb("neghalf", [P, C])
        idle = sb("idle", [P, 1])
        idle_ones = sb("idle_ones", [P, P], BF16)
        xf = sb("xf", [P, C, D])
        xfT = sb("xfT", [P, 2, D])

        lg = sb("lg", [P, C, E])
        lg2 = sb("lg2", [P, C, E])
        key = sb("key", [P, C, E])
        top = sb("top", [P, 2, C])
        kmax = sb("kmax", [P, 2, C])
        pick = sb("pick", [P, 2, C, E], BF16)
        both = sb("both", [P, C, E], BF16)
        ex = sb("ex", [P, C, E])
        ex2 = sb("ex2", [P, C])
        wt = sb("wt", [P, 5, C])
        weight = sb("weight", [P, 2, C])
        ntl = sb("ntl", [P, E])
        over = sb("over", [P, E, E])
        base = sb("base", [P, E])
        ends = sb("ends", [P, E])
        place = sb("place", [P, C, E])
        slots = sb("slots", [P, 2, C, E])
        slot = sb("slot", [P, 2 * C], I32)
        lane = sb("lane", [P, 2 * C], I32)
        lanef = sb("lanef", [P, 2 * C])
        tilef = sb("tilef", [P, 2 * C])
        counts = sb("counts", [P, 3 * P], BF16)
        intile = sb("intile", [P, 2 * C, T0], BF16)
        tabv = prob[:, :, :].rearrange("p i w -> p (i w)")[:, 0:3 * C * T0].bitcast(BF16).rearrange(
            "p (q k t) -> p q k t", q=2 * C, k=3)
        onehot = probT[:, :, :].rearrange("p i w -> p (i w)")[:, 0:C * P].bitcast(BF16).rearrange(
            "p (q s) -> p q s", q=2 * C)
        slottok = sb("slottok", [P, T0])
        etile = sb("etile", [P, T0, E])
        esum = sb("esum", [P, T0])
        padrow = sb("padrow", [P, T0])

        expert = [sb(f"expert{l}", [P, t], I32) for l, t in enumerate((T0, T1))]
        token = [sb(f"token{l}", [P, t], U32) for l, t in enumerate((T0, T1))]
        used = [sb(f"used{l}", [P, 1], I32) for l in range(2)]
        dest = [sb(f"dest{l}", [P, t], U32) for l, t in enumerate((T0, T1))]

        xs = [sb(f"xs{i}", [P, 2 * D]) for i in range(RING)]
        xsT = [sb(f"xsT{i}", [P, P]) for i in range(2)]
        z = [sb(f"z{i}", [P, F0]) for i in range(2)]
        h = [sb(f"h{i}", [P, F1]) for i in range(2)]
        hT = [sb(f"hT{i}", [P, K1 * P]) for i in range(2)]
        keep = [sb(f"keep{i}", [P, D]) for i in range(4)]
        y = [sb(f"y{i}", [P, D]) for i in range(4)]

        x2n = xn
        x2T = xnT[:, :].rearrange("p (c t) -> p c t", c=C)
        x3T = qT[:, :].rearrange("p (c t) -> p c t", c=C)
        ybk = kblk[:, :, :, :].rearrange("p b h m -> p (b h m)")[:, 0:C * 2 * D].rearrange(
            "p (c j d) -> p c j d", c=C, j=2)
        x2 = wgu[:, 0:N].rearrange("p (c d) -> p c d", c=C)
        row1 = wgu[:, N:3 * N].rearrange("p (c j d) -> p c j d", c=C, j=2)
        prob2T = wgu[0:M, 3 * N:4 * N].rearrange("p (c t) -> p c t", c=C)
        prob2 = wgu[:, 4 * N:4 * N + C * M].rearrange("p (c m) -> p c m", c=C)
        stat2 = sb("stat2", [P, C, 6])
        mv2 = sb("mv2", [P, C, 2])
        rstd2 = sb("rstd2", [P, C])
        smax2 = sb("smax2", [P, C])
        ssum2 = sb("ssum2", [P, C])
        rsum2 = sb("rsum2", [P, C])
        stat3 = sb("stat3", [P, C, 6])
        mv3 = sb("mv3", [P, C, 2])
        rstd3 = sb("rstd3", [P, C])

        psS = [bank("psS0", 1024), bank("psS1", 1024)]
        psT = bank("psT", 1024)
        psO = bank("psO")
        psX = bank("psX")
        b0, b1, b2, b3 = psS[0][:, 0:512], psS[0][:, 512:1024], psS[1][:, 0:512], psS[1][:, 512:1024]
        b4, b5 = psT[:, 0:512], psT[:, 512:1024]
        mis_onT, mis_out, mis_xT = psX[:, 0:128], psX[:, 128:256], psX[:, 256:384]
        logit = psX[:, 384:448].rearrange("p (c e) -> p c e", e=E)

        def wait_past(eng, semaphore, count):
            if count > 0:
                eng.wait_ge(semaphore, count)

        def tiles_used(eng, l):
            eng.wait_ge(experts_ready[l], 1)
            return eng.value_load(used[l][0:1, 0:1], min_val=0, max_val=(T0, T1)[l])

        def cst(name, partitions=P):
            a, b = CONST_AT[name]
            return consts[0:partitions, a:b]

        def vec(name):
            i = VECS.index(name)
            return vecs[:, i:i + 1]

        ident = cst("ident")
        wq, wk, wv, wo = (wqkvo[:, i, :] for i in range(4))
        bo_row, gateb_row, br_row = rows[:, 0:D], rows[:, D:D + E], rows[:, D + E:D + 2 * E]

        x_in_s = [sem(f"x_loaded{b}") for b in range(B)]
        small_s = sem("attention_weights_loaded")
        rows_s = sem("row_vectors_loaded")
        ctx_s = sem("ctx_loaded")
        const_s = sem("first_consts_loaded")
        const2_s = sem("other_consts_loaded")
        counts_ready = sem("counts_ready")
        bias_s = sem("bias_loaded")
        parts_ready = sem("bias_parts_ready")
        parts_stored = sem("bias_parts_stored")
        bias3_s = sem("bias3_loaded")
        f0_w = sem("mixture0_weights_loaded")
        f1_w = sem("mixture1_weights_loaded")
        pool_step = sem("pool_step")
        var_ready = sem("variances_ready")
        rstd_ready = sem("rstd_ready")
        dve_step = sem("dve_step")
        xn_ready = sem("xn_ready")
        cn_ready = sem("cn_ready")
        ctxT_ps = sem("ctxT_in_psum")
        ctxT_ready = sem("ctxT_ready")
        xT_ps = sem("xT_in_psum")
        xnT_ready = sem("xnT_ready")
        idle_ones_ready = sem("idle_ones_ready")
        table_taken = sem("function_table_taken")
        k_ps = sem("k_in_psum")
        kT_ready = sem("kT_ready")
        v_ps = sem("v_in_psum")
        v_ready = sem("v_ready")
        vv_ps = sem("v_spread_in_psum")
        vblk_ready = sem("vblk_ready")
        q_ps = sem("q_in_psum")
        q_ready = sem("q_ready")
        kblk_ready = [sem(f"kblk_ready{b}") for b in range(B)]
        ones_column = sem("ones_columns_ready")
        xbo_ready = sem("xbo_ready")
        prob_zero = sem("prob_padding_zero")
        s_ps = sem("scores_in_psum")
        sub_ready = sem("scores_less_max_ready")
        exp_ready = sem("exp_ready")
        pT_ps = sem("probT_in_psum")
        pT_ready = sem("probT_ready")
        o_ps = sem("heads_in_psum")
        on_ready = sem("heads_normalized")
        onT_ps = sem("headsT_in_psum")
        onT_ready = sem("headsT_ready")
        out_ps = sem("projection_in_psum")
        x1_ready = sem("x1_ready")
        xf_ready = sem("xf_ready")
        xf_stored = sem("xf_stored")
        xfT_ps = sem("xfT_in_psum")
        xfT_ready = sem("xfT_ready")
        logit_ps = sem("gate_logits_in_psum")

        l_less = [sem(f"logits_less_max{l}") for l in range(2)]
        ex_ready = sem("gate_exp_ready")
        pick_ready = [sem(f"picks_ready{l}") for l in range(2)]
        rank_ps = [sem(f"ranks_in_psum{l}") for l in range(2)]
        spread_ready = [sem(f"slots_spread{l}") for l in range(2)]
        table_ps = [sem(f"table_in_psum{l}") for l in range(2)]
        experts_ready = [sem(f"experts_ready{l}") for l in range(2)]
        intile_ready = [sem(f"pairs_tiles_ready{l}") for l in range(2)]
        onehot_ready = [sem(f"onehots_ready{l}") for l in range(2)]
        token_ready = [sem(f"tokens_ready{l}") for l in range(2)]
        dest_ready = [sem(f"destinations_ready{l}") for l in range(2)]

        gathered = [[sem(f"gathered{l}_{i}") for i in range(RING)] for l in range(2)]
        xsT_ps = [sem(f"xsT_in_psum{l}") for l in range(2)]
        xsT_ready = [sem(f"xsT_ready{l}") for l in range(2)]
        up_ps = [sem(f"hidden_in_psum{l}") for l in range(2)]
        up_half = sem("up_in_psum")
        z_up = sem("up_ready")
        z_ready = sem("gated_ready")
        h_ready = [sem(f"hidden_ready{l}") for l in range(2)]
        hT_ps = [sem(f"hiddenT_in_psum{l}") for l in range(2)]
        hT_ready = [sem(f"hiddenT_ready{l}") for l in range(2)]
        y_ps = [sem(f"y_in_psum{l}") for l in range(2)]
        y_ready = [sem(f"y_ready{l}") for l in range(2)]
        scattered = [[sem(f"scattered{l}_{i}") for i in range(4)] for l in range(2)]

        back_s = [sem(f"rows_back{b}") for b in range(B)]
        kept = sem("residual_rows_kept")
        x2n_ready = sem("x2n_ready")
        x2T_ps = sem("x2T_in_psum")
        x2T_ready = sem("x2T_ready")
        s2_ps = sem("scores2_in_psum")
        sub2_ready = sem("scores2_less_max_ready")
        exp2_ready = sem("exp2_ready")
        p2T_ps = sem("prob2T_in_psum")
        p2T_ready = sem("prob2T_ready")
        o2_ps = sem("attended_in_psum")
        row1_ready = sem("row1_ready")
        row1_stored = sem("row1_stored")
        x3T_ps = sem("x3T_in_psum")
        x3T_ready = sem("x3T_ready")
        logit1_ps = sem("router_logits_in_psum")

        block = stack.enter_context(nc.Block())

        @block.sync
        def _(sp):
            def load_x(b):
                sp.dma_start(x[:, CB * b:CB * (b + 1), :],
                             x_in[b].rearrange("(c p) d -> p c d", p=P)).then_inc(x_in_s[b], 16)

            sp.dma_start(ctx[:, :, :], ctx_in.rearrange("b m d -> m b d")).then_inc(ctx_s, 16)
            load_x(0)
            sp.dma_start(consts[:, 0:CONST_SPLIT], consts_in[:, 0:CONST_SPLIT]).then_inc(const_s, 16)
            sp.dma_start(vecs[:, :], vecs_in).then_inc(small_s, 16)
            sp.dma_start(wqkvo[:, :, :], wqkvo_in).then_inc(small_s, 16)
            load_x(1)
            sp.dma_start(consts[:, CONST_SPLIT:], consts_in[:, CONST_SPLIT:]).then_inc(const2_s, 16)
            sp.dma_start(rows[:, :], rows_in.partition_broadcast(P)).then_inc(rows_s, 16)
            sp.dma_start(gate[:, :, :], gate_in).then_inc(rows_s, 16)
            sp.dma_start(bias[:, :], bias_in).then_inc(bias_s, 16)
            half = E * F0
            sp.dma_start(wgu[:, 0:half], wgu_in[:, 0:half]).then_inc(f0_w, 16)
            sp.wait_ge(parts_ready, 3)
            for i in range(3):
                sp.dma_start(parts[i].rearrange("(p n) -> p n", p=P), part[:, i, :]).then_inc(parts_stored, 16)
            sp.dma_start(wgu[:, half:], wgu_in[:, half:]).then_inc(f0_w, 16)
            sp.wait_ge(parts_stored, 48)
            sp.dma_start(bias3[:, :], parts).then_inc(bias3_s, 16)
            sp.dma_start(dw[:, :], dw_in).then_inc(f0_w, 16)
            sp.dma_start(w1[:, :], w1_in).then_inc(f1_w, 16)
            sp.dma_start(w2[:, :], w2_in).then_inc(f1_w, 16)
            for c in range(C):
                sp.wait_ge(xf_ready, c + 1)
                sp.dma_start(rows0[P * c:P * (c + 1), :], xf[:, c, :]).then_inc(xf_stored, 16)

            def all_scattered(l):
                used_here = tiles_used(sp, l)
                with sp.If(used_here > ALWAYS[l]):
                    for i in range(4):
                        sp.wait_ge(scattered[l][i], 16 * len(range(i, (T0, T1)[l], 4)))
                with sp.Else():
                    for i in range(4):
                        sp.wait_ge(scattered[l][i], 16 * len(range(i, ALWAYS[l], 4)))

            all_scattered(0)
            for b in range(B):
                sp.dma_start(ybk[:, CB * b:CB * (b + 1), :, :],
                             back0[2 * P * CB * b:2 * P * CB * (b + 1), :].rearrange(
                                 "(c p j) d -> p c j d", p=P, j=2)).then_inc(back_s[b], 16)
            for b in range(B):
                sp.wait_ge(row1_ready, b + 1)
                sp.dma_start(rows1[P * CB * b:P * CB * (b + 1), :].rearrange("(c p) d -> p c d", p=P),
                             row1[:, CB * b:CB * (b + 1), :, :].rearrange("p c j d -> p c (j d)")
                             ).then_inc(row1_stored, 16)
            all_scattered(1)

        @block.gpsimd
        def _(pool):
            pool.memset(neghalf[:, :], -0.5).then_inc(pool_step, 1)
            pool.memset(ones3[:, :], 1.0).then_inc(pool_step, 1)
            pool.memset(idle_ones[:, :], 1.0).then_inc(idle_ones_ready, 1)
            roots = [0]

            def root(r):
                if roots[0] == 0:
                    pool.wait_ge(pool_step, 1)
                roots[0] += 1
                pool.wait_ge(var_ready, roots[0])
                pool.tensor_tensor(r, r, neghalf[0:r.shape[0], 0:r.shape[1]], ALU.pow).then_inc(rstd_ready, 1)

            pool.memset(prob[:, :, W:WP], 0.0).then_inc(prob_zero, 1)
            root(crstd[:, :])
            root(rstd[:, 0:CB])
            pool.wait_ge(const_s, 16)
            for b in range(B):
                for half in range(2):
                    pool.tensor_copy(vblk[:, b, half, :, :, DH],
                                     cst("blockmask").rearrange("p (j h) -> p j h", j=J)).then_inc(ones_column, 1)
            root(rstd[:, CB:C])
            pool.wait_ge(kT_ready, 1)
            pool.tensor_tensor(kblk[:, 1, :, :], kT[:, 1:2, :].broadcast_to([P, H, M]),
                               cst("headmask").unsqueeze(2).broadcast_to([P, H, M]), ALU.mult
                               ).then_inc(kblk_ready[1], 1)
            pool.wait_ge(const2_s, 16)
            small = CONST_AT["before"][0]
            pool.tensor_copy(counts[:, :], consts[:, small:small + 3 * P]).then_inc(counts_ready, 1)
            pool.wait_ge(rows_s, 32)
            for b in range(B):
                pool.wait_ge(x_in_s[b], 16)
                cs = slice(CB * b, CB * (b + 1))
                pool.tensor_tensor(xbo[:, cs, :], x[:, cs, :],
                                   bo_row.unsqueeze(1).broadcast_to([P, CB, D]), ALU.add).then_inc(xbo_ready, 1)
            pool.wait_ge(bias_s, 16)
            pool.tensor_copy(part[:, 0, :], bias[:, :]).then_inc(parts_ready, 1)
            pool.wait_ge(parts_ready, 1)
            pool.tensor_tensor(rest[:, 0, :], bias[:, :], part[:, 0, :], ALU.subtract).then_inc(pool_step, 1)
            pool.wait_ge(pool_step, 3)
            pool.tensor_copy(part[:, 1, :], rest[:, 0, :]).then_inc(parts_ready, 1)
            pool.wait_ge(parts_ready, 2)
            pool.tensor_tensor(rest[:, 1, :], rest[:, 0, :], part[:, 1, :], ALU.subtract).then_inc(pool_step, 1)
            pool.wait_ge(pool_step, 4)
            pool.tensor_copy(part[:, 2, :], rest[:, 1, :]).then_inc(parts_ready, 1)

            def gather(l, t):
                source, width = ((rows0, D), (rows1, 2 * D))[l]
                pool.indirect_dma_start(xs[t % RING][:, 0:width], None, source,
                                        bass.IndirectOffsetOnAxis(ap=token[l][:, t:t + 1], axis=0)
                                        ).then_inc(gathered[l][t % RING], 16)

            def scatter(l, t):
                target = (back0, out)[l]
                pool.indirect_dma_start(target, bass.IndirectOffsetOnAxis(ap=dest[l][:, t:t + 1], axis=0),
                                        y[t % 4][:, :], None, bounds_check=target.shape[0] - 1,
                                        oob_is_err=False).then_inc(scattered[l][t % 4], 16)

            for c in range(C):
                root(rstd1[:, c:c + 1])

            for l, tiles in enumerate((T0, T1)):
                if l == 1:
                    for r in (rstd2, rstd3):
                        for b in range(B):
                            root(r[:, CB * b:CB * (b + 1)])
                q = ((2 * C), C)[l]
                pool.wait_ge(intile_ready[l], 1)
                pool.tensor_tensor(tabv[:, 0:q, :, 0:tiles],
                                   intile[:, 0:q, 0:tiles].unsqueeze(2).broadcast_to([P, q, 3, tiles]),
                                   cst("tokval").rearrange("p (q k) -> p q k", k=3)[:, 0:q, :].unsqueeze(3)
                                   .broadcast_to([P, q, 3, tiles]), ALU.mult).then_inc(spread_ready[l], 1)
                pool.wait_ge((xf_stored, row1_stored)[l], (16 * C, 16 * B)[l])
                pool.wait_ge(token_ready[l], 1)
                for t in range(RING):
                    gather(l, t)
                pool.wait_ge(dest_ready[l], 1)
                used_here = tiles_used(pool, l)
                for t in range(ALWAYS[l]):
                    if t + RING < tiles:
                        pool.wait_ge(xsT_ps[l], t + 1)
                        if l == 1:
                            pool.wait_ge(kept, t + 1)
                        gather(l, t + RING)
                    pool.wait_ge(y_ready[l], t + 1)
                    scatter(l, t)
                with pool.If(used_here > ALWAYS[l]):
                    for t in range(ALWAYS[l], tiles):
                        pool.wait_ge(y_ready[l], t + 1)
                        scatter(l, t)

        @block.vector
        def _(dve):
            steps = [0]

            def link(ins):
                steps[0] += 1
                ins.then_inc(dve_step, 1)
                dve.wait_ge(dve_step, steps[0])

            rooted = [0]

            def stats(source, st, m, r, chunks, extra=0.0):
                n = source.shape[0]
                for c in chunks:
                    last = dve.bn_stats(st[0:n, c, :], source[:, c, :])
                link(last)
                for c in chunks:
                    last = dve.bn_aggr(m[0:n, c, :], st[0:n, c, :])
                link(last)
                a, b = chunks[0], chunks[-1] + 1
                dve.tensor_scalar(r[0:n, a:b], m[0:n, a:b, 1], 1.0 + extra, extra * extra if extra else EPS,
                                  ALU.mult, ALU.add).then_inc(var_ready, 1)
                rooted[0] += 1
                return rooted[0]

            def normal(target, source, m, r, c):
                n = source.shape[0]
                return dve.tensor_scalar(target, source[:, c, :], m[0:n, c, 0:1], r[0:n, c:c + 1],
                                         ALU.subtract, ALU.mult)

            def query_stats(b):
                dve.wait_ge(x_in_s[b], 16)
                stats(x[:, :, :], stat, mv, rstd, range(CB * b, CB * (b + 1)), extra=EPS)

            def query_rows(b):
                dve.wait_ge(rstd_ready, 2 + b)
                for c in range(CB * b, CB * (b + 1)):
                    normal(xn[:, c, :], x[:, :, :], mv, rstd, c).then_inc(xn_ready, 1)

            def queries(b, source):
                dve.wait_ge(q_ps, b + 1)
                dve.tensor_scalar(qT[:, 512 * b:512 * (b + 1)], source, vec("bq"), DH ** -0.5,
                                  ALU.add, ALU.mult).then_inc(q_ready, 1)

            dve.wait_ge(ctx_s, 16)
            stats(ctx[:, :, :], cstat, cmv, crstd, range(B))
            query_stats(0)
            dve.wait_ge(rstd_ready, 1)
            for b in range(B):
                normal(cn[:, b, :], ctx[:, :, :], cmv, crstd, b).then_inc(cn_ready, 1)
            query_rows(0)
            dve.wait_ge(small_s, 32)
            dve.wait_ge(ctxT_ps, 2)
            raw = b5[:, 0:2 * B * M].rearrange("p (k b m) -> p k b m", k=2, b=B)
            dve.tensor_scalar(ckT[:, :, :], raw[:, 0], vec("lnkw"), vec("lnkb"), ALU.mult, ALU.add
                              ).then_inc(ctxT_ready, 1)
            dve.wait_ge(k_ps, 1)
            dve.tensor_scalar(kT[:, :, :], psX[:, 0:B * M].rearrange("p (b m) -> p b m", b=B),
                              vec("bk"), None, ALU.add).then_inc(kT_ready, 1)
            dve.wait_ge(kT_ready, 1)
            for half in range(2):
                some = slice(HH * half, HH * (half + 1))
                dve.tensor_tensor(kblk[:, 0, some, :], kT[:, 0:1, :].broadcast_to([P, HH, M]),
                                  cst("headmask")[:, some].unsqueeze(2).broadcast_to([P, HH, M]), ALU.mult
                                  ).then_inc(kblk_ready[0], 1)
                if half == 0:
                    queries(0, b2)
            dve.tensor_scalar(cvT[:, :, :], raw[:, 0], vec("lnvw"), vec("lnvb"), ALU.mult, ALU.add
                              ).then_inc(ctxT_ready, 1)

            def values_as_rows():
                dve.tensor_copy(cT[:, :, :], raw[:, 1])
                dve.wait_ge(v_ps, 1)
                dve.tensor_copy(v[:, :, :], psO[0:M, 0:B * D].rearrange("p (b d) -> p b d", b=B)
                                ).then_inc(v_ready, 1)

            def values(b):
                mask = cst("blockmask").rearrange("p (j h) -> p j h", j=J).unsqueeze(3).broadcast_to([P, J, HH, DH])
                vv = psT[:, 0:J * D].rearrange("p (j s h c) -> p s j h c", j=J, s=2, h=HH)
                dve.wait_ge(vv_ps, b + 1)
                if b == 0:
                    dve.wait_ge(ones_column, 2 * B)
                for half in range(2):
                    last = dve.tensor_tensor(vblk[:, b, half, :, :, 0:DH], vv[:, half], mask, ALU.mult)
                last.then_inc(vblk_ready, 1)

            def scores(g):
                s = psS[g % 2][:, 0:W].rearrange("p (h m) -> p h m", h=HH)
                dve.wait_ge(s_ps, g + 1)
                link(dve.tensor_reduce(smax[:, g % 2, :], s, AX.X, ALU.max))
                if g == 0:
                    dve.wait_ge(prob_zero, 1)
                if g >= 3:
                    dve.wait_ge(pT_ps, g - 2)
                dve.tensor_tensor(prob[:, g % 3, 0:W].rearrange("p (h m) -> p h m", h=HH), s,
                                  smax[:, g % 2, :].unsqueeze(2).broadcast_to([P, HH, M]), ALU.subtract
                                  ).then_inc(sub_ready, 1)

            def heads(c):
                o = psO[:, 0:H * OW].rearrange("p (h w) -> p h w", h=H)
                dve.wait_ge(o_ps, 2 * c + 2)
                link(dve.reciprocal(rsum[:, :], o[:, :, DH]))
                if c >= 2:
                    dve.wait_ge(onT_ps, c - 1)
                dve.tensor_tensor(on[:, c % 2, :].rearrange("p (h w) -> p h w", h=H), o[:, :, 0:DH],
                                  rsum[:, :].unsqueeze(2).broadcast_to([P, H, DH]), ALU.mult
                                  ).then_inc(on_ready, 1)

            def residual(c):
                dve.wait_ge(out_ps, c + 1)
                if c % CB == 0:
                    dve.wait_ge(xbo_ready, c // CB + 1)
                dve.tensor_tensor(x1[:, c, :], mis_out, xbo[:, c, :], ALU.add).then_inc(x1_ready, 1)
                dve.wait_ge(x1_ready, c + 1)
                stats(x1[:, :, :], stat1, mv1, rstd1, range(c, c + 1))

            def rows_for_gate(c):
                dve.wait_ge(rstd_ready, 3 + c + 1)
                normal(xf[:, c, :], x1[:, :, :], mv1, rstd1, c).then_inc(xf_ready, 1)

            for g in range(G + 7):
                if g < G:
                    scores(g)
                if g == 0:
                    values_as_rows()
                if g == 1:
                    values(0)
                    values(1)
                if g == 2:
                    query_stats(1)
                if g == 3:
                    query_rows(1)
                if g == 5:
                    queries(1, psX[:, :])
                if g >= 8 and g % 2 == 0 and (g - 8) // 2 < C:
                    rows_for_gate((g - 8) // 2)
                if g >= 4 and g % 2 == 0 and (g - 4) // 2 < C:
                    heads((g - 4) // 2)
                if g >= 6 and g % 2 == 0 and (g - 6) // 2 < C:
                    residual((g - 6) // 2)

            def route(l):
                choices = (2, 1)[l]
                tiles = (T0, T1)[l]
                rev = cst("rev").rearrange("p (c e) -> p c e", e=E)
                dve.wait_ge((logit_ps, logit1_ps)[l], C)
                if l == 0:
                    dve.wait_ge(const2_s, 16)
                    dve.wait_ge(rows_s, 32)
                    dve.wait_ge(counts_ready, 1)
                bias_row = (gateb_row, br_row)[l]
                link(dve.tensor_tensor(lg[:, :, :], logit, bias_row.unsqueeze(1).broadcast_to([P, C, E]), ALU.add))
                link(dve.tensor_reduce(top[:, 0, :], lg[:, :, :], AX.X, ALU.max))
                dve.tensor_tensor(lg2[:, :, :], lg[:, :, :], top[:, 0, :].unsqueeze(2).broadcast_to([P, C, E]),
                                  ALU.subtract).then_inc(l_less[l], 1)
                dve.wait_ge(l_less[l], 1)
                link(dve.scalar_tensor_tensor(out=key[:, :, :], in0=lg2[:, :, :], scalar=0.0, in1=rev,
                                              op0=ALU.is_ge, op1=ALU.mult))
                link(dve.tensor_reduce(kmax[:, 0, :], key[:, :, :], AX.X, ALU.max))
                first = dve.tensor_tensor(pick[:, 0, :, :], rev, kmax[:, 0, :].unsqueeze(2).broadcast_to([P, C, E]),
                                          ALU.is_equal)
                if l == 1:
                    first.then_inc(pick_ready[l], 1)
                    dve.wait_ge(pick_ready[l], 1)
                else:
                    link(first)
                    link(dve.scalar_tensor_tensor(out=lg[:, :, :], in0=pick[:, 0, :, :], scalar=NEG,
                                                  in1=lg2[:, :, :], op0=ALU.mult, op1=ALU.add))
                    dve.tensor_reduce(top[:, 1, :], lg[:, :, :], AX.X, ALU.max).then_inc(l_less[l], 1)
                    dve.wait_ge(l_less[l], 2)
                    link(dve.tensor_tensor(key[:, :, :], lg[:, :, :],
                                           top[:, 1, :].unsqueeze(2).broadcast_to([P, C, E]), ALU.is_ge))
                    link(dve.tensor_tensor(key[:, :, :], key[:, :, :], rev, ALU.mult))
                    link(dve.tensor_reduce(kmax[:, 1, :], key[:, :, :], AX.X, ALU.max))
                    link(dve.tensor_tensor(pick[:, 1, :, :], rev,
                                           kmax[:, 1, :].unsqueeze(2).broadcast_to([P, C, E]), ALU.is_equal))
                    dve.tensor_tensor(both[:, :, :], pick[:, 0, :, :], pick[:, 1, :, :], ALU.add
                                      ).then_inc(pick_ready[l], 1)
                dve.wait_ge(rank_ps[l], 1)
                rank = b0[:, 0:C * E].rearrange("p (c e) -> p c e", e=E)
                count = b1[:, 0:E]
                link(dve.tensor_tensor(over[:, :, :], count.unsqueeze(2).broadcast_to([P, E, E]),
                                       cst("kstep").rearrange("p (e k) -> p e k", k=E), ALU.is_gt))
                link(dve.tensor_reduce(ntl[:, :], over[:, :, :], AX.X, ALU.add))
                link(dve.tensor_tensor(over[:, :, :], ntl[:, :].unsqueeze(1).broadcast_to([P, E, E]),
                                       cst("earlier").rearrange("p (e k) -> p e k", k=E), ALU.mult))
                link(dve.tensor_reduce(base[:, :], over[:, :, :], AX.X, ALU.add))
                link(dve.scalar_tensor_tensor(out=place[:, :, :], in0=base[:, :].unsqueeze(1).broadcast_to([P, C, E]),
                                              scalar=float(P), in1=rank, op0=ALU.mult, op1=ALU.add))
                link(dve.tensor_tensor(slots[:, 0:choices, :, :], pick[:, 0:choices, :, :],
                                       place[:, :, :].unsqueeze(1).broadcast_to([P, choices, C, E]), ALU.mult))
                q = choices * C
                with nc.allow_low_precision(reason="slot numbers are integers below 4096"):
                    link(dve.tensor_reduce(slot[:, 0:q], slots[:, 0:choices, :, :].rearrange("p j c e -> p (j c) e"),
                                           AX.X, ALU.add))
                link(dve.tensor_scalar(lane[:, 0:q], slot[:, 0:q], P - 1, None, ALU.bitwise_and))
                dve.tensor_copy(lanef[:, 0:q], lane[:, 0:q])
                link(dve.tensor_tensor(tilef[:, 0:q], slot[:, 0:q], lane[:, 0:q], ALU.subtract))
                dve.tensor_tensor(intile[:, 0:q, 0:tiles], cst("tstep")[:, 0:tiles].unsqueeze(1).broadcast_to([P, q, tiles]),
                                  tilef[:, 0:q].unsqueeze(2).broadcast_to([P, q, tiles]), ALU.is_equal
                                  ).then_inc(intile_ready[l], 1)
                for i in range(q):
                    dve.tensor_scalar(onehot[:, i, :], counts[:, 2 * P:3 * P], lanef[:, i:i + 1], None, ALU.is_equal
                                      ).then_inc(onehot_ready[l], 1)
                link(dve.tensor_tensor(ends[:, :], base[:, :], ntl[:, :], ALU.add))
                dve.tensor_copy(used[l][:, :], ends[:, E - 1:E])
                link(dve.tensor_tensor(etile[:, 0:tiles, :], ends[:, :].unsqueeze(1).broadcast_to([P, tiles, E]),
                                       cst("tilecol").rearrange("p (t e) -> p t e", e=E)[:, 0:tiles], ALU.is_le))
                link(dve.tensor_reduce(esum[:, 0:tiles], etile[:, 0:tiles, :], AX.X, ALU.add))
                dve.tensor_scalar(expert[l][:, :], esum[:, 0:tiles], float(E - 1), None, ALU.min
                                  ).then_inc(experts_ready[l], 1)
                dve.wait_ge(table_ps[l], 1)
                table = b5[:, 0:3 * tiles].rearrange("p (k t) -> p k t", k=3)
                link(dve.tensor_copy(slottok[:, 0:tiles], table[:, 0]))
                dve.tensor_tensor(token[l][:, :], slottok[:, 0:tiles], table[:, 2], ALU.add).then_inc(token_ready[l], 1)
                dve.tensor_scalar(padrow[:, 0:tiles], table[:, 1], 0.0, float(4 * N), ALU.is_equal, ALU.mult)
                link(dve.tensor_tensor(slottok[:, 0:tiles], slottok[:, 0:tiles], table[:, 2], ALU.add))
                if l == 0:
                    link(dve.scalar_tensor_tensor(out=slottok[:, 0:tiles], in0=slottok[:, 0:tiles], scalar=2.0,
                                                  in1=table[:, 1], op0=ALU.mult, op1=ALU.add))
                dve.scalar_tensor_tensor(out=dest[l][:, :], in0=slottok[:, 0:tiles], scalar=(-1.0, 0.0)[l],
                                         in1=padrow[:, 0:tiles], op0=ALU.add, op1=ALU.add
                                         ).then_inc(dest_ready[l], 1)

            def choice_weights():
                dve.wait_ge(ex_ready, 2)
                link(dve.tensor_reduce(wt[:, 0, :], ex[:, :, :], AX.X, ALU.add))
                link(dve.reciprocal(wt[:, 1, :], wt[:, 0, :]))
                link(dve.tensor_tensor(wt[:, 2, :], ex2[:, :], wt[:, 1, :], ALU.mult))
                link(dve.scalar_tensor_tensor(out=wt[:, 3, :], in0=wt[:, 1, :], scalar=1e-20, in1=wt[:, 2, :],
                                              op0=ALU.add, op1=ALU.add))
                link(dve.reciprocal(wt[:, 4, :], wt[:, 3, :]))
                for j in range(2):
                    last = dve.tensor_tensor(weight[:, j, :], wt[:, 1 + j, :], wt[:, 4, :], ALU.mult)
                link(last)

            route(0)
            choice_weights()

            def mix(l):
                tiles = (T0, T1)[l]
                rows_ = (FB0, P)[l]

                def step(n, tiles):
                    if l == 0 and n < tiles:
                        dve.wait_ge(up_ps[0], n + 1)
                        dve.wait_ge(z_up, n + 1)
                        dve.tensor_tensor(z[n % 2][:, :], (b1, b3)[n % 2][:, 0:F0], z[n % 2][:, :], ALU.mult
                                          ).then_inc(z_ready, 1)
                    if 1 <= n <= tiles:
                        dve.wait_ge(hT_ps[l], n)
                        wait_past(dve, y_ps[l], n - 2)
                        dve.tensor_copy(hT[(n - 1) % 2][0:rows_, :], b4[0:rows_, :]).then_inc(hT_ready[l], 1)
                    if 2 <= n <= tiles + 1:
                        dve.wait_ge(y_ps[l], n - 1)
                        wait_past(dve, scattered[l][(n - 2) % 4], (n - 2) // 4 * 16)
                        source = psO[:, 0:D]
                        if l == 0:
                            dve.tensor_copy(y[(n - 2) % 4][:, :], source).then_inc(y_ready[l], 1)
                        else:
                            dve.wait_ge(kept, n - 1)
                            dve.tensor_tensor(y[(n - 2) % 4][:, :], source, keep[(n - 2) % 4][:, :], ALU.add
                                              ).then_inc(y_ready[l], 1)

                used_here = tiles_used(dve, l)
                for n in range(ALWAYS[l]):
                    step(n, tiles)
                with dve.If(used_here > ALWAYS[l]):
                    for n in range(ALWAYS[l], tiles + 2):
                        step(n, tiles)
                with dve.Else():
                    for n in range(ALWAYS[l], ALWAYS[l] + 2):
                        step(n, ALWAYS[l])

            mix(0)

            groups = [range(CB * b, CB * (b + 1)) for b in range(B)]
            spans = [slice(g[0], g[-1] + 1) for g in groups]

            def combine(b):
                dve.wait_ge(back_s[b], 16)
                for j, before in enumerate((x1, x2)):
                    for c in groups[b]:
                        last = dve.scalar_tensor_tensor(out=x2[:, c, :], in0=ybk[:, c, j, :],
                                                        scalar=weight[:, j, c:c + 1], in1=before[:, c, :],
                                                        op0=ALU.mult, op1=ALU.add)
                    link(last)

            def attending_stats(b):
                first_root[b] = stats(x2[:, :, :], stat2, mv2, rstd2, groups[b])

            def attending_rows(b):
                dve.wait_ge(rstd_ready, first_root[b])
                for c in groups[b]:
                    last = normal(x2n[:, c, :], x2[:, :, :], mv2, rstd2, c)
                last.then_inc(x2n_ready, 1)

            def less_max(b):
                s2 = (b2, b3)[b][:, 0:CB * M].rearrange("p (c m) -> p c m", m=M)
                dve.wait_ge(s2_ps, b + 1)
                link(dve.tensor_reduce(smax2[:, spans[b]], s2, AX.X, ALU.max))
                dve.tensor_tensor(prob2[:, spans[b], :], s2, smax2[:, spans[b]].unsqueeze(2).broadcast_to([P, CB, M]),
                                  ALU.subtract).then_inc(sub2_ready, 1)

            def row_sums(b):
                dve.wait_ge(exp2_ready, b + 1)
                link(dve.tensor_reduce(ssum2[:, spans[b]], prob2[:, spans[b], :], AX.X, ALU.add))
                link(dve.reciprocal(rsum2[:, spans[b]], ssum2[:, spans[b]]))

            def residual2(b):
                dve.wait_ge(o2_ps, b + 1)
                o2 = (psO, b3)[b][:, :].rearrange("p (c d) -> p c d", c=CB)
                for i, c in enumerate(groups[b]):
                    last = dve.scalar_tensor_tensor(out=row1[:, c, 1, :], in0=o2[:, i, :], scalar=rsum2[:, c:c + 1],
                                                    in1=x2[:, c, :], op0=ALU.mult, op1=ALU.add)
                link(last)
                second_root[b] = stats(row1[:, :, 1, :], stat3, mv3, rstd3, groups[b])

            def mixed_rows(b):
                dve.wait_ge(rstd_ready, second_root[b])
                for c in groups[b]:
                    last = normal(row1[:, c, 0, :], row1[:, :, 1, :], mv3, rstd3, c)
                last.then_inc(row1_ready, 1)

            first_root, second_root = {}, {}
            combine(0)
            attending_stats(0)
            combine(1)
            attending_stats(1)
            attending_rows(0)
            attending_rows(1)
            less_max(0)
            row_sums(0)
            less_max(1)
            residual2(0)
            row_sums(1)
            residual2(1)
            mixed_rows(0)
            mixed_rows(1)

            route(1)
            mix(1)

        @block.scalar
        def _(act):
            def gate_rows(c):
                act.wait_ge(xfT_ps, c + 1)
                if c >= 2:
                    act.wait_ge(logit_ps, c - 1)
                act.copy(xfT[:, c % 2, :], mis_xT).then_inc(xfT_ready, 1)

            def query_rows(b, source):
                act.wait_ge(xT_ps, b + 1)
                act.activation(xnT[:, 512 * b:512 * (b + 1)], source, ACT.Identity, bias=vec("lnqb"),
                               scale=vec("lnqw")).then_inc(xnT_ready, 1)

            def take_table(func):
                act.activation(idle[:, :], neghalf[:, 0:1], func).then_inc(table_taken, 1)

            act.wait_ge(pool_step, 1)
            take_table(ACT.Exp)
            act.wait_ge(small_s, 32)
            query_rows(0, b0)

            for g in range(G + 8):
                if g == 5:
                    query_rows(1, psX[:, :])
                if 2 <= g < G + 2:
                    act.wait_ge(pT_ps, g - 1)
                    if g >= 4:
                        act.wait_ge(o_ps, g - 3)
                    act.copy(probT[:, g % 2, :], psT[:, 0:WP]).then_inc(pT_ready, 1)
                if g < G:
                    act.wait_ge(sub_ready, g + 1)
                    act.activation(prob[:, g % 3, 0:W], prob[:, g % 3, 0:W], ACT.Exp).then_inc(exp_ready, 1)
                if g >= 5 and g % 2 == 1 and (g - 5) // 2 < C:
                    c = (g - 5) // 2
                    act.wait_ge(onT_ps, c + 1)
                    if c >= 2:
                        act.wait_ge(xfT_ps, c - 1)
                    if c >= 2:
                        act.wait_ge(out_ps, c - 1)
                    act.activation(onT[:, c % 2, :], mis_onT, ACT.Identity, bias=vec("bv")).then_inc(onT_ready, 1)
                if g >= 9 and g % 2 == 1 and (g - 9) // 2 < C:
                    gate_rows((g - 9) // 2)
            act.wait_ge(l_less[0], 1)
            act.activation(ex[:, :, :], lg2[:, :, :], ACT.Exp).then_inc(ex_ready, 1)
            act.wait_ge(l_less[0], 2)
            act.activation(ex2[:, :], top[:, 1, :], ACT.Exp).then_inc(ex_ready, 1)
            act.wait_ge(table_taken, 1)
            take_table(ACT.Silu)

            def mix(l):
                tiles = (T0, T1)[l]

                def take(n):
                    act.wait_ge(xsT_ps[l], n + 1)
                    wait_past(act, up_ps[l], n - 1)
                    act.copy(xsT[n % 2][:, :], psX[:, 0:P]).then_inc(xsT_ready[l], 1)
                    if l == 1:
                        wait_past(act, y_ready[1], n - 3)
                        act.copy(keep[n % 4][:, :], xs[n % RING][:, D:2 * D]).then_inc(kept, 1)

                def step(n, tiles):
                    if n + 1 < tiles:
                        take(n + 1)
                    if n < tiles:
                        wait_past(act, hT_ps[l], n - 1)
                        if l == 0:
                            act.wait_ge(up_half, n + 1)
                            act.copy(z[n % 2][:, :], (b0, b2)[n % 2][:, 0:F0]).then_inc(z_up, 1)
                            act.wait_ge(z_ready, n + 1)
                            act.activation(h[n % 2][:, 0:F0], z[n % 2][:, :], ACT.Silu).then_inc(h_ready[0], 1)
                        else:
                            act.wait_ge(up_ps[1], n + 1)
                            act.activation(h[n % 2][:, :], (b0, b1)[n % 2], ACT.Gelu).then_inc(h_ready[1], 1)

                used_here = tiles_used(act, l)
                take(0)
                for n in range(ALWAYS[l]):
                    step(n, tiles)
                with act.If(used_here > ALWAYS[l]):
                    for n in range(ALWAYS[l], tiles + 2):
                        step(n, tiles)

            mix(0)
            act.wait_ge(table_taken, 2)
            take_table(ACT.Exp)

            def attending_rows(b):
                act.wait_ge(x2T_ps, b + 1)
                act.copy(x2T[:, CB * b:CB * (b + 1), :].rearrange("p c t -> p (c t)"), (b0, b1)[b]
                         ).then_inc(x2T_ready, 1)

            def exponentials(b):
                act.wait_ge(sub2_ready, b + 1)
                p2 = prob2[:, CB * b:CB * (b + 1), :].rearrange("p c m -> p (c m)")
                act.activation(p2, p2, ACT.Exp, scale=float(D) ** -0.5).then_inc(exp2_ready, 1)

            def probabilities(b):
                act.wait_ge(p2T_ps, b + 1)
                act.copy(prob2T[:, CB * b:CB * (b + 1), :].rearrange("m c t -> m (c t)"), (b4, b5)[b][0:M, :]
                         ).then_inc(p2T_ready, 1)

            def gate_rows2(b):
                act.wait_ge(x3T_ps, b + 1)
                act.copy(x3T[:, CB * b:CB * (b + 1), :].rearrange("p c t -> p (c t)"), (b0, b1)[b]
                         ).then_inc(x3T_ready, 1)

            attending_rows(0)
            attending_rows(1)
            exponentials(0)
            probabilities(0)
            exponentials(1)
            probabilities(1)
            act.wait_ge(table_taken, 3)
            take_table(ACT.Gelu)
            gate_rows2(0)
            gate_rows2(1)

            mix(1)

        @block.tensor
        def _(pe):
            def keep_warm(n, bank=b4):
                for i in range(n):
                    pe.matmul(bank[:, :].rearrange("p (k t) -> p k t", k=4), idle_ones[:, :],
                              idle_ones[:, :].unsqueeze(1).broadcast_to([P, 4, P]), start=True, stop=True)

            def query_rows(b, target):
                pe.wait_ge(xn_ready, CB * (b + 1))
                for c in range(CB):
                    last = pe.transpose(target[:, P * c:P * (c + 1)], xn[:, CB * b + c, :], ident)
                last.then_inc(xT_ps, 1)

            def queries(b, target):
                pe.wait_ge(xnT_ready, b + 1)
                pe.matmul(target, wq, xnT[:, 512 * b:512 * (b + 1)], start=True, stop=True).then_inc(q_ps, 1)

            pe.wait_ge(idle_ones_ready, 1)
            keep_warm(WARM_START)
            pe.wait_ge(const_s, 16)
            pe.wait_ge(cn_ready, B)
            for source, k in ((cn, 0), (ctx, 1)):
                for b in range(B):
                    i = k * B + b
                    last = pe.transpose(b5[:, i * M:(i + 1) * M], source[:, b, :], ident[0:M, 0:M])
                last.then_inc(ctxT_ps, 1)
            query_rows(0, b0)
            pe.wait_ge(small_s, 32)
            keep_warm(WARM_KEYS)
            pe.wait_ge(ctxT_ready, 1)
            pe.matmul(psX[:, 0:B * M], wk, ckT[:, :, :].rearrange("p b m -> p (b m)"), start=True, stop=True
                      ).then_inc(k_ps, 1)
            queries(0, b2)

            def values(b):
                pe.wait_ge(v_ready, 1)
                if b:
                    pe.wait_ge(vblk_ready, b)
                for j in range(J):
                    last = pe.matmul(psT[:, P * j:P * (j + 1)], cst("sel", M)[:, P * j:P * (j + 1)], v[:, b, :],
                                     start=True, stop=True)
                last.then_inc(vv_ps, 1)

            def scores(g):
                c, s = g // 2, g % 2
                b = c // CB
                if g in (0, G // 2):
                    pe.wait_ge(q_ready, b + 1)
                    pe.wait_ge(kblk_ready[b], 1)
                if g == 1:
                    pe.wait_ge(kblk_ready[0], 2)
                if g >= 2:
                    pe.wait_ge(sub_ready, g - 1)
                keys = kblk[:, b, HH * s:HH * (s + 1), :].rearrange("p h m -> p (h m)")
                pe.matmul(psS[g % 2][:, 0:512], qT[:, P * c:P * (c + 1)], keys[:, 0:512], start=True, stop=True)
                pe.matmul(psS[g % 2][:, 512:W], qT[:, P * c:P * (c + 1)], keys[:, 512:W], start=True, stop=True
                          ).then_inc(s_ps, 1)

            def turn(g):
                pe.wait_ge(exp_ready, g + 1)
                if g >= 1:
                    pe.wait_ge(pT_ready, g)
                else:
                    pe.wait_ge(vblk_ready, B)
                for j in range(J):
                    last = pe.transpose(psT[:, P * j:P * (j + 1)], prob[:, g % 3, P * j:P * (j + 1)], ident)
                last.then_inc(pT_ps, 1)

            def attend(g):
                c, s = g // 2, g % 2
                pe.wait_ge(pT_ready, g + 1)
                if s == 0 and c >= 1:
                    pe.wait_ge(on_ready, c)
                for j in range(J):
                    ha, hb = P * j // M, min((P * (j + 1) - 1) // M, HH - 1) + 1
                    a = OW * (HH * s + ha)
                    last = pe.matmul(psO[:, a:a + OW * (hb - ha)], probT[:, g % 2, P * j:P * (j + 1)],
                                     vblk[:, c // CB, s, j, ha:hb, :].rearrange("p h w -> p (h w)"),
                                     start=(j == 0), stop=(j == J - 1), skip_group_check=True)
                last.then_inc(o_ps, 1)

            for g in range(G + 9):
                if g < G:
                    scores(g)
                elif g < G + 4:
                    keep_warm(WARM_TAIL[0], b0)
                else:
                    keep_warm(WARM_TAIL[1], b0)
                if g == 0:
                    pe.wait_ge(ctxT_ready, 2)
                    for i in range(B):
                        last = pe.matmul(psO[0:M, i * D:(i + 1) * D], cvT[:, i, :], wv, start=True, stop=True)
                    last.then_inc(v_ps, 1)
                if g == 1:
                    keep_warm(WARM_VALUES, psX)
                    values(0)
                    keep_warm(WARM_VALUES, psX)
                    values(1)
                if 2 <= g < G + 2:
                    turn(g - 2)
                if 3 <= g < G + 3:
                    attend(g - 3)
                if g == 4:
                    query_rows(1, psX[:, :])
                if g == 5:
                    queries(1, psX[:, :])
                c = (g - 5) // 2
                if g >= 5 and g % 2 == 1 and c < C:
                    pe.wait_ge(on_ready, c + 1)
                    pe.wait_ge(q_ready, B)
                    if c >= 1:
                        pe.wait_ge(x1_ready, c)
                    pe.transpose(mis_onT, on[:, c % 2, :], ident).then_inc(onT_ps, 1)
                c = (g - 9) // 2
                if g >= 9 and g % 2 == 1 and c < C:
                    pe.wait_ge(xf_ready, c + 1)
                    pe.wait_ge(x1_ready, min(c + 2, C))
                    pe.transpose(mis_xT, xf[:, c, :], ident).then_inc(xfT_ps, 1)
                c = (g - 10) // 2
                if g >= 10 and g % 2 == 0 and c < C:
                    pe.wait_ge(xfT_ready, c + 1)
                    if c + 2 < C:
                        pe.wait_ge(onT_ready, c + 3)
                    pe.matmul(logit[:, c, :], xfT[:, c % 2, :], gate[:, 0, :], start=True, stop=True
                              ).then_inc(logit_ps, 1)
                c = (g - 6) // 2
                if g >= 6 and g % 2 == 0 and c < C:
                    pe.wait_ge(onT_ready, c + 1)
                    pe.matmul(mis_out, onT[:, c % 2, :], wo, start=True, stop=True).then_inc(out_ps, 1)

            def route(l):
                chosen = both[:, :, :] if l == 0 else pick[:, 0, :, :]
                before, ones = counts[:, 0:P], counts[:, P:2 * P]
                pe.wait_ge(counts_ready, 1)
                pe.wait_ge(pick_ready[l], 1)
                pe.matmul(b0[:, 0:C * E], before, chosen.rearrange("p c e -> p (c e)"), start=True, stop=False,
                          skip_group_check=True)
                for s in range(1, C):
                    pe.matmul(b0[:, s * E:C * E], ones, chosen[:, 0:C - s, :].rearrange("p c e -> p (c e)"),
                              start=False, stop=(s == C - 1), skip_group_check=True)
                for c in range(C):
                    last = pe.matmul(b1[:, 0:E], ones, chosen[:, c, :], start=(c == 0), stop=(c == C - 1))
                last.then_inc(rank_ps[l], 1)
                keep_warm(WARM_RANK[l])
                pe.wait_ge(spread_ready[l], 1)
                q, tiles = ((2 * C, T0), (C, T1))[l]
                for i in range(q):
                    pe.wait_ge(onehot_ready[l], i + 1)
                    last = pe.matmul(b5[:, 0:3 * tiles].rearrange("p (k t) -> p k t", k=3), onehot[:, i, :],
                                     tabv[:, i, :, 0:tiles], start=(i == 0), stop=(i == q - 1))
                last.then_inc(table_ps[l], 1)
                pe.wait_ge(experts_ready[l], 1)
                keep_warm(WARM_TABLE)

            def mix(l):
                tiles = (T0, T1)[l]

                its = {}

                def choose(n):
                    its[n] = pe.value_load(expert[l][0:1, n:n + 1], min_val=0, max_val=E - 1)

                def take(n):
                    pe.wait_ge(gathered[l][n % RING], (n // RING + 1) * 16)
                    wait_past(pe, xsT_ready[l], n)
                    pe.transpose(psX[:, 0:P], xs[n % RING][:, 0:D], ident
                                 ).then_inc(xsT_ps[l], 1)

                def up(n):
                    e = its[n]
                    pe.wait_ge(xsT_ready[l], n + 1)
                    wait_past(pe, (z_ready, h_ready[1])[l], n - 1)
                    if l == 0:
                        for k, target in enumerate(((b0, b1), (b2, b3))[n % 2]):
                            pe.matmul(target[:, 0:F0], xsT[n % 2][:, :], wgu[:, bass.ds(e * (2 * F0) + (1 - k) * F0, F0)],
                                      start=True, stop=False)
                            last = pe.matmul(target[:, 0:F0], ones3[:, :], bias3[:, bass.ds(e * BI0 + (1 - k) * F0, F0)],
                                             start=False, stop=True)
                            if k == 0:
                                last.then_inc(up_half, 1)
                    else:
                        target = (b0, b1)[n % 2]
                        pe.matmul(target, xsT[n % 2][:, :], w1[:, bass.ds(e * F1, F1)], start=True, stop=False)
                        last = pe.matmul(target, ones3[:, :], bias3[:, bass.ds(e * BI1 + E * BI0, F1)],
                                         start=False, stop=True)
                    last.then_inc(up_ps[l], 1)

                def turn(n):
                    pe.wait_ge(h_ready[l], n + 1)
                    wait_past(pe, hT_ready[l], n)
                    f = (FB0, P)[l]
                    for k in range(K0):
                        last = pe.transpose(b4[0:f, P * k:P * (k + 1)], h[n % 2][:, f * k:f * (k + 1)], ident)
                    last.then_inc(hT_ps[l], 1)

                def down(n):
                    e = its[n]
                    pe.wait_ge(hT_ready[l], n + 1)
                    wait_past(pe, y_ready[l], n)
                    f = (FB0, P)[l]
                    target = psO[:, 0:D]
                    w, stride, b_at = ((dw, K0 * D, e * BI0 + 2 * F0), (w2, K1 * D, e * BI1 + (E * BI0 + F1)))[l]
                    for k in range(K0):
                        pe.matmul(target, hT[n % 2][0:f, P * k:P * (k + 1)], w[:, bass.ds(e * stride + k * D, D)],
                                  start=(k == 0), stop=False)
                    pe.matmul(target, ones3[:, :], bias3[:, bass.ds(b_at, D)], start=False, stop=True
                              ).then_inc(y_ps[l], 1)

                def step(n, tiles):
                    if n + 1 < tiles:
                        take(n + 1)
                    if n < tiles:
                        up(n)
                    if 1 <= n <= tiles:
                        turn(n - 1)
                    if n + 1 < tiles:
                        choose(n + 1)
                    if 2 <= n <= tiles + 1:
                        down(n - 2)

                pe.wait_ge((f0_w, f1_w)[l], (48, 32)[l])
                used_here = tiles_used(pe, l)
                choose(0)
                take(0)
                for n in range(ALWAYS[l]):
                    step(n, tiles)
                with pe.If(used_here > ALWAYS[l]):
                    for n in range(ALWAYS[l], tiles + 2):
                        step(n, tiles)
                with pe.Else():
                    for n in range(ALWAYS[l], ALWAYS[l] + 2):
                        step(n, ALWAYS[l])
                    for n in range(ALWAYS[l] + 1, tiles):
                        pe.wait_ge(gathered[l][n % RING], (n // RING + 1) * 16)

            route(0)
            pe.wait_ge(bias3_s, 16)
            pe.wait_ge(pool_step, 4)
            mix(0)

            def rows_turned(b):
                pe.wait_ge(x2n_ready, b + 1)
                for c in range(CB):
                    last = pe.transpose((b0, b1)[b][:, P * c:P * (c + 1)], x2n[:, CB * b + c, :], ident)
                last.then_inc(x2T_ps, 1)

            def scores2(b):
                pe.wait_ge(x2T_ready, b + 1)
                for c in range(CB):
                    last = pe.matmul((b2, b3)[b][:, M * c:M * (c + 1)], x2T[:, CB * b + c, :], cT[:, b, :],
                                     start=True, stop=True)
                last.then_inc(s2_ps, 1)

            def probabilities_turned(b):
                pe.wait_ge(exp2_ready, b + 1)
                for c in range(CB):
                    last = pe.transpose((b4, b5)[b][0:M, P * c:P * (c + 1)], prob2[:, CB * b + c, :], ident)
                last.then_inc(p2T_ps, 1)

            def attend2(b):
                pe.wait_ge(p2T_ready, b + 1)
                for c in range(CB):
                    last = pe.matmul((psO, b3)[b][:, D * c:D * (c + 1)], prob2T[:, CB * b + c, :], ctx[:, b, :],
                                     start=True, stop=True)
                last.then_inc(o2_ps, 1)

            keep_warm(WARM_BETWEEN)
            rows_turned(0)
            keep_warm(WARM_STEP, psX)
            rows_turned(1)
            keep_warm(WARM_STEP, psX)
            scores2(0)
            scores2(1)
            keep_warm(WARM_STEP, psX)
            probabilities_turned(0)
            keep_warm(WARM_STEP, psX)
            attend2(0)
            keep_warm(WARM_STEP, psX)
            probabilities_turned(1)
            keep_warm(WARM_STEP, psX)
            attend2(1)
            keep_warm(WARM_NORM, psX)
            for b in range(B):
                pe.wait_ge(row1_ready, b + 1)
                for c in range(CB):
                    last = pe.transpose((b0, b1)[b][:, P * c:P * (c + 1)], row1[:, CB * b + c, 0, :], ident)
                last.then_inc(x3T_ps, 1)
                keep_warm(WARM_TURN)
                pe.wait_ge(x3T_ready, b + 1)
                for c in range(CB * b, CB * (b + 1)):
                    pe.matmul(logit[:, c, :], x3T[:, c, :], gate[:, 1, :], start=True, stop=True
                              ).then_inc(logit1_ps, 1)
            route(1)
            mix(1)


def constant_table():
    import numpy as np

    p = np.arange(P)[:, None]
    parts = {}
    parts["ident"] = np.eye(P)
    parts["headmask"] = p // DH == np.arange(H)[None, :]
    j, hh = np.arange(J)[:, None], np.arange(HH)[None, :]
    flat = P * j[None] + p[:, :, None]
    parts["blockmask"] = flat // M == hh[None]
    sel = np.zeros((P, WP))
    sel[np.arange(W) % M, np.arange(W)] = 1
    parts["sel"] = sel
    parts["before"] = p < np.arange(P)[None, :]
    parts["ones"] = np.ones((P, P))
    e = np.arange(E)
    one = np.ones((P, 1))
    parts["rev"] = one * np.tile(E - e, C)[None]
    parts["kstep"] = one * np.tile(P * e, E)[None]
    parts["earlier"] = one * (e[None, :] < e[:, None]).reshape(1, -1)
    parts["iota"] = one * np.arange(P)[None]
    parts["tstep"] = one * (P * np.arange(T0))[None]
    parts["tilecol"] = one * np.repeat(np.arange(T0), E)[None]
    q = np.arange(2 * C)[None, :]
    parts["tokval"] = np.stack([P * (q % C) + 0 * p, q // C + 1 + 0 * p, p + 0 * q], 2)
    return np.concatenate([parts[name].reshape(P, n) for name, n in CONST_PARTS], 1).astype(np.float32)


def kernel(**inputs):
    import numpy as np
    import concourse.bacc as bacc
    from concourse.bass_utils import run_bass_kernel_spmd

    a = {k: np.asarray(val) for k, val in inputs.items()}
    f0, f1, x0 = "L0_ffn_", "L1_ffn_", "L0_xattn_"
    arrays = {
        "x": a["x"],
        "ctx": a["ctx_1024"],
        "wqkvo": np.stack([a[x0 + w] for w in ("Wq", "Wk", "Wv", "Wo")], 1),
        "vecs": np.stack([a[x0 + w] for w in ("ln_q_w", "ln_q_b", "ln_k_w", "ln_k_b", "ln_v_w", "ln_v_b",
                                              "bq", "bk", "bv")], 1),
        "rows": np.concatenate([a[x0 + "bo"], a[f0 + "gate_b"], a[f1 + "br"]]),
        "consts": constant_table(),
        "gate": np.stack([a[f0 + "gate_w"].T, a[f1 + "wr"]], 1),
        "wgu": np.stack([a[f0 + "gp_w"], a[f0 + "up_w"]], 1).transpose(3, 0, 1, 2).reshape(P, -1),
        "dw": a[f0 + "down_w"].reshape(E, D, K0, FB0).transpose(3, 0, 2, 1).reshape(FB0, -1),
        "w1": a[f1 + "w1"].transpose(1, 0, 2).reshape(P, -1),
        "w2": a[f1 + "w2"].reshape(E, K1, P, D).transpose(2, 0, 1, 3).reshape(P, -1),
        "bias": np.concatenate([np.concatenate([a[f0 + "gp_b"], a[f0 + "up_b"], a[f0 + "down_b"]], 1).ravel(),
                                np.concatenate([a[f1 + "b1"], a[f1 + "b2"]], 1).ravel()]).reshape(P, BC),
    }
    arrays = {f"in_{k}": np.ascontiguousarray(val) for k, val in arrays.items()}
    nc = bacc.Bacc("TRN2", target_bir_lowering=False, num_devices=1)
    aps = [nc.dram_tensor(k, val.shape, mybir.dt.from_np(val.dtype), kind="ExternalInput").ap()
           for k, val in arrays.items()]
    out = nc.dram_tensor("out", (N, D), F32, kind="ExternalOutput").ap()
    two_blocks(nc, *aps, out)
    r = run_bass_kernel_spmd(nc, [arrays], core_ids=[0])
    return r.results[0]["out"].reshape(B, N // B, D)
```
